# Optimizing a Trainium2 kernel written in Bass

```python
import numpy as np
import jax
import jax.numpy as jnp

def _softmax(x, axis=-1):
    return jax.nn.softmax(x, axis=axis)

def _gelu(x):
    return jax.nn.gelu(x, approximate=True)

def _silu(x):
    return jax.nn.silu(x)

def _sigmoid(x):
    return jax.nn.sigmoid(x)

def _layernorm(x, axis=-1, eps=1e-05):
    m = jnp.mean(x, axis=axis, keepdims=True)
    v = jnp.var(x, axis=axis, keepdims=True)
    return (x - m) / jnp.sqrt(v + eps)

def _scatter_add(tgt, idx, src, axis=0):
    return tgt.at[idx].add(src)

def _segment_sum(src, seg, n):
    return jax.ops.segment_sum(src, seg, n)
kernel_name = 'mk_gnn_preln_d2_gnn_r8_c13c04'

def setup_inputs(seed: int=0):
    np.random.seed(seed)
    _w = jnp.asarray

    def _rec_inputs():
        import jax
        import jax.numpy as jnp
        _gk = jax.random.key(seed)
        x = -1.686e-05 + 1 * jax.random.normal(jax.random.fold_in(_gk, 1), (6250, 160), jnp.float32)
        _s = jax.random.randint(jax.random.fold_in(_gk, 2), (50000,), 0, 6250, jnp.int32)
        _d = jax.random.randint(jax.random.fold_in(_gk, 3), (50000,), 0, 6250, jnp.int32)
        _loop = jnp.arange(6250, dtype=jnp.int32)
        src = jnp.concatenate([_s, _d, _loop])
        dst = jnp.concatenate([_d, _s, _loop])
        _o = jnp.argsort(dst, stable=True)
        src = src[_o]
        dst = dst[_o]
        edge_attr_16 = jax.random.uniform(jax.random.fold_in(_gk, 11), (106250, 16), jnp.float32, 0.0, 1)
        edge_attr_4 = -0.000107899 + 1.00008 * jax.random.normal(jax.random.fold_in(_gk, 12), (106250, 4), jnp.float32)
        edge_attr_8 = jax.random.uniform(jax.random.fold_in(_gk, 13), (106250, 8), jnp.float32, 0.0, 1)
        return (x, src, dst, edge_attr_16, edge_attr_4, edge_attr_8)
    x, src, dst, edge_attr_16, edge_attr_4, edge_attr_8 = _rec_inputs()

    def _L0_gnn_setup():
        import jax, jax.numpy as jnp
        import numpy as np
        N = 6250
        E = 100000
        MUL0 = 64
        MUL1 = 32
        NB = 8
        HID = 64
        WNUM = MUL0 + MUL0 + MUL1 + MUL1
        D_IN = MUL0 + 3 * MUL1
        AVG_DEG = E / N
        key = jax.random.key(seed)
        ks = jax.random.split(key, 16)
        p = lambda i, s: jax.random.normal(ks[i], s, jnp.float32)
        return {'node_features': p(0, (N, D_IN)), 'edge_sh': p(1, (E, 4)), 'edge_embed': jax.random.uniform(ks[2], (E, NB), jnp.float32), 'W1_s': p(3, (MUL0, MUL0)), 'W1_v': p(4, (MUL1, MUL1)), 'fc_w1': p(5, (NB, HID)), 'fc_b1': jnp.zeros((HID,), jnp.float32), 'fc_w2': p(6, (HID, WNUM)) * 0.1, 'fc_b2': jnp.zeros((WNUM,), jnp.float32), 'W2_s': p(7, (96, 96)), 'W2_v': p(8, (96, MUL1)), 'Wsc_s': p(9, (MUL0, 96)), 'Wsc_v': p(10, (MUL1, MUL1)), 'edge_index': jax.random.randint(ks[11], (2, E), 0, N)}
    _L0_gnn_all = _L0_gnn_setup()
    _L0_gnn_in = {k: v for k, v in _L0_gnn_all.items() if k in ('W1_s', 'W1_v', 'fc_w1', 'fc_b1', 'fc_w2', 'fc_b2', 'W2_s', 'W2_v', 'Wsc_s', 'Wsc_v')}
    del _L0_gnn_all

    def _L1_gnn_setup():
        import jax, jax.numpy as jnp
        import numpy as np
        N, E = (2500, 40000)
        CS, CV = (64, 32)
        AS_, AV, H = (16, 8, 4)
        NB = 16
        SQRT3 = 1.7320508075688772
        SQRT2 = 1.4142135623730951
        EPS = 1e-05

        def _cg_tp(s, v, y0, y1, w_ss, w_sv, w_vs, w_vv0, w_vv1):
            out_s = jnp.concatenate([w_ss * s * y0[:, None], w_vv0 * (jnp.einsum('eci,ei->ec', v, y1) / SQRT3)], axis=-1)
            out_v = jnp.concatenate([(w_sv * s)[:, :, None] * y1[:, None, :], (w_vs * jnp.ones_like(v[..., 0]))[..., None] * v * y0[:, None, None], (w_vv1 * jnp.ones_like(v[..., 0]))[..., None] * (jnp.cross(v, y1[:, None, :]) / SQRT2)], axis=1)
            return (out_s, out_v)

        def _equiv_layernorm(s, v, gamma_s, beta_s, gamma_v):
            mu = jnp.mean(s, axis=-1, keepdims=True)
            var = jnp.var(s, axis=-1, keepdims=True)
            s_n = (s - mu) * jax.lax.rsqrt(var + EPS) * gamma_s + beta_s
            rms = jnp.sqrt(jnp.mean(jnp.sum(v * v, axis=-1), axis=-1, keepdims=True) + EPS)
            v_n = v / rms[..., None] * gamma_v[None, :, None]
            return (s_n, v_n)
        key = jax.random.key(seed)
        ks = jax.random.split(key, 26)

        def rn(k, shape, fan):
            return jax.random.normal(k, shape, jnp.float32) / np.sqrt(fan)
        D1S, D1V = (CS + CV, CS + 2 * CV)
        WN = 2 * CS + 3 * CV
        inp = {'node': jax.random.normal(ks[0], (N, CS + 3 * CV), jnp.float32), 'edge_index': jax.random.randint(ks[1], (2, E), 0, N, jnp.int64 if jax.config.jax_enable_x64 else jnp.int32), 'rbf': jax.random.uniform(ks[2], (E, NB), jnp.float32), 'rsh': jax.random.normal(ks[3], (E, 4), jnp.float32), 'gamma_s': jnp.ones((CS,), jnp.float32), 'beta_s': jnp.zeros((CS,), jnp.float32), 'gamma_v': jnp.ones((CV,), jnp.float32), 'Ws_src': rn(ks[4], (CS, CS), CS), 'Wv_src': rn(ks[5], (CV, CV), CV), 'Ws_dst': rn(ks[6], (CS, CS), CS), 'Wv_dst': rn(ks[7], (CV, CV), CV), 'W_rbf': rn(ks[8], (NB, WN), NB), 'W_alpha': rn(ks[9], (D1S, H * AS_), D1S), 'alpha_dot': rn(ks[10], (1, H, AS_), AS_), 'Ws_val': rn(ks[11], (D1S, CS), D1S), 'Wv_val': rn(ks[12], (D1V, CV), D1V), 'Wg': rn(ks[13], (CS, CV), CS), 'w2_ss': rn(ks[14], (CS,), 1), 'w2_sv': rn(ks[15], (CS,), 1), 'w2_vs': rn(ks[16], (CV,), 1), 'w2_vv0': rn(ks[17], (CV,), 1), 'w2_vv1': rn(ks[18], (CV,), 1), 'Ws_vlin': rn(ks[19], (D1S, H * AS_), D1S), 'Wv_vlin': rn(ks[20], (D1V, H * AV), D1V), 'Wps': rn(ks[21], (H * AS_, CS), H * AS_), 'Wpv': rn(ks[22], (H * AV, CV), H * AV)}
        return inp
    _L1_gnn_all = _L1_gnn_setup()
    _L1_gnn_in = {k: v for k, v in _L1_gnn_all.items() if k in ('gamma_s', 'beta_s', 'gamma_v', 'Ws_src', 'Wv_src', 'Ws_dst', 'Wv_dst', 'W_rbf', 'W_alpha', 'alpha_dot', 'Ws_val', 'Wv_val', 'Wg', 'w2_ss', 'w2_sv', 'w2_vs', 'w2_vv0', 'w2_vv1', 'Ws_vlin', 'Wv_vlin', 'Wps', 'Wpv')}
    del _L1_gnn_all
    return {'x': x, 'src': src, 'dst': dst, 'edge_attr_16': edge_attr_16, 'edge_attr_4': edge_attr_4, 'edge_attr_8': edge_attr_8, 'L0_gnn_W1_s': _L0_gnn_in['W1_s'], 'L0_gnn_W1_v': _L0_gnn_in['W1_v'], 'L0_gnn_fc_w1': _L0_gnn_in['fc_w1'], 'L0_gnn_fc_b1': _L0_gnn_in['fc_b1'], 'L0_gnn_fc_w2': _L0_gnn_in['fc_w2'], 'L0_gnn_fc_b2': _L0_gnn_in['fc_b2'], 'L0_gnn_W2_s': _L0_gnn_in['W2_s'], 'L0_gnn_W2_v': _L0_gnn_in['W2_v'], 'L0_gnn_Wsc_s': _L0_gnn_in['Wsc_s'], 'L0_gnn_Wsc_v': _L0_gnn_in['Wsc_v'], 'L1_gnn_gamma_s': _L1_gnn_in['gamma_s'], 'L1_gnn_beta_s': _L1_gnn_in['beta_s'], 'L1_gnn_gamma_v': _L1_gnn_in['gamma_v'], 'L1_gnn_Ws_src': _L1_gnn_in['Ws_src'], 'L1_gnn_Wv_src': _L1_gnn_in['Wv_src'], 'L1_gnn_Ws_dst': _L1_gnn_in['Ws_dst'], 'L1_gnn_Wv_dst': _L1_gnn_in['Wv_dst'], 'L1_gnn_W_rbf': _L1_gnn_in['W_rbf'], 'L1_gnn_W_alpha': _L1_gnn_in['W_alpha'], 'L1_gnn_alpha_dot': _L1_gnn_in['alpha_dot'], 'L1_gnn_Ws_val': _L1_gnn_in['Ws_val'], 'L1_gnn_Wv_val': _L1_gnn_in['Wv_val'], 'L1_gnn_Wg': _L1_gnn_in['Wg'], 'L1_gnn_w2_ss': _L1_gnn_in['w2_ss'], 'L1_gnn_w2_sv': _L1_gnn_in['w2_sv'], 'L1_gnn_w2_vs': _L1_gnn_in['w2_vs'], 'L1_gnn_w2_vv0': _L1_gnn_in['w2_vv0'], 'L1_gnn_w2_vv1': _L1_gnn_in['w2_vv1'], 'L1_gnn_Ws_vlin': _L1_gnn_in['Ws_vlin'], 'L1_gnn_Wv_vlin': _L1_gnn_in['Wv_vlin'], 'L1_gnn_Wps': _L1_gnn_in['Wps'], 'L1_gnn_Wpv': _L1_gnn_in['Wpv']}

def reference(x, src, dst, edge_attr_16, edge_attr_4, edge_attr_8, L0_gnn_W1_s, L0_gnn_W1_v, L0_gnn_fc_w1, L0_gnn_fc_b1, L0_gnn_fc_w2, L0_gnn_fc_b2, L0_gnn_W2_s, L0_gnn_W2_v, L0_gnn_Wsc_s, L0_gnn_Wsc_v, L1_gnn_gamma_s, L1_gnn_beta_s, L1_gnn_gamma_v, L1_gnn_Ws_src, L1_gnn_Wv_src, L1_gnn_Ws_dst, L1_gnn_Wv_dst, L1_gnn_W_rbf, L1_gnn_W_alpha, L1_gnn_alpha_dot, L1_gnn_Ws_val, L1_gnn_Wv_val, L1_gnn_Wg, L1_gnn_w2_ss, L1_gnn_w2_sv, L1_gnn_w2_vs, L1_gnn_w2_vv0, L1_gnn_w2_vv1, L1_gnn_Ws_vlin, L1_gnn_Wv_vlin, L1_gnn_Wps, L1_gnn_Wpv):
    import jax
    import jax.numpy as jnp

    def _L0_gnn_ref(node_features, edge_sh, edge_embed, W1_s, W1_v, fc_w1, fc_b1, fc_w2, fc_b2, W2_s, W2_v, Wsc_s, Wsc_v, edge_index):
        import jax, jax.numpy as jnp
        import numpy as np
        N = 6250
        E = 100000
        MUL0 = 64
        MUL1 = 32
        NB = 8
        HID = 64
        WNUM = MUL0 + MUL0 + MUL1 + MUL1
        D_IN = MUL0 + 3 * MUL1
        AVG_DEG = E / N
        n = node_features.shape[0]
        s = node_features[:, :MUL0]
        v = node_features[:, MUL0:].reshape(n, MUL1, 3)
        xs = s @ W1_s / np.sqrt(MUL0)
        xv = jnp.einsum('nmc,mk->nkc', v, W1_v) / np.sqrt(MUL1)
        src, dst = (edge_index[0], edge_index[1])
        sh0 = edge_sh[:, 0]
        sh1 = edge_sh[:, 1:4]
        w = jax.nn.silu(edge_embed @ fc_w1 + fc_b1) @ fc_w2 + fc_b2
        w_ss = w[:, :MUL0]
        w_sv = w[:, MUL0:2 * MUL0]
        w_vs = w[:, 2 * MUL0:2 * MUL0 + MUL1]
        w_vv = w[:, 2 * MUL0 + MUL1:]
        xs_e = xs[src]
        xv_e = xv[src]
        m0_a = w_ss * xs_e * sh0[:, None]
        m1_a = (w_sv * xs_e)[:, :, None] * sh1[:, None, :]
        m1_b = w_vs[:, :, None] * xv_e * sh0[:, None, None]
        m0_b = w_vv * jnp.einsum('emc,ec->em', xv_e, sh1) / np.sqrt(3.0)
        msg = jnp.concatenate([m0_a, m0_b, m1_a.reshape(-1, MUL0 * 3), m1_b.reshape(-1, MUL1 * 3)], axis=1)
        agg = jax.ops.segment_sum(msg, dst, num_segments=n) / np.sqrt(AVG_DEG)
        agg_s = agg[:, :96]
        agg_v = agg[:, 96:].reshape(n, 96, 3)
        out_s = agg_s @ W2_s / np.sqrt(96.0)
        out_v = jnp.einsum('nmc,mk->nkc', agg_v, W2_v) / np.sqrt(96.0)
        out_s = out_s + s @ Wsc_s / np.sqrt(MUL0)
        out_v = out_v + jnp.einsum('nmc,mk->nkc', v, Wsc_v) / np.sqrt(MUL1)
        scalars = jax.nn.silu(out_s[:, :MUL0])
        gates = jax.nn.silu(out_s[:, MUL0:MUL0 + MUL1])
        gated = out_v * gates[:, :, None]
        feats = jnp.concatenate([scalars, gated.reshape(n, MUL1 * 3)], axis=1)
        return node_features + feats

    def _L1_gnn_ref(node, rbf, rsh, gamma_s, beta_s, gamma_v, Ws_src, Wv_src, Ws_dst, Wv_dst, W_rbf, W_alpha, alpha_dot, Ws_val, Wv_val, Wg, w2_ss, w2_sv, w2_vs, w2_vv0, w2_vv1, Ws_vlin, Wv_vlin, Wps, Wpv, edge_index):
        import jax, jax.numpy as jnp
        import numpy as np
        N, E = (2500, 40000)
        CS, CV = (64, 32)
        AS_, AV, H = (16, 8, 4)
        NB = 16
        SQRT3 = 1.7320508075688772
        SQRT2 = 1.4142135623730951
        EPS = 1e-05

        def _cg_tp(s, v, y0, y1, w_ss, w_sv, w_vs, w_vv0, w_vv1):
            out_s = jnp.concatenate([w_ss * s * y0[:, None], w_vv0 * (jnp.einsum('eci,ei->ec', v, y1) / SQRT3)], axis=-1)
            out_v = jnp.concatenate([(w_sv * s)[:, :, None] * y1[:, None, :], (w_vs * jnp.ones_like(v[..., 0]))[..., None] * v * y0[:, None, None], (w_vv1 * jnp.ones_like(v[..., 0]))[..., None] * (jnp.cross(v, y1[:, None, :]) / SQRT2)], axis=1)
            return (out_s, out_v)

        def _equiv_layernorm(s, v, gamma_s, beta_s, gamma_v):
            mu = jnp.mean(s, axis=-1, keepdims=True)
            var = jnp.var(s, axis=-1, keepdims=True)
            s_n = (s - mu) * jax.lax.rsqrt(var + EPS) * gamma_s + beta_s
            rms = jnp.sqrt(jnp.mean(jnp.sum(v * v, axis=-1), axis=-1, keepdims=True) + EPS)
            v_n = v / rms[..., None] * gamma_v[None, :, None]
            return (s_n, v_n)
        n = node.shape[0]
        e = rsh.shape[0]
        s = node[:, :CS]
        v = node[:, CS:].reshape(n, CV, 3)
        s_n, v_n = _equiv_layernorm(s, v, gamma_s, beta_s, gamma_v)
        src, dst = (edge_index[0], edge_index[1])
        msg_s = (s_n @ Ws_src)[src] + (s_n @ Ws_dst)[dst]
        msg_v = jnp.einsum('ncx,cd->ndx', v_n, Wv_src)[src] + jnp.einsum('ncx,cd->ndx', v_n, Wv_dst)[dst]
        y0, y1 = (rsh[:, 0], rsh[:, 1:4])
        w1 = rbf @ W_rbf
        m1_s, m1_v = _cg_tp(msg_s, msg_v, y0, y1, w1[:, :CS], w1[:, CS:2 * CS], w1[:, 2 * CS:2 * CS + CV], w1[:, 2 * CS + CV:2 * CS + 2 * CV], w1[:, 2 * CS + 2 * CV:])
        a = (m1_s @ W_alpha).reshape(e, H, AS_)
        a = jnp.where(a > 0, a, 0.2 * a)
        a = jnp.sum(a * alpha_dot, axis=-1, keepdims=True)
        amax = jax.ops.segment_max(a, dst, num_segments=n)
        amax = jnp.where(jnp.isfinite(amax), amax, 0.0)
        ex = jnp.exp(a - amax[dst])
        den = jax.ops.segment_sum(ex, dst, num_segments=n)
        alpha = ex / (den[dst] + 1e-16)
        val_s = m1_s @ Ws_val
        val_v = jnp.einsum('ecx,cd->edx', m1_v, Wv_val)
        val_v = val_v * jax.nn.sigmoid(val_s @ Wg)[..., None]
        val_s = jax.nn.sigmoid(val_s)
        m2_s, m2_v = _cg_tp(val_s, val_v, y0, y1, w2_ss, w2_sv, w2_vs, w2_vv0, w2_vv1)
        hs = (m2_s @ Ws_vlin).reshape(e, H, AS_)
        hv = jnp.einsum('ecx,cd->edx', m2_v, Wv_vlin).reshape(e, H, AV, 3)
        h = jnp.concatenate([hs, hv.reshape(e, H, AV * 3)], axis=-1)
        agg = jax.ops.segment_sum(alpha * h, dst, num_segments=n)
        agg_s = agg[:, :, :AS_].reshape(n, H * AS_)
        agg_v = agg[:, :, AS_:].reshape(n, H * AV, 3)
        out = node + jnp.concatenate([agg_s @ Wps, jnp.einsum('ncx,cd->ndx', agg_v, Wpv).reshape(n, CV * 3)], axis=-1)
        return out
    edge_index = jnp.stack([src, dst])
    h = jnp.maximum(_layernorm(x, axis=-1), 0.0)
    x = x + _L0_gnn_ref(h, edge_attr_4, edge_attr_8, L0_gnn_W1_s, L0_gnn_W1_v, L0_gnn_fc_w1, L0_gnn_fc_b1, L0_gnn_fc_w2, L0_gnn_fc_b2, L0_gnn_W2_s, L0_gnn_W2_v, L0_gnn_Wsc_s, L0_gnn_Wsc_v, edge_index)
    h = jnp.maximum(_layernorm(x, axis=-1), 0.0)
    x = x + _L1_gnn_ref(h, edge_attr_16, edge_attr_4, L1_gnn_gamma_s, L1_gnn_beta_s, L1_gnn_gamma_v, L1_gnn_Ws_src, L1_gnn_Wv_src, L1_gnn_Ws_dst, L1_gnn_Wv_dst, L1_gnn_W_rbf, L1_gnn_W_alpha, L1_gnn_alpha_dot, L1_gnn_Ws_val, L1_gnn_Wv_val, L1_gnn_Wg, L1_gnn_w2_ss, L1_gnn_w2_sv, L1_gnn_w2_vs, L1_gnn_w2_vv0, L1_gnn_w2_vv1, L1_gnn_Ws_vlin, L1_gnn_Wv_vlin, L1_gnn_Wps, L1_gnn_Wpv, edge_index)
    return x

_drawn_inputs = setup_inputs


def setup_inputs(seed=0):
    import zlib

    import numpy as np

    out = dict(_drawn_inputs(seed))
    spreads = {'L0_gnn_fc_b1': (0.0, 0.595),
     'L0_gnn_fc_b2': (0.0, 0.1),
     'L1_gnn_gamma_s': (1.0, 0.6),
     'L1_gnn_beta_s': (0.0, 0.72),
     'L1_gnn_gamma_v': (1.0, 0.6)}
    factors = {'L1_gnn_Wv_src': 2.737, 'L1_gnn_Wg': 2.871, 'L1_gnn_w2_vv1': 4.222}
    for name, (base, spread) in spreads.items():
        noise = np.random.default_rng([zlib.crc32(name.encode()), seed]).standard_normal(out[name].shape)
        drawn = base * np.exp(spread * noise) if base else spread * noise
        out[name] = jnp.asarray(drawn.astype(out[name].dtype))
    for name, factor in factors.items():
        out[name] = (out[name] * factor).astype(out[name].dtype)
    return out
```

```python
from contextlib import ExitStack

import numpy as np

import concourse.bass as bass
from concourse import mybir

F32 = mybir.dt.float32
I32 = mybir.dt.int32
ALU = mybir.AluOpType
ACT = mybir.ActivationFunctionType
AX = mybir.AxisListType.X

P = 128
N = 6250
E = 106250
S0, V0 = 64, 32
D = S0 + 3 * V0
NB0, HID, WN0 = 8, 64, 2 * S0 + 2 * V0
NB1, WN1 = 16, 2 * S0 + 3 * V0
HEADS, AS, AV = 4, 16, 8
LANES = 4
GE = P * LANES
GROUPS = -(-E // GE)
EP = GROUPS * GE
WINDOWS = -(-N // P)
NP = WINDOWS * P
STEPS = GROUPS + WINDOWS - 1
CH = EP // P
AGG0 = 480
AGG1 = D + HEADS
QW = 352
BIG = 3.0e38
EPS = 1e-5
AVG_DEG = 16.0
R3 = float(np.sqrt(3.0))
R2 = float(np.sqrt(2.0))


def sweep(eng, n, step, lag=0, first=2, last=0):
    end = n - last - (n - last) % 2
    for g in range(first):
        step(g - g % 2, g % 2)
    with eng.Fori(first, end - 1, 2) as i:
        step(i, 0)
        step(i, 1)
    for g in range(end, n + lag):
        step(g - g % 2, g % 2)


def back(i, par, lag):
    q = (par - lag) % 2
    return i + (par - lag - q), q


def live(i, par, n):
    return not isinstance(i, int) or 0 <= i + par < n


def uses(i, n):
    return i * (8 * n) + 16 * n


def wait(eng, sem, val):
    if not isinstance(val, int) or val > 0:
        eng.wait_ge(sem, val)


def bc(ap, shape):
    return ap.to_broadcast(shape)


class Kernel:
    def __init__(self, nc, ctx, a):
        self.nc, self.ctx, self.a = nc, ctx, a
        self.psum = ctx.enter_context(nc.psum_tensor("psum", [P, 8 * 512], F32))
        dram = lambda name, shape, dt=F32: nc.dram_tensor(name, shape, dt, kind="Internal").ap()
        self.steps_row = dram("steps_row", [1, STEPS])
        self.table0 = dram("table0", [NP, D])
        self.table_src = dram("table_src", [NP, D])
        self.table_dst = dram("table_dst", [NP, D])
        self.agg0 = dram("agg0", [(WINDOWS + 2) * P, AGG0])
        self.agg1 = dram("agg1", [(WINDOWS + 2) * P, AGG1])
        self.logits = dram("logits", [EP, HEADS])
        self.weights_e = dram("weights_e", [EP, HEADS])
        self.values = dram("values", [EP, D])
        self.s_begin = {nc.sync.engine: self.sem("begin_sp"), nc.gpsimd.engine: self.sem("begin_pool")}
        sb = self.sb
        self.ident = sb("ident", [P, P])
        self.iota = sb("iota", [P, P])
        self.resid = sb("resid", [P, WINDOWS, D])
        self.step_group = sb("step_group", [1, STEPS], I32)
        self.step_row = sb("step_row", [1, STEPS], I32)
        self.step_base = sb("step_base", [P, STEPS])
        self.step_keep = sb("step_keep", [P, STEPS])

    def bank(self, i, n=1):
        return self.psum[:, 512 * i:512 * (i + n)]

    def wait(self, eng, sem, val):
        wait(eng, sem, val)
        if not isinstance(val, int):
            eng.sem_inc(self.s_begin[eng.engine], 1)

    def sb(self, name, shape, dt=F32, ctx=None):
        return (ctx or self.ctx).enter_context(self.nc.sbuf_tensor(name, shape, dt))

    def sem(self, name):
        return self.ctx.enter_context(self.nc.semaphore(name))


class Chain:

    def __init__(self, eng, sem):
        self.eng, self.sem, self.n = eng, sem, 0

    def __call__(self, ins):
        self.n += 1
        ins.then_inc(self.sem, 1)
        self.eng.wait_ge(self.sem, self.n)


def setup_steps(k):
    nc, a = k.nc, k.a
    with ExitStack() as ctx:
        sb = lambda name, shape, dt=F32: k.sb(name, shape, dt, ctx)
        first = sb("first", [P, GROUPS], I32)
        win_i = sb("win_i", [P, GROUPS], I32)
        start = sb("start", [P, GROUPS])
        col = sb("col", [P, GROUPS])
        kp = sb("kp", [P, 2])
        cmp = sb("cmp", [P, 2, GROUPS])
        gk = sb("gk", [P, 2])
        gk_out = sb("gk_out", [P, 2])
        grp = sb("grp", [P, STEPS])
        kk = sb("kk", [P, STEPS])
        win = sb("win", [P, STEPS])
        fin = sb("fin", [P, STEPS])
        pid = sb("pid", [P, 1])
        spare = sb("spare", [P, STEPS])
        s_first, s_iota, s_chain = k.sem("su_first"), k.sem("su_iota"), k.sem("su_chain")
        s_gk, s_row, s_grp = k.sem("su_gk"), k.sem("su_row"), k.sem("su_grp")
        with nc.Block() as block:

            @block.sync
            def _(sp):
                sp.dma_start(first[:, :], a["dst_first"].to_broadcast([P, GROUPS])).then_inc(s_first, 16)
                sp.wait_ge(s_gk, 1)
                for q in range(2):
                    sp.dma_start(k.steps_row[0:1, q * P:(q + 1) * P].rearrange("a p -> p a"),
                                 gk_out[:, q:q + 1]).then_inc(s_row, 16)
                sp.wait_ge(s_row, 32)
                sp.dma_start(grp[:, :], k.steps_row.to_broadcast([P, STEPS])).then_inc(s_grp, 16)

            @block.gpsimd
            def _(pool):
                kw = dict(allow_small_or_imprecise_dtypes=True)
                pool.iota(k.iota[:, :], [[1, P]], 0, 0, **kw).then_inc(s_iota, 1)
                pool.iota(col[:, :], [[1, GROUPS]], 0, 0, **kw).then_inc(s_iota, 1)
                pool.iota(kp[:, :], [[P, 2]], 0, 1, **kw).then_inc(s_iota, 1)
                pool.iota(kk[:, :], [[1, STEPS]], 0, 0, **kw).then_inc(s_iota, 1)
                pool.iota(spare[:, :], [[0, STEPS // 2], [1, 2]], WINDOWS, 0, **kw).then_inc(s_iota, 1)
                pool.iota(pid[:, :], [[1, 1]], 0, 1, **kw).then_inc(s_iota, 1)

            @block.vector
            def _(dve):
                link = Chain(dve, s_chain)
                dve.wait_ge(s_iota, 6)
                link(dve.tensor_scalar(k.ident[:, :], k.iota[:, :], pid[:, 0:1], None, ALU.is_equal))
                dve.wait_ge(s_first, 16)
                link(dve.tensor_scalar(win_i[:, :], first[:, :], 7, None, ALU.arith_shift_right))
                link(dve.tensor_tensor(start[:, :], win_i[:, :], col[:, :], ALU.add))
                link(dve.memset(start[:, 0:1], float(2 * STEPS)))
                for q in range(2):
                    link(dve.tensor_scalar(cmp[:, q, :], start[:, :], kp[:, q:q + 1], None, ALU.is_le))
                link(dve.tensor_reduce(gk[:, :], cmp[:, :, :], AX, ALU.add))
                dve.tensor_copy(gk_out[:, :], gk[:, :]).then_inc(s_gk, 1)
                dve.wait_ge(s_grp, 16)
                link(dve.tensor_copy(k.step_group[0:1, :], grp[0:1, :]))
                link(dve.tensor_tensor(win[:, :], kk[:, :], grp[:, :], ALU.subtract))
                link(dve.tensor_scalar(k.step_base[:, :], win[:, :], float(P), None, ALU.mult))
                link(dve.memset(k.step_keep[:, 0:1], 0.0))
                link(dve.memset(fin[:, STEPS - 1:STEPS], 1.0))
                link(dve.tensor_tensor(k.step_keep[:, 1:STEPS], win[:, 1:STEPS], win[:, 0:STEPS - 1], ALU.is_equal))
                link(dve.tensor_tensor(fin[:, 0:STEPS - 1], win[:, 0:STEPS - 1], win[:, 1:STEPS], ALU.not_equal))
                link(dve.tensor_tensor(win[:, :], win[:, :], spare[:, :], ALU.subtract))
                link(dve.tensor_tensor(win[:, :], win[:, :], fin[:, :], ALU.mult))
                link(dve.tensor_tensor(win[:, :], win[:, :], spare[:, :], ALU.add))
                link(dve.tensor_copy(k.step_row[0:1, :], win[0:1, :]))


def place(sp, sem, tile, row, col, w):
    n, done, r = w.shape[0], 0, 0
    while r < n:
        m = min(n - r, P - (row + r) % P)
        q = (row + r) % P
        c = (row + r) // P
        sp.dma_start(tile[q:q + m, c, col:col + w.shape[1]], w[r:r + m, :]).then_inc(sem, 16)
        done += 16
        r += m
    return done


def node_phase(k, layer):
    nc, a, W = k.nc, k.a, WINDOWS
    L = f"n{layer}_"
    cols = 352 if layer == 0 else 320
    with ExitStack() as ctx:
        sb = lambda name, shape, dt=F32: k.sb(L + name, shape, dt, ctx)
        raw = sb("raw", [P, W, D])
        feat = sb("feat", [P, W, D])
        stat = sb("stat", [P, 4, W])
        wt = sb("wt", [P, 2, cols])
        stage = sb("stage", [P, 2, D])
        turned = sb("turned", [P, 2, 2 * P])
        outb = sb("outb", [P, 2, cols])
        if layer == 1:
            gamma_s, beta_s = sb("gamma_s", [P, S0]), sb("beta_s", [P, S0])
            gamma_v = sb("gamma_v", [P, V0])
        s_load, s_zero, s_chain = k.sem(L + "load"), k.sem(L + "zero"), k.sem(L + "chain")
        s_weights, s_std_in, s_std_out = k.sem(L + "weights"), k.sem(L + "std_in"), k.sem(L + "std_out")
        s_ready, s_stage, s_turn, s_turned = k.sem(L + "ready"), k.sem(L + "stage"), k.sem(L + "turn"), k.sem(L + "turned")
        s_prod, s_out = k.sem(L + "prod"), k.sem(L + "out")
        s_store = [k.sem(L + f"store{q}") for q in range(2)]
        turn_ps = [k.bank(0), k.bank(1)]
        prod_ps = [k.bank(2), k.bank(3)]
        n_weights = 8 * 16
        n_store = 1 if layer == 0 else 2
        with nc.Block() as block:

            @block.sync
            def _(sp):
                if layer == 0:
                    sp.dma_start(raw[:, :, :], a["x"].rearrange("(j p) d -> p j d", p=P)).then_inc(s_load, 16)
                sp.wait_ge(s_zero, 1)
                w_n = 0
                if layer == 0:
                    Ws, Wv, Cs, Cv = a["L0_gnn_W1_s"], a["L0_gnn_W1_v"], a["L0_gnn_Wsc_s"], a["L0_gnn_Wsc_v"]
                    w_n += place(sp, s_weights, wt, 0, 0, Ws)
                    w_n += place(sp, s_weights, wt, 0, D, Cs)
                    for c in range(3):
                        w_n += place(sp, s_weights, wt, S0 + V0 * c, S0 + V0 * c, Wv)
                        w_n += place(sp, s_weights, wt, S0 + V0 * c, D + 96 + V0 * c, Cv)
                else:
                    for q, end in enumerate(("src", "dst")):
                        w_n += place(sp, s_weights, wt, 0, D * q, a[f"L1_gnn_Ws_{end}"])
                        for c in range(3):
                            w_n += place(sp, s_weights, wt, S0 + V0 * c, D * q + S0 + V0 * c, a[f"L1_gnn_Wv_{end}"])
                    for t, name in ((gamma_s, "gamma_s"), (beta_s, "beta_s"), (gamma_v, "gamma_v")):
                        row = a["L1_gnn_" + name].rearrange("(a n) -> a n", a=1)
                        sp.dma_start(t[:, :], row.to_broadcast([P, row.shape[1]])).then_inc(s_load, 16)

                def store(i, par):
                    k.wait(sp, s_out, i + (par + 1))
                    rows = bass.ds((i + par) * P, P)
                    if layer == 0:
                        sp.dma_start(k.table0[rows, :], outb[:, par, 0:D]).then_inc(s_store[par], 16)
                    else:
                        sp.dma_start(k.table_src[rows, :], outb[:, par, 0:D]).then_inc(s_store[par], 16)
                        sp.dma_start(k.table_dst[rows, :], outb[:, par, D:2 * D]).then_inc(s_store[par], 16)

                sweep(sp, W, store)
                sp.wait_ge(s_store[0], 16 * n_store * ((W + 1) // 2))
                sp.wait_ge(s_store[1], 16 * n_store * (W // 2))
                assert w_n == n_weights

            @block.gpsimd
            def _(pool):
                pool.memset(wt[:, :, :], 0.0).then_inc(s_zero, 1)
                pool.wait_ge(s_ready, 1)

                def copy(i, par):
                    k.wait(pool, s_turn, i + (par - 1))
                    pool.tensor_copy(stage[:, par, :], feat[:, i + par, :] if isinstance(i, int) else
                                     feat[:, bass.ds(i + par, 1), :]).then_inc(s_stage, 1)

                sweep(pool, W, copy)

            @block.tensor
            def _(pe):
                def turn(i, par):
                    pe.wait_ge(s_stage, i + (par + 1))
                    wait(pe, s_turned, (i + (par - 1)) * 2)
                    pe.transpose(turn_ps[par][:, 0:P], stage[:, par, 0:P], k.ident[:, :])
                    pe.transpose(turn_ps[par][0:D - P, P:2 * P], stage[:, par, P:D], k.ident[:, :]).then_inc(s_turn, 1)

                def product(i, par):
                    pe.wait_ge(s_turned, (i + (par + 1)) * 2)
                    wait(pe, s_out, i + (par - 1))
                    pe.matmul(prod_ps[par][:, 0:cols], turned[:, par, 0:P], wt[:, 0, :], start=True, stop=False)
                    pe.matmul(prod_ps[par][:, 0:cols], turned[0:D - P, par, P:2 * P], wt[0:D - P, 1, :],
                              start=False, stop=True).then_inc(s_prod, 1)

                def step(i, par):
                    if live(i, par, W):
                        turn(i, par)
                    j, q = back(i, par, 1)
                    if live(j, q, W):
                        product(j, q)

                pe.wait_ge(s_ready, 1)
                sweep(pe, W, step, 1)

            @block.scalar
            def _(act):
                for n in range(1 if layer == 0 else 3):
                    act.wait_ge(s_std_in, n + 1)
                    act.activation(stat[:, 3, :], stat[:, 2, :], ACT.Sqrt).then_inc(s_std_out, 1)

                def evacuate(i, par):
                    act.wait_ge(s_turn, i + (par + 1))
                    wait(act, s_prod, i + (par - 1))
                    act.copy(turned[:, par, 0:P], turn_ps[par][:, 0:P]).then_inc(s_turned, 1)
                    act.copy(turned[0:D - P, par, P:2 * P], turn_ps[par][0:D - P, P:2 * P]).then_inc(s_turned, 1)

                sweep(act, W, evacuate)

            @block.vector
            def _(dve):
                link = Chain(dve, s_chain)
                comp = lambda t, lo=S0: t[:, :, lo:lo + 3 * V0].rearrange("p j (c m) -> p j c m", c=3)
                inter = lambda t: t[:, :, S0:D].rearrange("p j (m c) -> p j c m", c=3)
                mean, rstd = stat[:, 0, :], stat[:, 1, :]
                over = lambda s, n: bc(s.rearrange("p (j a) -> p j a", a=1), [P, W, n])

                def over3(s):
                    return bc(s.rearrange("p (j a b) -> p j a b", a=1, b=1), [P, W, 3, V0])

                def norm_relu(src, src_vec):
                    link(dve.tensor_reduce(mean, src[:, :, :], AX, ALU.add))
                    link(dve.tensor_scalar(mean, mean, 1.0 / D, None, ALU.mult))
                    link(dve.tensor_tensor(feat[:, :, 0:S0], src[:, :, 0:S0], over(mean, S0), ALU.subtract))
                    link(dve.tensor_tensor(comp(feat), src_vec(src), over3(mean), ALU.subtract))

                def scale_of(x, scratch, lo, hi, inv_n, turn):
                    link(dve.tensor_tensor(scratch[:, :, lo:hi], x[:, :, lo:hi], x[:, :, lo:hi], ALU.mult))
                    link(dve.tensor_reduce(rstd, scratch[:, :, lo:hi], AX, ALU.add))
                    dve.tensor_scalar(stat[:, 2, :], rstd, inv_n, EPS, ALU.mult, ALU.add).then_inc(s_std_in, 1)
                    dve.wait_ge(s_std_out, turn)
                    link(dve.reciprocal(rstd, stat[:, 3, :]))

                if layer == 0:
                    dve.wait_ge(s_load, 16)
                    norm_relu(raw, inter)
                    scale_of(feat, k.resid, 0, D, 1.0 / D, 1)
                    link(dve.scalar_tensor_tensor(feat[:, :, :], feat[:, :, :], 0.0, over(rstd, D), ALU.max, ALU.mult))
                    link(dve.tensor_tensor(k.resid[:, :, 0:S0], feat[:, :, 0:S0], raw[:, :, 0:S0], ALU.add))
                    link(dve.tensor_tensor(comp(k.resid), comp(feat), inter(raw), ALU.add))
                else:
                    norm_relu(k.resid, comp)
                    scale_of(feat, raw, 0, D, 1.0 / D, 1)
                    link(dve.scalar_tensor_tensor(feat[:, :, :], feat[:, :, :], 0.0, over(rstd, D), ALU.max, ALU.mult))
                    link(dve.tensor_tensor(k.resid[:, :, :], feat[:, :, :], k.resid[:, :, :], ALU.add))
                    dve.wait_ge(s_load, 48)
                    fs = feat[:, :, 0:S0]
                    along = lambda t, n: bc(t[:, :].rearrange("p (a n) -> p a n", a=1), [P, W, n])
                    link(dve.tensor_reduce(mean, fs, AX, ALU.add))
                    link(dve.tensor_scalar(mean, mean, 1.0 / S0, None, ALU.mult))
                    link(dve.tensor_tensor(fs, fs, over(mean, S0), ALU.subtract))
                    scale_of(feat, raw, 0, S0, 1.0 / S0, 2)
                    link(dve.tensor_tensor(fs, fs, over(rstd, S0), ALU.mult))
                    link(dve.tensor_tensor(fs, fs, along(gamma_s, S0), ALU.mult))
                    link(dve.tensor_tensor(fs, fs, along(beta_s, S0), ALU.add))
                    scale_of(feat, raw, S0, D, 1.0 / V0, 3)
                    fv = feat[:, :, S0:D]
                    link(dve.tensor_tensor(fv, fv, over(rstd, 3 * V0), ALU.mult))
                    for c in range(3):
                        fc = feat[:, :, S0 + V0 * c:S0 + V0 * (c + 1)]
                        link(dve.tensor_tensor(fc, fc, along(gamma_v, V0), ALU.mult))
                dve.wait_ge(s_weights, n_weights)
                if layer == 0:
                    link(dve.tensor_scalar(wt[0:S0, 0, :], wt[0:S0, 0, :], 1.0 / np.sqrt(S0), None, ALU.mult))
                    link(dve.tensor_scalar(wt[S0:P, 0, :], wt[S0:P, 0, :], float(1.0 / np.sqrt(V0)), None, ALU.mult))
                    link(dve.tensor_scalar(wt[0:V0, 1, :], wt[0:V0, 1, :], float(1.0 / np.sqrt(V0)), None, ALU.mult))
                dve.tensor_copy(stat[:, 2, 0:1], stat[:, 3, 0:1]).then_inc(s_ready, 1)

                def emit(i, par):
                    dve.wait_ge(s_prod, i + (par + 1))
                    wait(dve, s_store[par], i * (8 * n_store))
                    if layer == 0:
                        j = (i + par) if isinstance(i, int) else bass.ds(i + par, 1)
                        dve.tensor_copy(k.selfc[:, j, :], prod_ps[par][:, D:cols])
                        dve.tensor_copy(outb[:, par, 0:D], prod_ps[par][:, 0:D]).then_inc(s_out, 1)
                    else:
                        dve.tensor_copy(outb[:, par, :], prod_ps[par][:, 0:cols]).then_inc(s_out, 1)

                sweep(dve, W, emit)


def layer0_update(k):
    nc, a, W = k.nc, k.a, WINDOWS
    with ExitStack() as ctx:
        sb = lambda name, shape, dt=F32: k.sb("u_" + name, shape, dt, ctx)
        wt = sb("wt", [P, 4, 192])
        sums = sb("sums", [P, 2, AGG0])
        turned = sb("turned", [P, 2, 512])
        scol = sb("scol", [P, 4])
        sil = sb("sil", [P, W, 96])
        s_zero, s_weights, s_chain, s_wready = k.sem("u_zero"), k.sem("u_weights"), k.sem("u_chain"), k.sem("u_wready")
        s_sums = [k.sem(f"u_sums{q}") for q in range(2)]
        s_turn, s_turned, s_prod, s_out, s_sil = k.sem("u_turn"), k.sem("u_turned"), k.sem("u_prod"), k.sem("u_out"), k.sem("u_sil")
        turn_ps = [k.bank(0), k.bank(1)]
        prod_ps = [k.bank(2), k.bank(3)]
        W2s, W2v = a["L0_gnn_W2_s"], a["L0_gnn_W2_v"]
        blocks = [(0, 0, W2s[0:S0, :]), (192, 96, W2v[0:S0, :]), (256, 128, W2v[0:S0, :]), (352, 160, W2v[0:S0, :])]
        blocks += [(S0 + V0 * c, 96 + V0 * c, W2v[S0:96, :]) for c in range(3)]
        blocks += [(r, 0, W2s[S0:96, :]) for r in (160, 320, 448)]
        n_dma = 16 * (len(blocks) + 1)
        with nc.Block() as block:

            @block.gpsimd
            def _(pool):
                pool.memset(wt[:, :, :], 0.0).then_inc(s_zero, 1)

            @block.sync
            def _(sp):
                sp.wait_ge(s_zero, 1)
                n = sum(place(sp, s_weights, wt, r, c, w) for r, c, w in blocks)
                assert n == n_dma

                def load(i, par):
                    k.wait(sp, s_turn, i + (par - 1))
                    sp.dma_start(sums[:, par, :], k.agg0[bass.ds((i + par) * P, P), :]).then_inc(s_sums[par], 16)

                sweep(sp, W, load)

            @block.tensor
            def _(pe):
                def turn(i, par):
                    pe.wait_ge(s_sums[par], uses(i, 1))
                    wait(pe, s_turned, i + (par - 1))
                    for c in range(4):
                        m = min(P, AGG0 - c * P)
                        ins = pe.transpose(turn_ps[par][0:m, c * P:(c + 1) * P], sums[:, par, c * P:c * P + m], k.ident[:, :])
                    ins.then_inc(s_turn, 1)

                def product(i, par):
                    pe.wait_ge(s_turned, i + (par + 1))
                    wait(pe, s_out, i + (par - 1))
                    for c in range(4):
                        m = min(P, AGG0 - c * P)
                        ins = pe.matmul(prod_ps[par][:, 0:192], turned[0:m, par, c * P:(c + 1) * P], wt[0:m, c, :],
                                        start=(c == 0), stop=(c == 3))
                    ins.then_inc(s_prod, 1)

                def step(i, par):
                    if live(i, par, W):
                        turn(i, par)
                    j, q = back(i, par, 1)
                    if live(j, q, W):
                        product(j, q)

                pe.wait_ge(s_wready, 1)
                sweep(pe, W, step, 1)

            @block.scalar
            def _(act):
                def evacuate(i, par):
                    act.wait_ge(s_turn, i + (par + 1))
                    wait(act, s_prod, i + (par - 1))
                    act.copy(turned[:, par, 0:384], turn_ps[par][:, 0:384])
                    act.copy(turned[0:96, par, 384:512], turn_ps[par][0:96, 384:512]).then_inc(s_turned, 1)

                sweep(act, W, evacuate)
                act.wait_ge(s_out, W)
                act.activation(sil[:, :, :], k.selfc[:, :, 0:96], ACT.Silu).then_inc(s_sil, 1)

            @block.vector
            def _(dve):
                link = Chain(dve, s_chain)
                base = float(1.0 / (np.sqrt(AVG_DEG) * np.sqrt(96.0)))
                link(dve.memset(scol[:, :], base))
                for row in (160, 320, 448):
                    q, c = row % P, row // P
                    link(dve.memset(scol[q:q + V0, c:c + 1], base / R3))
                dve.wait_ge(s_weights, n_dma)
                for c in range(4):
                    link(dve.tensor_scalar(wt[:, c, :], wt[:, c, :], scol[:, c:c + 1], None, ALU.mult))
                dve.tensor_copy(scol[:, 0:1], scol[:, 1:2]).then_inc(s_wready, 1)

                def add(i, par):
                    dve.wait_ge(s_prod, i + (par + 1))
                    j = bass.ds(i + par, 1)
                    dve.tensor_tensor(k.selfc[:, j, :], k.selfc[:, j, :],
                                      prod_ps[par][:, 0:192].rearrange("p (a n) -> p a n", a=1), ALU.add).then_inc(s_out, 1)

                sweep(dve, W, add)
                dve.wait_ge(s_sil, 1)
                link(dve.tensor_tensor(k.resid[:, :, 0:S0], k.resid[:, :, 0:S0], sil[:, :, 0:S0], ALU.add))
                comp = lambda t, lo: t[:, :, lo:lo + 96].rearrange("p j (c m) -> p j c m", c=3)
                for c in range(3):
                    t = k.selfc[:, :, 96 + V0 * c:96 + V0 * (c + 1)]
                    link(dve.tensor_tensor(t, t, sil[:, :, S0:96], ALU.mult))
                link(dve.tensor_tensor(k.resid[:, :, S0:D], k.resid[:, :, S0:D], k.selfc[:, :, 96:192], ALU.add))


def edges0(k):
    nc, a = k.nc, k.a
    with ExitStack() as ctx:
        sb = lambda name, shape, dt=F32: k.sb("e0_" + name, shape, dt, ctx)
        fc1, b1 = sb("fc1", [NB0, HID]), sb("b1", [HID, 1])
        fc2 = sb("fc2", [HID + 1, WN0])
        idx, dst = sb("idx", [P, 2, LANES], I32), sb("dst", [P, 2, LANES], I32)
        sh = sb("sh", [P, 2, LANES, 4])
        embed = sb("embed", [NB0, 2, GE])
        hid = sb("hid", [HID + 1, 2, GE])
        xg = sb("xg", [P, 2, LANES, D])
        rel = sb("rel", [P, 2, LANES])
        sel = sb("sel", [P, 2, LANES, 4, P])
        msg = sb("msg", [P, 2, LANES, 320])
        acc = sb("acc", [P, 2, AGG0])
        names = ["weights", "ones", "hid", "hidS", "wps", "vec", "agg", "acc"]
        s_weights, s_ones, s_hid, s_hidS, s_wps, s_vec, s_agg, s_acc = [k.sem("e0_" + n) for n in names]
        s_load = [k.sem(f"e0_load{q}") for q in range(2)]
        s_gather = [k.sem(f"e0_gather{q}") for q in range(2)]
        s_flush = [k.sem(f"e0_flush{q}") for q in range(2)]
        hid_ps = k.bank(0)
        w_ps = [k.bank(q, 2).rearrange("p (l n) -> p l n", l=LANES) for q in (1, 3)]
        agg_ps = [k.bank(5), k.bank(6)]
        NV = 22
        with nc.Block() as block:

            @block.sync
            def _(sp):
                sp.dma_start(fc1[:, :], a["L0_gnn_fc_w1"]).then_inc(s_weights, 16)
                sp.dma_start(b1[:, :], a["L0_gnn_fc_b1"].rearrange("(n a) -> n a", a=1)).then_inc(s_weights, 16)
                sp.dma_start(fc2[0:HID, :], a["L0_gnn_fc_w2"]).then_inc(s_weights, 16)
                sp.dma_start(fc2[HID:HID + 1, :], a["L0_gnn_fc_b2"].rearrange("(a n) -> a n", a=1)).then_inc(s_weights, 16)

                def load(i, par):
                    s = i + par
                    g = sp.value_load(k.step_group[0:1, bass.ds(s, 1)], min_val=0, max_val=GROUPS - 1)
                    k.wait(sp, s_gather[par], i * 32)
                    k.wait(sp, s_vec, (i + (par - 1)) * NV)
                    k.wait(sp, s_hid, i + (par - 1))
                    for t, name in ((idx, "src_g"), (dst, "dst_g"), (sh, "ea4_g")):
                        out = t[:, par, :, :].rearrange("p l c -> p (l c)") if name == "ea4_g" else t[:, par, :]
                        sp.dma_start(out, a[name][bass.ds(g * P, P), :]).then_inc(s_load[par], 16)
                    sp.dma_start(embed[:, par, :], a["ea8_g"][bass.ds(g * NB0, NB0), :]).then_inc(s_load[par], 16)

                def flush(i, par):
                    s = i + par
                    r = sp.value_load(k.step_row[0:1, bass.ds(s, 1)], min_val=0, max_val=WINDOWS + 1)
                    k.wait(sp, s_acc, s + 1)
                    sp.dma_start(k.agg0[bass.ds(r * P, P), :], acc[:, par, :]).then_inc(s_flush[par], 16)

                def step(i, par):
                    if live(i, par, STEPS):
                        load(i, par)
                    j, q = back(i, par, 2)
                    if live(j, q, STEPS):
                        flush(j, q)

                sweep(sp, STEPS, step, 2)
                for q in range(2):
                    sp.wait_ge(s_flush[q], 16 * (STEPS // 2))

            @block.gpsimd
            def _(pool):
                pool.memset(hid[HID:HID + 1, :, :], 1.0).then_inc(s_ones, 1)

                def gather(i, par):
                    k.wait(pool, s_load[par], uses(i, 4))
                    k.wait(pool, s_vec, (i + (par - 1)) * NV)
                    for lane in range(LANES):
                        pool.indirect_dma_start(
                            out=xg[:, par, lane, :], out_offset=None, in_=k.table0[:, :],
                            in_offset=bass.IndirectOffsetOnAxis(ap=idx[:, par, lane:lane + 1], axis=0),
                        ).then_inc(s_gather[par], 16)

                sweep(pool, STEPS, gather)

            @block.tensor
            def _(pe):
                def hidden(i, par):
                    pe.wait_ge(s_load[par], uses(i, 4))
                    wait(pe, s_hidS, i + par)
                    pe.matmul(hid_ps[0:HID, :], fc1[:, :], embed[:, par, :], start=True, stop=True).then_inc(s_hid, 1)

                def weights(i, par):
                    pe.wait_ge(s_hidS, i + (par + 1))
                    wait(pe, s_vec, (i + (par - 1)) * NV)
                    for lane in range(LANES):
                        ins = pe.matmul(w_ps[par][:, lane, 0:WN0],
                                        hid[:, par, lane * P:(lane + 1) * P], fc2[:, :], start=True, stop=True)
                    ins.then_inc(s_wps, 1)

                def sums(i, par):
                    pe.wait_ge(s_vec, (i + (par + 1)) * NV)
                    wait(pe, s_acc, i + (par - 1))
                    parts = ((0, 0, 160), (160, 160, 256), (256, 192, 288), (352, 192, 320))
                    for c, (o, lo, hi) in enumerate(parts):
                        for lane in range(LANES):
                            ins = pe.matmul(agg_ps[par][:, o:o + hi - lo], sel[:, par, lane, c, :], msg[:, par, lane, lo:hi],
                                            start=(lane == 0), stop=(lane == LANES - 1))
                    ins.then_inc(s_agg, 1)

                def step(i, par):
                    if live(i, par, STEPS):
                        hidden(i, par)
                        weights(i, par)
                    j, q = back(i, par, 1)
                    if live(j, q, STEPS):
                        sums(j, q)

                pe.wait_ge(s_weights, 64)
                pe.wait_ge(s_ones, 1)
                sweep(pe, STEPS, step, 1)

            @block.scalar
            def _(act):
                act.wait_ge(s_weights, 64)

                def silu(i, par):
                    act.wait_ge(s_hid, i + (par + 1))
                    wait(act, s_wps, i + (par - 1))
                    act.activation(hid[0:HID, par, :], hid_ps[0:HID, :], ACT.Silu, bias=b1[:, 0:1]).then_inc(s_hidS, 1)

                sweep(act, STEPS, silu)

            @block.vector
            def _(dve):
                def messages(i, par):
                    n0 = (i + par) * NV
                    dve.wait_ge(s_load[par], uses(i, 4))
                    wait(dve, s_agg, i + (par - 1))
                    base = k.step_base[:, bass.ds(i + par, 1)]
                    dve.tensor_scalar(rel[:, par, :], dst[:, par, :], base, None, ALU.subtract).then_inc(s_vec, 1)
                    dve.wait_ge(s_vec, n0 + 1)
                    for lane in range(LANES):
                        for c in range(4):
                            dve.tensor_scalar(sel[:, par, lane, c, :], k.iota[:, :], rel[:, par, lane:lane + 1],
                                              sh[:, par, lane, c:c + 1], ALU.is_equal, ALU.mult).then_inc(s_vec, 1)
                    dve.wait_ge(s_gather[par], uses(i, 4))
                    dve.wait_ge(s_wps, i + (par + 1))
                    w = w_ps[par]
                    s = xg[:, par, :, 0:S0]
                    v = xg[:, par, :, S0:D].rearrange("p l (c m) -> p l c m", c=3)
                    wv = lambda lo, n: bc(w[:, :, lo:lo + V0].rearrange("p l (a m) -> p l a m", a=1), [P, LANES, n, V0])
                    out = msg[:, par]
                    dve.tensor_tensor(out[:, :, 0:S0], w[:, :, 0:S0], s, ALU.mult).then_inc(s_vec, 1)
                    dve.tensor_tensor(out[:, :, 192:256], w[:, :, S0:2 * S0], s, ALU.mult).then_inc(s_vec, 1)
                    dve.tensor_tensor(out[:, :, S0:160].rearrange("p l (c m) -> p l c m", c=3), wv(128, 3), v,
                                      ALU.mult).then_inc(s_vec, 1)
                    dve.tensor_tensor(out[:, :, 160:192], w[:, :, 160:192], xg[:, par, :, S0:S0 + V0],
                                      ALU.mult).then_inc(s_vec, 1)
                    dve.tensor_tensor(out[:, :, 256:320].rearrange("p l (c m) -> p l c m", c=2), wv(160, 2), v[:, :, 1:3, :],
                                      ALU.mult).then_inc(s_vec, 1)

                add_sums = accumulate(k, dve, STEPS, s_agg, s_acc, s_flush, acc, agg_ps, AGG0)

                def step(i, par):
                    if live(i, par, STEPS):
                        messages(i, par)
                    j, q = back(i, par, 1)
                    if live(j, q, STEPS):
                        add_sums(j, q)

                sweep(dve, STEPS, step, 1)


def accumulate(k, dve, steps, s_agg, s_acc, s_flush, acc, agg_ps, width):
    def add_sums(i, par):
        dve.wait_ge(s_agg, i + (par + 1))
        wait(dve, s_flush[par], i * 8)
        wait(dve, s_acc, i + par)
        if isinstance(i, int) and i + par == 0:
            dve.tensor_copy(acc[:, par, :], agg_ps[par][:, 0:width]).then_inc(s_acc, 1)
        else:
            dve.scalar_tensor_tensor(acc[:, par, :], acc[:, 1 - par, :], k.step_keep[:, bass.ds(i + par, 1)],
                                     agg_ps[par][:, 0:width], ALU.mult, ALU.add).then_inc(s_acc, 1)
    return add_sums


class Count:

    def __init__(self, eng, sem, item, per):
        self.eng, self.sem, self.item, self.per, self.n = eng, sem, item, per, 0

    def __call__(self, ins):
        self.n += 1
        assert self.n <= self.per
        ins.then_inc(self.sem, 1)

    def last(self):
        self.eng.wait_ge(self.sem, self.item * self.per + self.n)


def edges1(k):
    nc, a = k.nc, k.a
    with ExitStack() as ctx:
        sb = lambda name, shape, dt=F32: k.sb("e1_" + name, shape, dt, ctx)
        w_rbf = sb("w_rbf", [NB1, WN1])
        ws_val, ws_val_t, wg = sb("ws_val", [96, S0]), sb("ws_val_t", [S0, 96]), sb("wg", [S0, V0])
        adot = sb("adot", [P, HEADS * AS])
        w1a, w1b, w1c = sb("w1a", [96, 160]), sb("w1b", [P, P]), sb("w1c", [P, P])
        w2a, w2b, w2c = sb("w2a", [96, D]), sb("w2b", [P, 192]), sb("w2c", [P, 192])
        c2a, c2b, c2c = sb("c2a", [96, 1]), sb("c2b", [P, 1]), sb("c2c", [P, 1])
        idx_s, idx_d = sb("idx_s", [P, 2, LANES], I32), sb("idx_d", [P, 2, LANES], I32)
        y_in = sb("y_in", [P, 2, LANES, 4])
        rbf = sb("rbf", [NB1, 2, GE])
        row_s, row_d = sb("row_s", [P, 2, LANES, D]), sb("row_d", [P, 2, LANES, D])
        y = sb("y", [P, 2, LANES, 6])
        y_late = sb("y_late", [P, 2, LANES, 3])
        msg, msg0 = sb("msg", [P, LANES, D]), sb("msg0", [P, LANES, D])
        vy = sb("vy", [P, LANES, 3, V0])
        cross_a, cross_b = sb("cross_a", [P, LANES, 96]), sb("cross_b", [P, LANES, 96])
        dot = sb("dot", [P, LANES, V0])
        dot2 = sb("dot2", [P, LANES, V0])
        q1, q2 = sb("q1", [P, LANES, QW]), sb("q2", [P, LANES, QW])
        t1, t2 = sb("t1", [P, 3, GE]), sb("t2", [P, 3, GE])
        gate = sb("gate", [P, LANES, V0])
        low = sb("low", [P, LANES, HEADS * AS])
        leaky = sb("leaky", [P, LANES, HEADS * AS])
        val = sb("val", [P, LANES, 96])
        sxy = sb("sxy", [P, LANES, 3, V0])
        outv = sb("outv", [P, 2, LANES, 192])
        outl = sb("outl", [P, 2, LANES, HEADS])
        names = ["zero", "weights", "chain", "pre", "wg", "ready", "w", "tp1", "mid", "post", "turn1", "turned1", "turn2",
                 "turned2", "val", "sig", "prod2", "copied"]
        (s_zero, s_weights, s_chain, s_pre, s_wg, s_ready, s_w, s_tp1, s_mid, s_post, s_turn1, s_turned1, s_turn2,
         s_turned2, s_val, s_sig, s_prod2, s_copied) = [k.sem("e1_" + n) for n in names]
        s_load = [k.sem(f"e1_load{q}") for q in range(2)]
        s_gather = [k.sem(f"e1_gather{q}") for q in range(2)]
        s_store = [k.sem(f"e1_store{q}") for q in range(2)]
        w_ps = k.bank(0, 2).rearrange("p (l n) -> p l n", l=LANES)
        turn_ps = k.bank(2)
        val_ps = k.bank(3, 2).rearrange("p (l n) -> p l n", l=LANES)
        vec_ps = k.bank(5).rearrange("p (l n) -> p l n", l=LANES)
        out_ps = k.bank(6, 2).rearrange("p (l n) -> p l n", l=LANES)
        K1, KM, KP = 17, 17, 4
        CHUNKS = ((0, 96), (96, P), (224, P))
        Wsv, Wvv, Wvs, Wvl = a["L1_gnn_Ws_val"], a["L1_gnn_Wv_val"], a["L1_gnn_Ws_vlin"], a["L1_gnn_Wv_vlin"]
        col = lambda name: a["L1_gnn_" + name].rearrange("(n a) -> n a", a=1)

        def head_cols(ap, lo, n):
            return ap[:, 0:D].rearrange("p (h n) -> p h n", h=HEADS)[:, :, lo:lo + n]

        def weight_loads():
            by_head = lambda w, n: w.rearrange("p (h n) -> p h n", h=HEADS)
            yield w_rbf[:, :], a["L1_gnn_W_rbf"]
            yield ws_val[:, :], Wsv
            yield wg[:, :], a["L1_gnn_Wg"]
            yield adot[:, :], a["L1_gnn_alpha_dot"].rearrange("a h s -> a (h s)").to_broadcast([P, HEADS * AS])
            yield w1a[:, 0:S0], Wsv
            yield w1a[:, 96:160], a["L1_gnn_W_alpha"]
            yield w1b[0:S0, 96:P], Wvv[0:S0, :]
            yield w1b[64:96, 0:32], Wvv[S0:96, :]
            yield w1b[96:P, 32:64], Wvv[S0:96, :]
            yield w1c[0:32, 64:96], Wvv[S0:96, :]
            for c in range(3):
                yield w1c[32 + 32 * c:64 + 32 * c, 32 * c:32 * c + 32], Wvv[96:P, :]
            yield head_cols(w2a[:, :], 0, AS), by_head(Wvs, AS)
            yield w2b[0:S0, D:192], Wvl[0:S0, :]
            for c in range(2):
                yield head_cols(w2b[64 + 32 * c:96 + 32 * c, :], AS + AV * c, AV), by_head(Wvl[S0:96, :], AV)
            yield head_cols(w2c[0:32, :], AS + 2 * AV, AV), by_head(Wvl[S0:96, :], AV)
            for c in range(3):
                yield head_cols(w2c[32 + 32 * c:64 + 32 * c, :], AS + AV * c, AV), by_head(Wvl[96:P, :], AV)
            yield c2a[0:S0, :], col("w2_ss")
            yield c2a[S0:96, :], col("w2_vv0")
            yield c2b[0:S0, :], col("w2_sv")
            yield c2b[64:96, :], col("w2_vs")
            yield c2b[96:P, :], col("w2_vs")
            yield c2c[0:32, :], col("w2_vs")
            for c in range(3):
                yield c2c[32 + 32 * c:64 + 32 * c, :], col("w2_vv1")

        n_weights = 16 * 30
        with nc.Block() as block:

            @block.sync
            def _(sp):
                sp.wait_ge(s_zero, 5)
                n = 0
                for t, w in weight_loads():
                    sp.dma_start(t, w).then_inc(s_weights, 16)
                    n += 16
                assert n == n_weights, n

                def load(i, par):
                    g = i + par
                    k.wait(sp, s_gather[par], i * 64)
                    k.wait(sp, s_tp1, (i + (par - 1)) * K1)
                    k.wait(sp, s_w, i + (par - 1))
                    sp.dma_start(idx_s[:, par, :], a["src_g"][bass.ds(g * P, P), :]).then_inc(s_load[par], 16)
                    sp.dma_start(idx_d[:, par, :], a["dst_g"][bass.ds(g * P, P), :]).then_inc(s_load[par], 16)
                    sp.dma_start(y_in[:, par, :, :].rearrange("p l c -> p (l c)"),
                                 a["ea4_g"][bass.ds(g * P, P), :]).then_inc(s_load[par], 16)
                    sp.dma_start(rbf[:, par, :], a["ea16_g"][bass.ds(g * NB1, NB1), :]).then_inc(s_load[par], 16)

                def store(i, par):
                    g = i + par
                    k.wait(sp, s_post, (g + 1) * KP)
                    sp.dma_start(k.values.rearrange("(q l) d -> q l d", l=LANES)[bass.ds(g * P, P), :, :],
                                 outv[:, par, :, 0:D]).then_inc(s_store[par], 16)
                    sp.dma_start(k.logits.rearrange("(q l) h -> q (l h)", l=LANES)[bass.ds(g * P, P), :],
                                 outl[:, par, :, :].rearrange("p l h -> p (l h)")).then_inc(s_store[par], 16)

                def step(i, par):
                    if live(i, par, GROUPS):
                        load(i, par)
                    j, q = back(i, par, 4)
                    if live(j, q, GROUPS):
                        store(j, q)

                sweep(sp, GROUPS, step, 4, first=4)
                for q in range(2):
                    sp.wait_ge(s_store[q], 32 * (GROUPS // 2))

            @block.gpsimd
            def _(pool):
                for t in (w1b, w1c, w2a, w2b, w2c):
                    pool.memset(t[:, :], 0.0).then_inc(s_zero, 1)

                def gather(i, par):
                    k.wait(pool, s_load[par], uses(i, 4))
                    k.wait(pool, s_tp1, (i + (par - 1)) * K1)
                    for lane in range(LANES):
                        for rows, table, idx in ((row_s, k.table_src, idx_s), (row_d, k.table_dst, idx_d)):
                            pool.indirect_dma_start(
                                out=rows[:, par, lane, :], out_offset=None, in_=table[:, :],
                                in_offset=bass.IndirectOffsetOnAxis(ap=idx[:, par, lane:lane + 1], axis=0),
                            ).then_inc(s_gather[par], 16)

                sweep(pool, GROUPS, gather)

            @block.tensor
            def _(pe):
                pe.wait_ge(s_weights, n_weights)
                pe.transpose(turn_ps[0:S0, 0:96], ws_val[:, :], k.ident[0:96, 0:96]).then_inc(s_pre, 1)
                pe.wait_ge(s_wg, 1)
                pe.matmul(val_ps[0:96, 0, 0:V0], ws_val_t[:, :], wg[:, :], start=True, stop=True).then_inc(s_pre, 1)
                pe.wait_ge(s_ready, 1)

                def radial(i, par):
                    pe.wait_ge(s_load[par], uses(i, 4))
                    wait(pe, s_tp1, (i + par) * K1)
                    for lane in range(LANES):
                        ins = pe.matmul(w_ps[:, lane, 0:WN1], rbf[:, par, lane * P:(lane + 1) * P], w_rbf[:, :],
                                        start=True, stop=True)
                    ins.then_inc(s_w, 1)

                def turn(src, chunk, sem):
                    lo, m = CHUNKS[chunk]
                    for lane in range(LANES):
                        ins = pe.transpose(turn_ps[0:m, lane * P:(lane + 1) * P], src[:, lane, lo:lo + m], k.ident[:, :])
                    ins.then_inc(sem, 1)

                def turn_first(i, par):
                    g = i + par
                    pe.wait_ge(s_tp1, (g + 1) * K1)
                    wait(pe, s_turned2, (g - 1) * 3)
                    for c in range(3):
                        wait(pe, s_turned1, g * 3 + c)
                        turn(q1, c, s_turn1)

                def turn_second(i, par):
                    g = i + par
                    pe.wait_ge(s_mid, (g + 1) * KM)
                    pe.wait_ge(s_turned1, min(g + 2, GROUPS) * 3 if isinstance(g, int) else (g + 2) * 3)
                    for c in range(3):
                        wait(pe, s_turned2, g * 3 + c)
                        turn(q2, c, s_turn2)

                def values(i, par):
                    g = i + par
                    pe.wait_ge(s_turned1, (g + 1) * 3)
                    wait(pe, s_mid, g * KM)
                    for lane in range(LANES):
                        e = slice(lane * P, (lane + 1) * P)
                        pe.matmul(val_ps[:, lane, 0:160], t1[0:96, 0, e], w1a[:, :], start=True, stop=True)
                        pe.matmul(vec_ps[:, lane, :], t1[:, 1, e], w1b[:, :], start=True, stop=False)
                        ins = pe.matmul(vec_ps[:, lane, :], t1[:, 2, e], w1c[:, :], start=False, stop=True)
                    ins.then_inc(s_val, 1)

                def outputs(i, par):
                    g = i + par
                    pe.wait_ge(s_turned2, (g + 1) * 3)
                    wait(pe, s_copied, g)
                    for lane in range(LANES):
                        e = slice(lane * P, (lane + 1) * P)
                        pe.matmul(out_ps[:, lane, 0:192], t2[:, 1, e], w2b[:, :], start=True, stop=False)
                        pe.matmul(out_ps[:, lane, 0:D], t2[0:96, 0, e], w2a[:, :], start=False, stop=False,
                                  skip_group_check=True)
                        ins = pe.matmul(out_ps[:, lane, 0:192], t2[:, 2, e], w2c[:, :], start=False, stop=True)
                    ins.then_inc(s_prod2, 1)

                def step(i, par):
                    if live(i, par, GROUPS):
                        turn_first(i, par)
                    j, q = back(i, par, -1)
                    if not isinstance(j, int) or j + q < GROUPS:
                        radial(j, q)
                    j, q = back(i, par, 1)
                    if live(j, q, GROUPS):
                        turn_second(j, q)
                        outputs(j, q)
                    if live(i, par, GROUPS):
                        values(i, par)

                radial(0, 0)
                sweep(pe, GROUPS, step, 1, last=2)

            @block.scalar
            def _(act):
                act.wait_ge(s_pre, 1)
                act.copy(ws_val_t[:, :], turn_ps[0:S0, 0:96]).then_inc(s_wg, 1)

                def evacuate(i, par, dst, turn_sem, turned_sem):
                    g = i + par
                    for c, (lo, m) in enumerate(CHUNKS):
                        act.wait_ge(turn_sem, g * 3 + (c + 1))
                        if c == 0:
                            wait(act, s_val if dst is t1 else s_prod2, g)
                        act.copy(dst[0:m, c, :], turn_ps[0:m, :]).then_inc(turned_sem, 1)

                def gates(i, par):
                    g = i + par
                    act.wait_ge(s_val, g + 1)
                    act.activation(q2[:, :, 96:160], val_ps[:, :, 0:S0], ACT.Sigmoid).then_inc(s_sig, 1)
                    act.activation(gate[:, :, :], val_ps[:, :, S0:96], ACT.Sigmoid).then_inc(s_sig, 1)
                    act.mul(low[:, :, :], val_ps[:, :, 96:160], 0.2).then_inc(s_sig, 1)

                def copy_out(i, par):
                    g = i + par
                    act.wait_ge(s_prod2, g + 1)
                    wait(act, s_store[par], i * 16)
                    act.copy(outv[:, par, :, :], out_ps[:, :, 0:192]).then_inc(s_copied, 1)

                def step(i, par):
                    if live(i, par, GROUPS):
                        evacuate(i, par, t1, s_turn1, s_turned1)
                    j, q = back(i, par, 1)
                    if live(j, q, GROUPS):
                        evacuate(j, q, t2, s_turn2, s_turned2)
                        copy_out(j, q)
                    if live(i, par, GROUPS):
                        gates(i, par)

                sweep(act, GROUPS, step, 1)

            @block.vector
            def _(dve):
                link = Chain(dve, s_chain)
                dve.wait_ge(s_weights, n_weights)
                dve.wait_ge(s_pre, 2)
                link(dve.tensor_copy(w1a[:, S0:96], val_ps[0:96, 0, 0:V0]))
                link(dve.tensor_scalar(w1a[S0:96, :], w1a[S0:96, :], 1.0 / R3, None, ALU.mult))
                for c in range(3):
                    r = slice(32 + 32 * c, 64 + 32 * c)
                    link(dve.tensor_scalar(w1c[r, :], w1c[r, :], 1.0 / R2, None, ALU.mult))
                    link(dve.tensor_scalar(c2c[r, :], c2c[r, :], 1.0 / R2, None, ALU.mult))
                link(dve.tensor_scalar(c2a[S0:96, :], c2a[S0:96, :], 1.0 / R3, None, ALU.mult))
                for w, c in ((w2a, c2a), (w2b, c2b), (w2c, c2c)):
                    link(dve.tensor_scalar(w[:, :], w[:, :], c[:, 0:1], None, ALU.mult))
                dve.memset(dot2[:, 0, 0:1], 0.0).then_inc(s_ready, 1)

                lane = lambda ap, n: bc(ap, [P, LANES, n])
                comp = lambda ap: ap.rearrange("p l (c m) -> p l c m", c=3)
                one = lambda ap: ap.rearrange("p l (a m) -> p l a m", a=1)

                def times_y(done, out, v, ys):
                    done(dve.tensor_tensor(out, v, bc(ys.rearrange("p l (c a) -> p l c a", a=1), [P, LANES, 3, V0]), ALU.mult))

                def cross_dot(done, v, ys):
                    two = lambda ap: ap.rearrange("p l (c m) -> p l c m", c=2)
                    yb = lambda lo, n: bc(ys[:, :, lo:lo + n].rearrange("p l (c a) -> p l c a", a=1), [P, LANES, n, V0])
                    done(dve.tensor_tensor(two(cross_a[:, :, 0:64]), two(v[:, :, 32:96]), yb(3, 2), ALU.mult))
                    done(dve.tensor_tensor(one(cross_a[:, :, 64:96]), one(v[:, :, 0:32]), yb(5, 1), ALU.mult))
                    done(dve.tensor_tensor(one(cross_b[:, :, 0:32]), one(v[:, :, 64:96]), yb(2, 1), ALU.mult))
                    done(dve.tensor_tensor(two(cross_b[:, :, 32:96]), two(v[:, :, 0:64]), yb(3, 2), ALU.mult))
                    times_y(done, vy[:, :, :, :], comp(v), ys[:, :, 1:4])
                    done.last()
                    done(dve.tensor_tensor(dot2[:, :, :], vy[:, :, 0, :], vy[:, :, 1, :], ALU.add))

                def first(i, par):
                    g = i + par
                    done = Count(dve, s_tp1, g, K1)
                    wait(dve, s_mid, (g - 1) * KM)
                    dve.wait_ge(s_load[par], uses(i, 4))
                    done(dve.tensor_copy(y[:, par, :, 0:4], y_in[:, par, :, :]))
                    done(dve.tensor_copy(y[:, par, :, 4:6], y_in[:, par, :, 1:3]))
                    dve.wait_ge(s_gather[par], uses(i, 8))
                    done(dve.tensor_tensor(msg[:, :, :], row_s[:, par, :, :], row_d[:, par, :, :], ALU.add))
                    done.last()
                    ys = y[:, par, :, :]
                    done(dve.tensor_tensor(msg0[:, :, :], msg[:, :, :], lane(ys[:, :, 0:1], D), ALU.mult))
                    cross_dot(done, msg[:, :, S0:D], ys)
                    done.last()
                    done(dve.tensor_tensor(dot[:, :, :], dot2[:, :, :], vy[:, :, 2, :], ALU.add))
                    done(dve.tensor_tensor(cross_a[:, :, :], cross_a[:, :, :], cross_b[:, :, :], ALU.subtract))
                    wait(dve, s_turn1, g * 3)
                    dve.wait_ge(s_w, g + 1)
                    w = w_ps
                    wv = lambda lo: bc(one(w[:, :, lo:lo + V0]), [P, LANES, 3, V0])
                    done(dve.tensor_tensor(q1[:, :, 0:S0], w[:, :, 0:S0], msg0[:, :, 0:S0], ALU.mult))
                    done(dve.tensor_tensor(q1[:, :, 96:160], w[:, :, S0:2 * S0], msg[:, :, 0:S0], ALU.mult))
                    done(dve.tensor_tensor(comp(q1[:, :, 160:256]), wv(128), comp(msg0[:, :, S0:D]), ALU.mult))
                    done.last()
                    done(dve.tensor_tensor(q1[:, :, S0:96], w[:, :, 160:192], dot[:, :, :], ALU.mult))
                    done(dve.tensor_tensor(comp(q1[:, :, 256:352]), wv(192), comp(cross_a[:, :, :]), ALU.mult))
                    assert done.n == K1, done.n

                def middle(i, par):
                    g = i + par
                    done = Count(dve, s_mid, g, KM)
                    ys = y[:, par, :, :]
                    dve.wait_ge(s_tp1, min(g + 2, GROUPS) * K1 if isinstance(g, int) else (g + 2) * K1)
                    wait(dve, s_post, g * KP)
                    dve.wait_ge(s_sig, (g + 1) * 3)
                    times_y(done, sxy[:, :, :, :], bc(one(vec_ps[:, :, 96:P]), [P, LANES, 3, V0]), ys[:, :, 1:4])
                    done.last()
                    done(dve.tensor_tensor(comp(val[:, :, :]), sxy[:, :, :, :], comp(vec_ps[:, :, 0:96]), ALU.add))
                    done(dve.tensor_tensor(leaky[:, :, :], val_ps[:, :, 96:160], low[:, :, :], ALU.max))
                    done.last()
                    done(dve.tensor_tensor(comp(val[:, :, :]), comp(val[:, :, :]), bc(one(gate[:, :, :]), [P, LANES, 3, V0]), ALU.mult))
                    done(dve.tensor_tensor(leaky[:, :, :], leaky[:, :, :],
                                           bc(adot[:, :].rearrange("p (a n) -> p a n", a=1), [P, LANES, HEADS * AS]), ALU.mult))
                    done(dve.tensor_copy(y_late[:, par, :, :], ys[:, :, 1:4]))
                    done.last()
                    wait(dve, s_store[par], i * 16)
                    done(dve.tensor_reduce(outl[:, par, :, :], leaky[:, :, :].rearrange("p l (h s) -> p l h s", h=HEADS),
                                           AX, ALU.add))
                    done(dve.tensor_tensor(q2[:, :, 0:S0], q2[:, :, 96:160], lane(ys[:, :, 0:1], S0), ALU.mult))
                    done(dve.tensor_tensor(q2[:, :, 160:256], val[:, :, :], lane(ys[:, :, 0:1], 96), ALU.mult))
                    cross_dot(done, val[:, :, :], ys)
                    done.last()
                    done(dve.tensor_tensor(q2[:, :, S0:96], dot2[:, :, :], vy[:, :, 2, :], ALU.add))
                    done(dve.tensor_tensor(q2[:, :, 256:352], cross_a[:, :, :], cross_b[:, :, :], ALU.subtract))
                    assert done.n == KM, done.n

                def post(i, par):
                    g = i + par
                    done = Count(dve, s_post, g, KP)
                    dve.wait_ge(s_copied, g + 1)
                    dve.wait_ge(s_mid, (g + 1) * KM)
                    times_y(done, sxy[:, :, :, :], bc(one(outv[:, par, :, D:192]), [P, LANES, 3, V0]), y_late[:, par, :, :])
                    done.last()
                    for c in range(3):
                        lo = AS + AV * c
                        t = outv[:, par, :, 0:D].rearrange("p l (h n) -> p l h n", h=HEADS)[:, :, :, lo:lo + AV]
                        done(dve.tensor_tensor(t, t, sxy[:, :, c, :].rearrange("p l (h n) -> p l h n", h=HEADS), ALU.add))

                def step(i, par):
                    if live(i, par, GROUPS):
                        first(i, par)
                    j, q = back(i, par, 2)
                    if live(j, q, GROUPS):
                        post(j, q)
                    j, q = back(i, par, 1)
                    if live(j, q, GROUPS):
                        middle(j, q)

                sweep(dve, GROUPS, step, 2)


def softmax_weights(k):
    nc, a = k.nc, k.a
    with ExitStack() as ctx:
        sb = lambda name, shape, dt=F32: k.sb("sm_" + name, shape, dt, ctx)
        lg, run, top = sb("lg", [P, CH, HEADS]), sb("run", [P, CH, HEADS]), sb("top", [P, CH, HEADS])
        cur, near = sb("cur", [P, CH], I32), sb("near", [P, 2, CH], I32)
        pen = sb("pen", [P, 2, CH])
        ends = sb("ends", [P, 2 * HEADS])
        rows = sb("rows", [HEADS, 2 * P])
        inc = sb("inc", [HEADS, P])
        hand = sb("hand", [HEADS, P])
        start = sb("start", [P, HEADS])
        s_load, s_chain, s_pe, s_ends = k.sem("sm_load"), k.sem("sm_chain"), k.sem("sm_pe"), k.sem("sm_ends")
        s_exp, s_max, s_out = k.sem("sm_exp"), k.sem("sm_max"), k.sem("sm_out")
        flat = lambda t: t.rearrange("(p n) h -> p (n h)", p=P)
        edge = a["dst_edge"]
        with nc.Block() as block:

            @block.sync
            def _(sp):
                sp.dma_start(lg[:, :, :].rearrange("p n h -> p (n h)"), flat(k.logits)).then_inc(s_load, 16)
                for t, off in ((cur[:, :], 1), (near[:, 0, :], 0), (near[:, 1, :], 2)):
                    sp.dma_start(t, edge[off:off + EP].rearrange("(p n) -> p n", p=P)).then_inc(s_load, 16)
                sp.wait_ge(s_exp, 1)
                sp.dma_start(flat(k.weights_e), lg[:, :, :].rearrange("p n h -> p (n h)")).then_inc(s_out, 16)
                sp.wait_ge(s_out, 16)

            @block.tensor
            def _(pe):
                for d in range(2):
                    pe.wait_ge(s_ends, 2 * d + 1)
                    pe.transpose(k.bank(0)[0:HEADS, 0:P], ends[:, 0:HEADS], k.ident[:, :])
                    pe.transpose(k.bank(0)[0:HEADS, P:2 * P], ends[:, HEADS:2 * HEADS], k.ident[:, :]).then_inc(s_pe, 1)
                    pe.wait_ge(s_ends, 2 * d + 2)
                    pe.transpose(k.bank(1)[:, 0:HEADS], hand[:, :], k.ident[0:HEADS, 0:HEADS]).then_inc(s_pe, 1)

            @block.scalar
            def _(act):
                act.wait_ge(s_max, 1)
                act.activation(lg[:, :, :], lg[:, :, :], ACT.Exp).then_inc(s_exp, 1)

            @block.vector
            def _(dve):
                link = Chain(dve, s_chain)
                dve.wait_ge(s_load, 64)
                for d in range(2):
                    link(dve.tensor_tensor(pen[:, d, :], cur[:, :], near[:, d, :], ALU.is_equal))
                    link(dve.tensor_scalar(pen[:, d, :], pen[:, d, :], 1.0, BIG, ALU.subtract, ALU.mult))
                for d, (src, out) in enumerate(((lg, run), (run, top))):
                    way = (lambda t: t[:, ::-1]) if d else (lambda t: t)
                    end = 0 if d else CH - 1
                    for h in range(HEADS):
                        link(dve.tensor_tensor_scan(way(out[:, :, h]), way(pen[:, d, :]), way(src[:, :, h]), -BIG,
                                                    ALU.add, ALU.max))
                    link(dve.tensor_copy(ends[:, 0:HEADS], out[:, end, :]))
                    link(dve.tensor_reduce(ends[:, HEADS:HEADS + 1], pen[:, d, :], AX, ALU.min))
                    dve.tensor_copy(ends[:, HEADS + 1:2 * HEADS],
                                    bc(ends[:, HEADS:HEADS + 1], [P, HEADS - 1])).then_inc(s_ends, 1)
                    dve.wait_ge(s_pe, 2 * d + 1)
                    link(dve.tensor_copy(rows[:, :], k.bank(0)[0:HEADS, 0:2 * P]))
                    link(dve.tensor_tensor_scan(way(inc[:, :]), way(rows[:, P:2 * P]), way(rows[:, 0:P]), -BIG, ALU.add, ALU.max))
                    link(dve.memset(hand[:, :], -BIG))
                    if d:
                        dve.tensor_copy(hand[:, 0:P - 1], inc[:, 1:P]).then_inc(s_ends, 1)
                    else:
                        dve.tensor_copy(hand[:, 1:P], inc[:, 0:P - 1]).then_inc(s_ends, 1)
                    dve.wait_ge(s_pe, 2 * d + 2)
                    link(dve.tensor_copy(start[:, :], k.bank(1)[:, 0:HEADS]))
                    for h in range(HEADS):
                        link(dve.tensor_tensor_scan(way(out[:, :, h]), way(pen[:, d, :]), way(src[:, :, h]),
                                                    start[:, h:h + 1], ALU.add, ALU.max))
                dve.tensor_tensor(lg[:, :, :], lg[:, :, :], top[:, :, :], ALU.subtract).then_inc(s_max, 1)


def sums1(k):
    nc, a = k.nc, k.a
    with ExitStack() as ctx:
        sb = lambda name, shape, dt=F32: k.sb("s1_" + name, shape, dt, ctx)
        dst = sb("dst", [P, 2, LANES], I32)
        ex = sb("ex", [P, 2, LANES, HEADS])
        value = sb("value", [P, 2, LANES, D])
        rel = sb("rel", [P, 2, LANES])
        sel = sb("sel", [P, 2, LANES, P])
        rhs = sb("rhs", [P, 2, LANES, AGG1])
        acc = sb("acc", [P, 2, AGG1])
        s_vec, s_agg, s_acc = k.sem("s1_vec"), k.sem("s1_agg"), k.sem("s1_acc")
        s_load = [k.sem(f"s1_load{q}") for q in range(2)]
        s_flush = [k.sem(f"s1_flush{q}") for q in range(2)]
        agg_ps = [k.bank(5), k.bank(6)]
        NV = 7
        with nc.Block() as block:

            @block.sync
            def _(sp):
                def load(i, par):
                    g = sp.value_load(k.step_group[0:1, bass.ds(i + par, 1)], min_val=0, max_val=GROUPS - 1)
                    k.wait(sp, s_vec, (i + (par - 1)) * NV)
                    sp.dma_start(dst[:, par, :], a["dst_g"][bass.ds(g * P, P), :]).then_inc(s_load[par], 16)
                    sp.dma_start(ex[:, par, :, :].rearrange("p l h -> p (l h)"),
                                 k.weights_e.rearrange("(q l) h -> q (l h)", l=LANES)[bass.ds(g * P, P), :]).then_inc(s_load[par], 16)
                    sp.dma_start(value[:, par, :, :].rearrange("p l d -> p (l d)"),
                                 k.values.rearrange("(q l) d -> q (l d)", l=LANES)[bass.ds(g * P, P), :]).then_inc(s_load[par], 16)

                def flush(i, par):
                    r = sp.value_load(k.step_row[0:1, bass.ds(i + par, 1)], min_val=0, max_val=WINDOWS + 1)
                    k.wait(sp, s_acc, i + (par + 1))
                    sp.dma_start(k.agg1[bass.ds(r * P, P), :], acc[:, par, :]).then_inc(s_flush[par], 16)

                def step(i, par):
                    if live(i, par, STEPS):
                        load(i, par)
                    j, q = back(i, par, 2)
                    if live(j, q, STEPS):
                        flush(j, q)

                sweep(sp, STEPS, step, 2)
                for q in range(2):
                    sp.wait_ge(s_flush[q], 16 * (STEPS // 2))

            @block.tensor
            def _(pe):
                def sums(i, par):
                    pe.wait_ge(s_vec, (i + (par + 1)) * NV)
                    wait(pe, s_acc, i + (par - 1))
                    for lane in range(LANES):
                        ins = pe.matmul(agg_ps[par][:, 0:AGG1], sel[:, par, lane, :], rhs[:, par, lane, :],
                                        start=(lane == 0), stop=(lane == LANES - 1))
                    ins.then_inc(s_agg, 1)

                sweep(pe, STEPS, sums)

            @block.vector
            def _(dve):
                def weigh(i, par):
                    done = Count(dve, s_vec, i + par, NV)
                    dve.wait_ge(s_load[par], uses(i, 3))
                    wait(dve, s_agg, i + (par - 1))
                    done(dve.tensor_scalar(rel[:, par, :], dst[:, par, :], k.step_base[:, bass.ds(i + par, 1)], None, ALU.subtract))
                    done.last()
                    for lane in range(LANES):
                        done(dve.tensor_scalar(sel[:, par, lane, :], k.iota[:, :], rel[:, par, lane:lane + 1], None, ALU.is_equal))
                    by_head = lambda t: t.rearrange("p l (h n) -> p l h n", h=HEADS)
                    done(dve.tensor_tensor(by_head(rhs[:, par, :, 0:D]), by_head(value[:, par, :, :]),
                                           bc(ex[:, par, :, :].rearrange("p l (h a) -> p l h a", a=1), [P, LANES, HEADS, D // HEADS]), ALU.mult))
                    done(dve.tensor_copy(rhs[:, par, :, D:AGG1], ex[:, par, :, :]))

                add_sums = accumulate(k, dve, STEPS, s_agg, s_acc, s_flush, acc, agg_ps, AGG1)

                def step(i, par):
                    if live(i, par, STEPS):
                        weigh(i, par)
                    j, q = back(i, par, 1)
                    if live(j, q, STEPS):
                        add_sums(j, q)

                sweep(dve, STEPS, step, 1)


def output(k):
    nc, a, W = k.nc, k.a, WINDOWS
    with ExitStack() as ctx:
        sb = lambda name, shape, dt=F32: k.sb("o_" + name, shape, dt, ctx)
        sums = sb("sums", [P, W, AGG1])
        rden = sb("rden", [P, W, HEADS])
        wt = sb("wt", [P, 2, D])
        stage = sb("stage", [P, 2, D])
        turned = sb("turned", [P, 2, 2 * P])
        outb = sb("outb", [P, 2, D])
        s_zero, s_weights, s_sums, s_chain = k.sem("o_zero"), k.sem("o_weights"), k.sem("o_sums"), k.sem("o_chain")
        s_stage, s_turn, s_turned, s_prod, s_out = [k.sem("o_" + n) for n in ("stage", "turn", "turned", "prod", "out")]
        s_store = [k.sem(f"o_store{q}") for q in range(2)]
        turn_ps, prod_ps = [k.bank(0), k.bank(1)], [k.bank(2), k.bank(3)]
        n_dma = 17 * 16
        with nc.Block() as block:

            @block.gpsimd
            def _(pool):
                pool.memset(wt[:, :, :], 0.0).then_inc(s_zero, 1)

            @block.sync
            def _(sp):
                sp.dma_start(sums[:, :, :], k.agg1[0:NP, :].rearrange("(j p) d -> p j d", p=P)).then_inc(s_sums, 16)
                sp.wait_ge(s_zero, 1)
                n = 0
                for h in range(HEADS):
                    r = 40 * h
                    n += place(sp, s_weights, wt, r, 0, a["L1_gnn_Wps"][AS * h:AS * (h + 1), :])
                    for c in range(3):
                        n += place(sp, s_weights, wt, r + AS + AV * c, S0 + V0 * c, a["L1_gnn_Wpv"][AV * h:AV * (h + 1), :])
                assert n == n_dma, n

                def store(i, par):
                    g = i + par
                    k.wait(sp, s_out, g + 1)
                    m = N - g * P if isinstance(g, int) and g == W - 1 else P
                    sp.dma_start(a["out"][bass.ds(g * P, m), :], outb[0:m, par, :]).then_inc(s_store[par], 16)

                sweep(sp, W, store)
                sp.wait_ge(s_store[0], 16 * ((W + 1) // 2))
                sp.wait_ge(s_store[1], 16 * (W // 2))

            @block.tensor
            def _(pe):
                def turn(i, par):
                    pe.wait_ge(s_stage, i + (par + 1))
                    wait(pe, s_turned, (i + (par - 1)) * 2)
                    pe.transpose(turn_ps[par][:, 0:P], stage[:, par, 0:P], k.ident[:, :])
                    pe.transpose(turn_ps[par][0:D - P, P:2 * P], stage[:, par, P:D], k.ident[:, :]).then_inc(s_turn, 1)

                def product(i, par):
                    pe.wait_ge(s_turned, (i + (par + 1)) * 2)
                    wait(pe, s_out, i + (par - 1))
                    pe.matmul(prod_ps[par][:, 0:D], turned[:, par, 0:P], wt[:, 0, :], start=True, stop=False)
                    pe.matmul(prod_ps[par][:, 0:D], turned[0:D - P, par, P:2 * P], wt[0:D - P, 1, :],
                              start=False, stop=True).then_inc(s_prod, 1)

                def step(i, par):
                    if live(i, par, W):
                        turn(i, par)
                    j, q = back(i, par, 1)
                    if live(j, q, W):
                        product(j, q)

                pe.wait_ge(s_weights, n_dma)
                sweep(pe, W, step, 1)

            @block.scalar
            def _(act):
                def evacuate(i, par):
                    act.wait_ge(s_turn, i + (par + 1))
                    wait(act, s_prod, i + (par - 1))
                    act.copy(turned[:, par, 0:P], turn_ps[par][:, 0:P]).then_inc(s_turned, 1)
                    act.copy(turned[0:D - P, par, P:2 * P], turn_ps[par][0:D - P, P:2 * P]).then_inc(s_turned, 1)

                sweep(act, W, evacuate)

            @block.vector
            def _(dve):
                link = Chain(dve, s_chain)
                dve.wait_ge(s_sums, 16)
                link(dve.tensor_scalar(rden[:, :, :], sums[:, :, D:AGG1], 1e-16, None, ALU.add))
                link(dve.reciprocal(rden[:, :, :], rden[:, :, :]))
                def scale(i, par):
                    wait(dve, s_turn, i + (par - 1))
                    j = bass.ds(i + par, 1)
                    dve.tensor_tensor(stage[:, par, :].rearrange("p (a h n) -> p a h n", a=1, h=HEADS),
                                      sums[:, j, 0:D].rearrange("p a (h n) -> p a h n", h=HEADS),
                                      bc(rden[:, j, :].rearrange("p a (h b) -> p a h b", b=1), [P, 1, HEADS, D // HEADS]),
                                      ALU.mult).then_inc(s_stage, 1)

                def emit(i, par):
                    dve.wait_ge(s_prod, i + (par + 1))
                    wait(dve, s_store[par], i * 8)
                    j = bass.ds(i + par, 1)
                    dve.tensor_tensor(outb[:, par, 0:S0].rearrange("p (a n) -> p a n", a=1),
                                      prod_ps[par][:, 0:S0].rearrange("p (a n) -> p a n", a=1), k.resid[:, j, 0:S0], ALU.add)
                    dve.tensor_tensor(outb[:, par, S0:D].rearrange("p (a m c) -> p a c m", a=1, c=3),
                                      prod_ps[par][:, S0:D].rearrange("p (a c m) -> p a c m", a=1, c=3),
                                      k.resid[:, j, S0:D].rearrange("p a (c m) -> p a c m", c=3), ALU.add).then_inc(s_out, 1)

                def step(i, par):
                    if live(i, par, W):
                        scale(i, par)
                    j, q = back(i, par, 1)
                    if live(j, q, W):
                        emit(j, q)

                sweep(dve, W, step, 1)


def build(nc, a):
    with ExitStack() as ctx:
        k = Kernel(nc, ctx, a)
        setup_steps(k)
        with ExitStack() as first:
            k.selfc = k.sb("selfc", [P, WINDOWS, 192], ctx=first)
            node_phase(k, 0)
            edges0(k)
            layer0_update(k)
        node_phase(k, 1)
        edges1(k)
        softmax_weights(k)
        sums1(k)
        output(k)


def kernel(**inputs):
    import numpy as _np
    import concourse.bacc as _bacc
    from concourse import mybir as _mybir
    from concourse.bass_utils import run_bass_kernel_spmd as _run

    nc = _bacc.Bacc("TRN2", target_bir_lowering=False, num_devices=1)
    pad = EP - E
    lay = lambda x: _np.ascontiguousarray(x)
    src = _np.pad(lay(inputs["src"]), (0, pad))
    dst = _np.pad(lay(inputs["dst"]), (0, pad), constant_values=N)
    rows = {n: _np.pad(lay(inputs[n]), ((0, pad), (0, 0))) for n in ("edge_attr_16", "edge_attr_4", "edge_attr_8")}
    turned = lambda x: lay(x.reshape(GROUPS, P, LANES, -1).transpose(0, 3, 2, 1)).reshape(-1, GE)
    arrays = {
        "x": _np.pad(lay(inputs["x"]), ((0, NP - N), (0, 0))),
        "src_g": src.reshape(-1, LANES),
        "dst_g": dst.reshape(-1, LANES),
        "dst_first": lay(dst[::GE]).reshape(1, GROUPS),
        "dst_edge": _np.pad(dst, (1, 1), constant_values=-1),
        "ea4_g": rows["edge_attr_4"].reshape(-1, LANES * 4),
        "ea8_g": turned(rows["edge_attr_8"]),
        "ea16_g": turned(rows["edge_attr_16"]),
    }
    for name in inputs:
        if name.startswith("L"):
            arrays[name] = lay(inputs[name])
    a = {n: nc.dram_tensor("in_" + n, v.shape, _mybir.dt.from_np(v.dtype), kind="ExternalInput").ap() for n, v in arrays.items()}
    a["out"] = nc.dram_tensor("out_0", (N, D), F32, kind="ExternalOutput").ap()
    build(nc, a)
    r = _run(nc, [{"in_" + n: v for n, v in arrays.items()}], core_ids=[0])
    return r.results[0]["out_0"]
```

```python
from contextlib import ExitStack

import numpy as np

import concourse.bass as bass
from concourse import mybir

F32 = mybir.dt.float32
I32 = mybir.dt.int32
ALU = mybir.AluOpType
ACT = mybir.ActivationFunctionType
AX = mybir.AxisListType.X

P = 128
N = 6250
E = 106250
S0, V0 = 64, 32
D = S0 + 3 * V0
NB0, HID, WN0 = 8, 64, 2 * S0 + 2 * V0
NB1, WN1 = 16, 2 * S0 + 3 * V0
HEADS, AS, AV = 4, 16, 8
LANES = 4
GE = P * LANES
GROUPS = -(-E // GE)
EP = GROUPS * GE
WINDOWS = -(-N // P)
NP = WINDOWS * P
STEPS = GROUPS + WINDOWS - 1
CH = EP // P
AGG0 = 448
AGG1 = D + HEADS
QW = 352
BIG = 3.0e38
EPS = 1e-5
AVG_DEG = 16.0
R3 = float(np.sqrt(3.0))
R2 = float(np.sqrt(2.0))


def sweep(eng, n, step, lag=0, first=None, last=0, unroll=2):
    first = first or unroll
    end = n - last - (n - last) % unroll
    for g in range(first):
        step(g - g % unroll, g % unroll)
    with eng.Fori(first, end - unroll + 1, unroll) as i:
        for par in range(unroll):
            step(i, par)
    for g in range(end, n + lag):
        step(g - g % unroll, g % unroll)


def back(i, par, lag, unroll=2):
    q = (par - lag) % unroll
    return i + (par - lag - q), q


def live(i, par, n):
    return not isinstance(i, int) or 0 <= i + par < n


def landed(i, par, slots, n):
    return i * (16 * n // slots) + (par // slots + 1) * 16 * n


def left(i, par, slots, n):
    return i * (16 * n // slots) + par // slots * 16 * n


def uses(i, n):
    return i * (8 * n) + 16 * n


def wait(eng, sem, val):
    if not isinstance(val, int) or val > 0:
        eng.wait_ge(sem, val)


def bc(ap, shape):
    return ap.to_broadcast(shape)


class Kernel:
    def __init__(self, nc, ctx, a):
        self.nc, self.ctx, self.a = nc, ctx, a
        self.psum = ctx.enter_context(nc.psum_tensor("psum", [P, 8 * 512], F32))
        dram = lambda name, shape, dt=F32: nc.dram_tensor(name, shape, dt, kind="Internal").ap()
        self.steps_row = dram("steps_row", [1, STEPS])
        self.table0 = dram("table0", [NP, D])
        self.table_src = dram("table_src", [NP, D])
        self.table_dst = dram("table_dst", [NP, D])
        self.agg0 = dram("agg0", [(WINDOWS + 2) * P, AGG0])
        self.agg1 = dram("agg1", [(WINDOWS + 2) * P, AGG1])
        self.logits = dram("logits", [EP, HEADS])
        self.weights_e = dram("weights_e", [EP, HEADS])
        self.values = dram("values", [EP, D])
        self.s_begin = {nc.sync.engine: self.sem("begin_sp"), nc.gpsimd.engine: self.sem("begin_pool")}
        sb = self.sb
        self.ident = sb("ident", [P, P])
        self.iota = sb("iota", [P, P])
        self.resid = sb("resid", [P, WINDOWS, D])
        self.step_group = sb("step_group", [1, STEPS], I32)
        self.step_row = sb("step_row", [1, STEPS], I32)
        self.step_base = sb("step_base", [P, STEPS])
        self.step_keep = sb("step_keep", [P, STEPS])

    def bank(self, i, n=1):
        return self.psum[:, 512 * i:512 * (i + n)]

    def wait(self, eng, sem, val):
        wait(eng, sem, val)
        if not isinstance(val, int):
            eng.sem_inc(self.s_begin[eng.engine], 1)

    def sb(self, name, shape, dt=F32, ctx=None):
        return (ctx or self.ctx).enter_context(self.nc.sbuf_tensor(name, shape, dt))

    def sem(self, name):
        return self.ctx.enter_context(self.nc.semaphore(name))


class Chain:

    def __init__(self, eng, sem):
        self.eng, self.sem, self.n = eng, sem, 0

    def __call__(self, ins):
        self.n += 1
        ins.then_inc(self.sem, 1)
        self.eng.wait_ge(self.sem, self.n)


def setup_steps(k):
    nc, a = k.nc, k.a
    with ExitStack() as ctx:
        sb = lambda name, shape, dt=F32: k.sb(name, shape, dt, ctx)
        first = sb("first", [P, GROUPS], I32)
        win_i = sb("win_i", [P, GROUPS], I32)
        start = sb("start", [P, GROUPS])
        col = sb("col", [P, GROUPS])
        kp = sb("kp", [P, 2])
        cmp = sb("cmp", [P, 2, GROUPS])
        gk = sb("gk", [P, 2])
        gk_out = sb("gk_out", [P, 2])
        grp = sb("grp", [P, STEPS])
        kk = sb("kk", [P, STEPS])
        win = sb("win", [P, STEPS])
        fin = sb("fin", [P, STEPS])
        pid = sb("pid", [P, 1])
        spare = sb("spare", [P, STEPS])
        s_first, s_iota, s_chain = k.sem("su_first"), k.sem("su_iota"), k.sem("su_chain")
        s_gk, s_row, s_grp = k.sem("su_gk"), k.sem("su_row"), k.sem("su_grp")
        with nc.Block() as block:

            @block.sync
            def _(sp):
                sp.dma_start(first[:, :], a["dst_first"].to_broadcast([P, GROUPS])).then_inc(s_first, 16)
                sp.wait_ge(s_gk, 1)
                for q in range(2):
                    sp.dma_start(k.steps_row[0:1, q * P:(q + 1) * P].rearrange("a p -> p a"),
                                 gk_out[:, q:q + 1]).then_inc(s_row, 16)
                sp.wait_ge(s_row, 32)
                sp.dma_start(grp[:, :], k.steps_row.to_broadcast([P, STEPS])).then_inc(s_grp, 16)

            @block.gpsimd
            def _(pool):
                kw = dict(allow_small_or_imprecise_dtypes=True)
                pool.iota(k.iota[:, :], [[1, P]], 0, 0, **kw).then_inc(s_iota, 1)
                pool.iota(col[:, :], [[1, GROUPS]], 0, 0, **kw).then_inc(s_iota, 1)
                pool.iota(kp[:, :], [[P, 2]], 0, 1, **kw).then_inc(s_iota, 1)
                pool.iota(kk[:, :], [[1, STEPS]], 0, 0, **kw).then_inc(s_iota, 1)
                pool.iota(spare[:, :], [[0, STEPS // 2], [1, 2]], WINDOWS, 0, **kw).then_inc(s_iota, 1)
                pool.iota(pid[:, :], [[1, 1]], 0, 1, **kw).then_inc(s_iota, 1)

            @block.vector
            def _(dve):
                link = Chain(dve, s_chain)
                dve.wait_ge(s_iota, 6)
                link(dve.tensor_scalar(k.ident[:, :], k.iota[:, :], pid[:, 0:1], None, ALU.is_equal))
                dve.wait_ge(s_first, 16)
                link(dve.tensor_scalar(win_i[:, :], first[:, :], 7, None, ALU.arith_shift_right))
                link(dve.tensor_tensor(start[:, :], win_i[:, :], col[:, :], ALU.add))
                link(dve.memset(start[:, 0:1], float(2 * STEPS)))
                for q in range(2):
                    link(dve.tensor_scalar(cmp[:, q, :], start[:, :], kp[:, q:q + 1], None, ALU.is_le))
                link(dve.tensor_reduce(gk[:, :], cmp[:, :, :], AX, ALU.add))
                dve.tensor_copy(gk_out[:, :], gk[:, :]).then_inc(s_gk, 1)
                dve.wait_ge(s_grp, 16)
                link(dve.tensor_copy(k.step_group[0:1, :], grp[0:1, :]))
                link(dve.tensor_tensor(win[:, :], kk[:, :], grp[:, :], ALU.subtract))
                link(dve.tensor_scalar(k.step_base[:, :], win[:, :], float(P), None, ALU.mult))
                link(dve.memset(k.step_keep[:, 0:1], 0.0))
                link(dve.memset(fin[:, STEPS - 1:STEPS], 1.0))
                link(dve.tensor_tensor(k.step_keep[:, 1:STEPS], win[:, 1:STEPS], win[:, 0:STEPS - 1], ALU.is_equal))
                link(dve.tensor_tensor(fin[:, 0:STEPS - 1], win[:, 0:STEPS - 1], win[:, 1:STEPS], ALU.not_equal))
                link(dve.tensor_tensor(win[:, :], win[:, :], spare[:, :], ALU.subtract))
                link(dve.tensor_tensor(win[:, :], win[:, :], fin[:, :], ALU.mult))
                link(dve.tensor_tensor(win[:, :], win[:, :], spare[:, :], ALU.add))
                link(dve.tensor_copy(k.step_row[0:1, :], win[0:1, :]))


def place(sp, sem, tile, row, col, w):
    n, done, r = w.shape[0], 0, 0
    while r < n:
        m = min(n - r, P - (row + r) % P)
        q = (row + r) % P
        c = (row + r) // P
        sp.dma_start(tile[q:q + m, c, col:col + w.shape[1]], w[r:r + m, :]).then_inc(sem, 16)
        done += 16
        r += m
    return done


def node_phase(k, layer):
    nc, a, W = k.nc, k.a, WINDOWS
    L = f"n{layer}_"
    cols = 352 if layer == 0 else 320
    with ExitStack() as ctx:
        sb = lambda name, shape, dt=F32: k.sb(L + name, shape, dt, ctx)
        raw = sb("raw", [P, W, D])
        feat = sb("feat", [P, W, D])
        stat = sb("stat", [P, 4, W])
        wt = sb("wt", [P, 2, cols])
        stage = sb("stage", [P, 2, D])
        turned = sb("turned", [P, 2, 2 * P])
        outb = sb("outb", [P, 2, cols])
        if layer == 1:
            gamma_s, beta_s = sb("gamma_s", [P, S0]), sb("beta_s", [P, S0])
            gamma_v = sb("gamma_v", [P, V0])
        s_load, s_zero, s_chain = k.sem(L + "load"), k.sem(L + "zero"), k.sem(L + "chain")
        s_weights, s_std_in, s_std_out = k.sem(L + "weights"), k.sem(L + "std_in"), k.sem(L + "std_out")
        s_ready, s_stage, s_turn, s_turned = k.sem(L + "ready"), k.sem(L + "stage"), k.sem(L + "turn"), k.sem(L + "turned")
        s_prod, s_out = k.sem(L + "prod"), k.sem(L + "out")
        s_store = [k.sem(L + f"store{q}") for q in range(2)]
        turn_ps = [k.bank(0), k.bank(1)]
        prod_ps = [k.bank(2), k.bank(3)]
        n_weights = 8 * 16
        n_store = 1 if layer == 0 else 2
        with nc.Block() as block:

            @block.sync
            def _(sp):
                if layer == 0:
                    sp.dma_start(raw[:, :, :], a["x"].rearrange("(j p) d -> p j d", p=P)).then_inc(s_load, 16)
                sp.wait_ge(s_zero, 1)
                w_n = 0
                if layer == 0:
                    Ws, Wv, Cs, Cv = a["L0_gnn_W1_s"], a["L0_gnn_W1_v"], a["L0_gnn_Wsc_s"], a["L0_gnn_Wsc_v"]
                    w_n += place(sp, s_weights, wt, 0, 0, Ws)
                    w_n += place(sp, s_weights, wt, 0, D, Cs)
                    for c in range(3):
                        w_n += place(sp, s_weights, wt, S0 + V0 * c, S0 + V0 * c, Wv)
                        w_n += place(sp, s_weights, wt, S0 + V0 * c, D + 96 + V0 * c, Cv)
                else:
                    for q, end in enumerate(("src", "dst")):
                        w_n += place(sp, s_weights, wt, 0, D * q, a[f"L1_gnn_Ws_{end}"])
                        for c in range(3):
                            w_n += place(sp, s_weights, wt, S0 + V0 * c, D * q + S0 + V0 * c, a[f"L1_gnn_Wv_{end}"])
                    for t, name in ((gamma_s, "gamma_s"), (beta_s, "beta_s"), (gamma_v, "gamma_v")):
                        row = a["L1_gnn_" + name].rearrange("(a n) -> a n", a=1)
                        sp.dma_start(t[:, :], row.to_broadcast([P, row.shape[1]])).then_inc(s_load, 16)

                def store(i, par):
                    k.wait(sp, s_out, i + (par + 1))
                    rows = bass.ds((i + par) * P, P)
                    if layer == 0:
                        sp.dma_start(k.table0[rows, :], outb[:, par, 0:D]).then_inc(s_store[par], 16)
                    else:
                        sp.dma_start(k.table_src[rows, :], outb[:, par, 0:D]).then_inc(s_store[par], 16)
                        sp.dma_start(k.table_dst[rows, :], outb[:, par, D:2 * D]).then_inc(s_store[par], 16)

                sweep(sp, W, store)
                sp.wait_ge(s_store[0], 16 * n_store * ((W + 1) // 2))
                sp.wait_ge(s_store[1], 16 * n_store * (W // 2))
                assert w_n == n_weights

            @block.gpsimd
            def _(pool):
                pool.memset(wt[:, :, :], 0.0).then_inc(s_zero, 1)
                pool.wait_ge(s_ready, 1)

                def copy(i, par):
                    k.wait(pool, s_turn, i + (par - 1))
                    pool.tensor_copy(stage[:, par, :], feat[:, i + par, :] if isinstance(i, int) else
                                     feat[:, bass.ds(i + par, 1), :]).then_inc(s_stage, 1)

                sweep(pool, W, copy)

            @block.tensor
            def _(pe):
                def turn(i, par):
                    pe.wait_ge(s_stage, i + (par + 1))
                    wait(pe, s_turned, (i + (par - 1)) * 2)
                    pe.transpose(turn_ps[par][:, 0:P], stage[:, par, 0:P], k.ident[:, :])
                    pe.transpose(turn_ps[par][0:D - P, P:2 * P], stage[:, par, P:D], k.ident[:, :]).then_inc(s_turn, 1)

                def product(i, par):
                    pe.wait_ge(s_turned, (i + (par + 1)) * 2)
                    wait(pe, s_out, i + (par - 1))
                    pe.matmul(prod_ps[par][:, 0:cols], turned[:, par, 0:P], wt[:, 0, :], start=True, stop=False)
                    pe.matmul(prod_ps[par][:, 0:cols], turned[0:D - P, par, P:2 * P], wt[0:D - P, 1, :],
                              start=False, stop=True).then_inc(s_prod, 1)

                def step(i, par):
                    if live(i, par, W):
                        turn(i, par)
                    j, q = back(i, par, 1)
                    if live(j, q, W):
                        product(j, q)

                pe.wait_ge(s_ready, 1)
                sweep(pe, W, step, 1)

            @block.scalar
            def _(act):
                for n in range(1 if layer == 0 else 3):
                    act.wait_ge(s_std_in, n + 1)
                    act.activation(stat[:, 3, :], stat[:, 2, :], ACT.Sqrt).then_inc(s_std_out, 1)

                def evacuate(i, par):
                    act.wait_ge(s_turn, i + (par + 1))
                    wait(act, s_prod, i + (par - 1))
                    act.copy(turned[:, par, 0:P], turn_ps[par][:, 0:P]).then_inc(s_turned, 1)
                    act.copy(turned[0:D - P, par, P:2 * P], turn_ps[par][0:D - P, P:2 * P]).then_inc(s_turned, 1)

                sweep(act, W, evacuate)

            @block.vector
            def _(dve):
                link = Chain(dve, s_chain)
                comp = lambda t, lo=S0: t[:, :, lo:lo + 3 * V0].rearrange("p j (c m) -> p j c m", c=3)
                inter = lambda t: t[:, :, S0:D].rearrange("p j (m c) -> p j c m", c=3)
                mean, rstd = stat[:, 0, :], stat[:, 1, :]
                over = lambda s, n: bc(s.rearrange("p (j a) -> p j a", a=1), [P, W, n])

                def over3(s):
                    return bc(s.rearrange("p (j a b) -> p j a b", a=1, b=1), [P, W, 3, V0])

                def norm_relu(src, src_vec):
                    link(dve.tensor_reduce(mean, src[:, :, :], AX, ALU.add))
                    link(dve.tensor_scalar(mean, mean, 1.0 / D, None, ALU.mult))
                    link(dve.tensor_tensor(feat[:, :, 0:S0], src[:, :, 0:S0], over(mean, S0), ALU.subtract))
                    link(dve.tensor_tensor(comp(feat), src_vec(src), over3(mean), ALU.subtract))

                def scale_of(x, scratch, lo, hi, inv_n, turn):
                    link(dve.tensor_tensor(scratch[:, :, lo:hi], x[:, :, lo:hi], x[:, :, lo:hi], ALU.mult))
                    link(dve.tensor_reduce(rstd, scratch[:, :, lo:hi], AX, ALU.add))
                    dve.tensor_scalar(stat[:, 2, :], rstd, inv_n, EPS, ALU.mult, ALU.add).then_inc(s_std_in, 1)
                    dve.wait_ge(s_std_out, turn)
                    link(dve.reciprocal(rstd, stat[:, 3, :]))

                if layer == 0:
                    dve.wait_ge(s_load, 16)
                    norm_relu(raw, inter)
                    scale_of(feat, k.resid, 0, D, 1.0 / D, 1)
                    link(dve.scalar_tensor_tensor(feat[:, :, :], feat[:, :, :], 0.0, over(rstd, D), ALU.max, ALU.mult))
                    link(dve.tensor_tensor(k.resid[:, :, 0:S0], feat[:, :, 0:S0], raw[:, :, 0:S0], ALU.add))
                    link(dve.tensor_tensor(comp(k.resid), comp(feat), inter(raw), ALU.add))
                else:
                    norm_relu(k.resid, comp)
                    scale_of(feat, raw, 0, D, 1.0 / D, 1)
                    link(dve.scalar_tensor_tensor(feat[:, :, :], feat[:, :, :], 0.0, over(rstd, D), ALU.max, ALU.mult))
                    link(dve.tensor_tensor(k.resid[:, :, :], feat[:, :, :], k.resid[:, :, :], ALU.add))
                    dve.wait_ge(s_load, 48)
                    fs = feat[:, :, 0:S0]
                    along = lambda t, n: bc(t[:, :].rearrange("p (a n) -> p a n", a=1), [P, W, n])
                    link(dve.tensor_reduce(mean, fs, AX, ALU.add))
                    link(dve.tensor_scalar(mean, mean, 1.0 / S0, None, ALU.mult))
                    link(dve.tensor_tensor(fs, fs, over(mean, S0), ALU.subtract))
                    scale_of(feat, raw, 0, S0, 1.0 / S0, 2)
                    link(dve.tensor_tensor(fs, fs, over(rstd, S0), ALU.mult))
                    link(dve.tensor_tensor(fs, fs, along(gamma_s, S0), ALU.mult))
                    link(dve.tensor_tensor(fs, fs, along(beta_s, S0), ALU.add))
                    scale_of(feat, raw, S0, D, 1.0 / V0, 3)
                    fv = feat[:, :, S0:D]
                    link(dve.tensor_tensor(fv, fv, over(rstd, 3 * V0), ALU.mult))
                    for c in range(3):
                        fc = feat[:, :, S0 + V0 * c:S0 + V0 * (c + 1)]
                        link(dve.tensor_tensor(fc, fc, along(gamma_v, V0), ALU.mult))
                dve.wait_ge(s_weights, n_weights)
                if layer == 0:
                    link(dve.tensor_scalar(wt[0:S0, 0, :], wt[0:S0, 0, :], 1.0 / np.sqrt(S0), None, ALU.mult))
                    link(dve.tensor_scalar(wt[S0:P, 0, :], wt[S0:P, 0, :], float(1.0 / np.sqrt(V0)), None, ALU.mult))
                    link(dve.tensor_scalar(wt[0:V0, 1, :], wt[0:V0, 1, :], float(1.0 / np.sqrt(V0)), None, ALU.mult))
                dve.tensor_copy(stat[:, 2, 0:1], stat[:, 3, 0:1]).then_inc(s_ready, 1)

                def emit(i, par):
                    dve.wait_ge(s_prod, i + (par + 1))
                    wait(dve, s_store[par], i * (8 * n_store))
                    if layer == 0:
                        j = (i + par) if isinstance(i, int) else bass.ds(i + par, 1)
                        dve.tensor_copy(k.selfc[:, j, :], prod_ps[par][:, D:cols])
                        dve.tensor_copy(outb[:, par, 0:D], prod_ps[par][:, 0:D]).then_inc(s_out, 1)
                    else:
                        dve.tensor_copy(outb[:, par, :], prod_ps[par][:, 0:cols]).then_inc(s_out, 1)

                sweep(dve, W, emit)


def layer0_update(k):
    nc, a, W = k.nc, k.a, WINDOWS
    with ExitStack() as ctx:
        sb = lambda name, shape, dt=F32: k.sb("u_" + name, shape, dt, ctx)
        wt = sb("wt", [P, 4, 192])
        sums = sb("sums", [P, 2, AGG0])
        turned = sb("turned", [P, 2, 512])
        scol = sb("scol", [P, 4])
        sil = sb("sil", [P, W, 96])
        s_zero, s_weights, s_chain, s_wready = k.sem("u_zero"), k.sem("u_weights"), k.sem("u_chain"), k.sem("u_wready")
        s_sums = [k.sem(f"u_sums{q}") for q in range(2)]
        s_turn, s_turned, s_prod, s_out, s_sil = k.sem("u_turn"), k.sem("u_turned"), k.sem("u_prod"), k.sem("u_out"), k.sem("u_sil")
        turn_ps = [k.bank(0), k.bank(1)]
        prod_ps = [k.bank(2), k.bank(3)]
        W2s, W2v = a["L0_gnn_W2_s"], a["L0_gnn_W2_v"]
        blocks = [(0, 0, W2s[0:S0, :])]
        blocks += [(S0 + V0 * c, 96 + V0 * c, W2v[S0:96, :]) for c in range(3)]
        blocks += [(160 + S0 * c, 96 + V0 * c, W2v[0:S0, :]) for c in range(3)]
        blocks += [(352 + V0 * c, 0, W2s[S0:96, :]) for c in range(3)]
        n_dma = 16 * (len(blocks) + 1)
        with nc.Block() as block:

            @block.gpsimd
            def _(pool):
                pool.memset(wt[:, :, :], 0.0).then_inc(s_zero, 1)

            @block.sync
            def _(sp):
                sp.wait_ge(s_zero, 1)
                n = sum(place(sp, s_weights, wt, r, c, w) for r, c, w in blocks)
                assert n == n_dma

                def load(i, par):
                    k.wait(sp, s_turn, i + (par - 1))
                    sp.dma_start(sums[:, par, :], k.agg0[bass.ds((i + par) * P, P), :]).then_inc(s_sums[par], 16)

                sweep(sp, W, load)

            @block.tensor
            def _(pe):
                def turn(i, par):
                    pe.wait_ge(s_sums[par], uses(i, 1))
                    wait(pe, s_turned, i + (par - 1))
                    for c in range(4):
                        m = min(P, AGG0 - c * P)
                        ins = pe.transpose(turn_ps[par][0:m, c * P:(c + 1) * P], sums[:, par, c * P:c * P + m], k.ident[:, :])
                    ins.then_inc(s_turn, 1)

                def product(i, par):
                    pe.wait_ge(s_turned, i + (par + 1))
                    wait(pe, s_out, i + (par - 1))
                    for c in range(4):
                        m = min(P, AGG0 - c * P)
                        ins = pe.matmul(prod_ps[par][:, 0:192], turned[0:m, par, c * P:(c + 1) * P], wt[0:m, c, :],
                                        start=(c == 0), stop=(c == 3))
                    ins.then_inc(s_prod, 1)

                def step(i, par):
                    if live(i, par, W):
                        turn(i, par)
                    j, q = back(i, par, 1)
                    if live(j, q, W):
                        product(j, q)

                pe.wait_ge(s_wready, 1)
                sweep(pe, W, step, 1)

            @block.scalar
            def _(act):
                def evacuate(i, par):
                    act.wait_ge(s_turn, i + (par + 1))
                    wait(act, s_prod, i + (par - 1))
                    act.copy(turned[:, par, 0:384], turn_ps[par][:, 0:384])
                    act.copy(turned[0:AGG0 - 384, par, 384:512], turn_ps[par][0:AGG0 - 384, 384:512]).then_inc(s_turned, 1)

                sweep(act, W, evacuate)
                act.wait_ge(s_out, W)
                act.activation(sil[:, :, :], k.selfc[:, :, 0:96], ACT.Silu).then_inc(s_sil, 1)

            @block.vector
            def _(dve):
                link = Chain(dve, s_chain)
                base = float(1.0 / (np.sqrt(AVG_DEG) * np.sqrt(96.0)))
                link(dve.memset(scol[:, :], base))
                for row in (352, 384, 416):
                    q, c = row % P, row // P
                    link(dve.memset(scol[q:q + V0, c:c + 1], base / R3))
                dve.wait_ge(s_weights, n_dma)
                for c in range(4):
                    link(dve.tensor_scalar(wt[:, c, :], wt[:, c, :], scol[:, c:c + 1], None, ALU.mult))
                dve.tensor_copy(scol[:, 0:1], scol[:, 1:2]).then_inc(s_wready, 1)

                def add(i, par):
                    dve.wait_ge(s_prod, i + (par + 1))
                    j = bass.ds(i + par, 1)
                    dve.tensor_tensor(k.selfc[:, j, :], k.selfc[:, j, :],
                                      prod_ps[par][:, 0:192].rearrange("p (a n) -> p a n", a=1), ALU.add).then_inc(s_out, 1)

                sweep(dve, W, add)
                dve.wait_ge(s_sil, 1)
                link(dve.tensor_tensor(k.resid[:, :, 0:S0], k.resid[:, :, 0:S0], sil[:, :, 0:S0], ALU.add))
                comp = lambda t, lo: t[:, :, lo:lo + 96].rearrange("p j (c m) -> p j c m", c=3)
                for c in range(3):
                    t = k.selfc[:, :, 96 + V0 * c:96 + V0 * (c + 1)]
                    link(dve.tensor_tensor(t, t, sil[:, :, S0:96], ALU.mult))
                link(dve.tensor_tensor(k.resid[:, :, S0:D], k.resid[:, :, S0:D], k.selfc[:, :, 96:192], ALU.add))


def edges0(k):
    nc, a = k.nc, k.a
    U = 4
    with ExitStack() as ctx:
        sb = lambda name, shape, dt=F32: k.sb("e0_" + name, shape, dt, ctx)
        fc1, b1 = sb("fc1", [NB0, HID]), sb("b1", [HID, 1])
        fc2 = sb("fc2", [HID + 1, WN0])
        idx, dst = sb("idx", [P, U, LANES], I32), sb("dst", [P, U, LANES], I32)
        sh = sb("sh", [P, U, LANES, 6])
        embed = sb("embed", [NB0, U, GE])
        hid = sb("hid", [HID + 1, 2, GE])
        xg = sb("xg", [P, U, LANES, D])
        x0 = sb("x0", [P, 2, LANES, D])
        rel = sb("rel", [P, 2, LANES])
        sel = sb("sel", [P, 2, LANES, P])
        wsv, wvv = sb("wsv", [P, 2, LANES, S0]), sb("wvv", [P, 2, LANES, 96])
        msg = sb("msg", [P, 2, LANES, AGG0])
        acc = sb("acc", [P, 2, AGG0])
        names = ["weights", "ones", "hid", "hidS", "wps", "vec", "agg", "acc", "x0", "far"]
        s_weights, s_ones, s_hid, s_hidS, s_wps, s_vec, s_agg, s_acc, s_x0, s_far = [k.sem("e0_" + n) for n in names]
        s_load = [k.sem(f"e0_load{q}") for q in range(U)]
        s_gather = [k.sem(f"e0_gather{q}") for q in range(U)]
        s_flush = [k.sem(f"e0_flush{q}") for q in range(2)]
        hid_ps = k.bank(0)
        w_ps = [k.bank(q, 2).rearrange("p (l n) -> p l n", l=LANES) for q in (1, 3)]
        agg_ps = [k.bank(5), k.bank(6)]
        NV = 8
        NF = 6
        with nc.Block() as block:

            @block.sync
            def _(sp):
                sp.dma_start(fc1[:, :], a["L0_gnn_fc_w1"]).then_inc(s_weights, 16)
                sp.dma_start(b1[:, :], a["L0_gnn_fc_b1"].rearrange("(n a) -> n a", a=1)).then_inc(s_weights, 16)
                sp.dma_start(fc2[0:HID, :], a["L0_gnn_fc_w2"]).then_inc(s_weights, 16)
                sp.dma_start(fc2[HID:HID + 1, :], a["L0_gnn_fc_b2"].rearrange("(a n) -> a n", a=1)).then_inc(s_weights, 16)

                def load(i, par):
                    g = sp.value_load(k.step_group[0:1, bass.ds(i + par, 1)], min_val=0, max_val=GROUPS - 1)
                    k.wait(sp, s_gather[par], left(i, par, U, 4))
                    k.wait(sp, s_vec, (i + (par - U + 1)) * NV)
                    k.wait(sp, s_far, (i + (par - U + 1)) * NF)
                    k.wait(sp, s_hid, i + (par - U + 1))
                    for t, name in ((idx, "src_g"), (dst, "dst_g"), (sh, "ea6_g")):
                        out = t[:, par, :, :].rearrange("p l c -> p (l c)") if name == "ea6_g" else t[:, par, :]
                        sp.dma_start(out, a[name][bass.ds(g * P, P), :]).then_inc(s_load[par], 16)
                    sp.dma_start(embed[:, par, :], a["ea8_g"][bass.ds(g * NB0, NB0), :]).then_inc(s_load[par], 16)

                def flush(i, par):
                    r = sp.value_load(k.step_row[0:1, bass.ds(i + par, 1)], min_val=0, max_val=WINDOWS + 1)
                    k.wait(sp, s_acc, i + (par + 1))
                    sp.dma_start(k.agg0[bass.ds(r * P, P), :], acc[:, par % 2, :]).then_inc(s_flush[par % 2], 16)

                def step(i, par):
                    if live(i, par, STEPS):
                        load(i, par)
                    j, q = back(i, par, 5, U)
                    if live(j, q, STEPS):
                        flush(j, q)

                sweep(sp, STEPS, step, 5, first=2 * U, unroll=U)
                for q in range(2):
                    sp.wait_ge(s_flush[q], 16 * (STEPS // 2))

            @block.gpsimd
            def _(pool):
                pool.memset(hid[HID:HID + 1, :, :], 1.0).then_inc(s_ones, 1)

                def gather(i, par):
                    k.wait(pool, s_load[par], landed(i, par, U, 4))
                    k.wait(pool, s_vec, (i + (par - U + 1)) * NV)
                    k.wait(pool, s_x0, (i + (par - U + 1)) * LANES)
                    for lane in range(LANES):
                        pool.indirect_dma_start(
                            out=xg[:, par, lane, :], out_offset=None, in_=k.table0[:, :],
                            in_offset=bass.IndirectOffsetOnAxis(ap=idx[:, par, lane:lane + 1], axis=0),
                        ).then_inc(s_gather[par], 16)

                sweep(pool, STEPS, gather, unroll=U)

            @block.tensor
            def _(pe):
                def hidden(i, par):
                    pe.wait_ge(s_load[par], landed(i, par, U, 4))
                    wait(pe, s_hidS, i + par)
                    pe.matmul(hid_ps[0:HID, :], fc1[:, :], embed[:, par, :], start=True, stop=True).then_inc(s_hid, 1)

                def weights(i, par):
                    pe.wait_ge(s_hidS, i + (par + 1))
                    wait(pe, s_vec, (i + (par - 1)) * NV)
                    for lane in range(LANES):
                        ins = pe.matmul(w_ps[par % 2][:, lane, 0:WN0], hid[:, par % 2, lane * P:(lane + 1) * P], fc2[:, :],
                                        start=True, stop=True)
                    ins.then_inc(s_wps, 1)

                def sums(i, par):
                    pe.wait_ge(s_vec, (i + (par + 1)) * NV)
                    pe.wait_ge(s_far, (i + (par + 1)) * NF)
                    wait(pe, s_acc, i + (par - 1))
                    for lane in range(LANES):
                        ins = pe.matmul(agg_ps[par % 2][:, 0:AGG0], sel[:, par % 2, lane, :], msg[:, par % 2, lane, :],
                                        start=(lane == 0), stop=(lane == LANES - 1))
                    ins.then_inc(s_agg, 1)

                def step(i, par):
                    if live(i, par, STEPS):
                        hidden(i, par)
                    j, q = back(i, par, 1, U)
                    if live(j, q, STEPS):
                        weights(j, q)
                    j, q = back(i, par, 3, U)
                    if live(j, q, STEPS):
                        sums(j, q)

                pe.wait_ge(s_weights, 64)
                pe.wait_ge(s_ones, 1)
                sweep(pe, STEPS, step, 3, unroll=U)

            @block.scalar
            def _(act):
                act.wait_ge(s_weights, 64)

                def silu(i, par):
                    act.wait_ge(s_hid, i + (par + 1))
                    wait(act, s_wps, i + (par - 1))
                    act.activation(hid[0:HID, par % 2, :], hid_ps[0:HID, :], ACT.Silu, bias=b1[:, 0:1]).then_inc(s_hidS, 1)

                def times_y0(i, par):
                    act.wait_ge(s_load[par], landed(i, par, U, 4))
                    act.wait_ge(s_gather[par], landed(i, par, U, 4))
                    wait(act, s_vec, (i + (par - 1)) * NV)
                    for lane in range(LANES):
                        act.mul(x0[:, par % 2, lane, :], xg[:, par, lane, :], sh[:, par, lane, 0:1]).then_inc(s_x0, 1)

                def far_lanes(i, par):
                    act.wait_ge(s_vec, (i + par) * NV + 2)
                    wait(act, s_agg, i + (par - 1))
                    for lane in (2, 3):
                        for c in range(3):
                            act.mul(msg[:, par % 2, lane, 160 + S0 * c:160 + S0 * (c + 1)], wsv[:, par % 2, lane, :],
                                    sh[:, par, lane, 1 + c:2 + c]).then_inc(s_far, 1)

                def step(i, par):
                    j, q = back(i, par, 2, U)
                    if live(j, q, STEPS):
                        times_y0(j, q)
                    j, q = back(i, par, 3, U)
                    if live(j, q, STEPS):
                        far_lanes(j, q)
                    if live(i, par, STEPS):
                        silu(i, par)

                sweep(act, STEPS, step, 3, unroll=U)

            @block.vector
            def _(dve):
                def messages(i, par):
                    done = Count(dve, s_vec, i + par, NV)
                    t = par % 2
                    dve.wait_ge(s_load[par], landed(i, par, U, 4))
                    dve.wait_ge(s_gather[par], landed(i, par, U, 4))
                    dve.wait_ge(s_wps, i + (par + 1))
                    wait(dve, s_agg, i + (par - 1))
                    wait(dve, s_far, (i + (par - 1)) * NF)
                    w = w_ps[t]
                    out = msg[:, t]
                    s, v = xg[:, par, :, 0:S0], xg[:, par, :, S0:D].rearrange("p l (c m) -> p l c m", c=3)
                    comp = lambda ap, n=V0: ap.rearrange("p l (c m) -> p l c m", m=n)
                    wv = lambda lo: bc(w[:, :, lo:lo + V0].rearrange("p l (a m) -> p l a m", a=1), [P, LANES, 3, V0])
                    yc = lambda lanes, n: bc(sh[:, par, 0:lanes, 1:4].rearrange("p l (c a) -> p l c a", a=1), [P, lanes, 3, n])
                    done(dve.tensor_scalar(rel[:, t, :], dst[:, par, :], k.step_base[:, bass.ds(i + par, 1)], None, ALU.subtract))
                    done(dve.tensor_tensor(wsv[:, t], w[:, :, S0:2 * S0], s, ALU.mult))
                    done(dve.tensor_tensor(comp(wvv[:, t]), wv(160), v, ALU.mult))
                    done.at(1)
                    done(dve.tensor_tensor(sel[:, t], bc(k.iota[:, :].rearrange("p (a n) -> p a n", a=1), [P, LANES, P]),
                                           bc(rel[:, t, :].rearrange("p (l a) -> p l a", a=1), [P, LANES, P]), ALU.is_equal))
                    done.at(3)
                    done(dve.tensor_tensor(comp(out[:, 0:2, 160:352], S0),
                                           bc(wsv[:, t, 0:2].rearrange("p l (a m) -> p l a m", a=1), [P, 2, 3, S0]), yc(2, S0), ALU.mult))
                    done(dve.tensor_tensor(comp(out[:, :, 352:448]), comp(wvv[:, t]), yc(LANES, V0), ALU.mult))
                    dve.wait_ge(s_x0, (i + (par + 1)) * LANES)
                    done(dve.tensor_tensor(out[:, :, 0:S0], w[:, :, 0:S0], x0[:, t, :, 0:S0], ALU.mult))
                    done(dve.tensor_tensor(comp(out[:, :, S0:160]), wv(128), comp(x0[:, t, :, S0:D]), ALU.mult))
                    assert done.n == NV

                add_sums = accumulate(k, dve, s_agg, s_acc, s_flush, acc, agg_ps, AGG0)

                def step(i, par):
                    if live(i, par, STEPS):
                        messages(i, par)
                    j, q = back(i, par, 2, U)
                    if live(j, q, STEPS):
                        add_sums(j, q)

                sweep(dve, STEPS, step, 2, unroll=U)


def accumulate(k, dve, s_agg, s_acc, s_flush, acc, agg_ps, width):
    def add_sums(i, par):
        t = par % 2
        dve.wait_ge(s_agg, i + (par + 1))
        wait(dve, s_flush[t], left(i, par, 2, 1))
        wait(dve, s_acc, i + par)
        if isinstance(i, int) and i + par == 0:
            dve.tensor_copy(acc[:, t, :], agg_ps[t][:, 0:width]).then_inc(s_acc, 1)
        else:
            dve.scalar_tensor_tensor(acc[:, t, :], acc[:, 1 - t, :], k.step_keep[:, bass.ds(i + par, 1)],
                                     agg_ps[t][:, 0:width], ALU.mult, ALU.add).then_inc(s_acc, 1)
    return add_sums


class Count:

    def __init__(self, eng, sem, item, per):
        self.eng, self.sem, self.item, self.per, self.n = eng, sem, item, per, 0

    def __call__(self, ins):
        self.n += 1
        assert self.n <= self.per
        ins.then_inc(self.sem, 1)

    def at(self, n):
        self.eng.wait_ge(self.sem, self.item * self.per + n)

    def last(self):
        self.at(self.n)


def edges1(k):
    nc, a = k.nc, k.a
    U, SLOTS = 8, 4
    with ExitStack() as ctx:
        sb = lambda name, shape, dt=F32: k.sb("e1_" + name, shape, dt, ctx)
        w_rbf = sb("w_rbf", [NB1, WN1])
        ws_val, ws_val_t, wg = sb("ws_val", [96, S0]), sb("ws_val_t", [S0, 96]), sb("wg", [S0, V0])
        adot = sb("adot", [P, HEADS * AS])
        w1a, w1b, w1c = sb("w1a", [96, 164]), sb("w1b", [P, P]), sb("w1c", [P, P])
        w2a, w2b, w2c = sb("w2a", [96, D]), sb("w2b", [P, 192]), sb("w2c", [P, 192])
        c2a, c2b, c2c = sb("c2a", [96, 1]), sb("c2b", [P, 1]), sb("c2c", [P, 1])
        idx_s, idx_d = sb("idx_s", [P, U, LANES], I32), sb("idx_d", [P, U, LANES], I32)
        y = sb("y", [P, U, LANES, 6])
        rbf = sb("rbf", [NB1, U, GE])
        msg = sb("msg", [P, SLOTS, LANES, D])
        msg0 = sb("msg0", [P, 2, LANES, D])
        y_late = sb("y_late", [P, 2, LANES, 3])
        vy = [sb(f"vy{q}", [P, LANES, 3, V0]) for q in range(2)]
        cross_a, cross_b = [sb(f"cross_a{q}", [P, LANES, 96]) for q in range(2)], [sb(f"cross_b{q}", [P, LANES, 96]) for q in range(2)]
        dot2, dot = [sb(f"dot2{q}", [P, LANES, V0]) for q in range(2)], sb("dot", [P, LANES, V0])
        q1, q2 = sb("q1", [P, 2, LANES, QW]), sb("q2", [P, 2, LANES, QW])
        t1, t2 = sb("t1", [P, 3, GE]), sb("t2", [P, 3, GE])
        gate = sb("gate", [P, 2, LANES, V0])
        absa, lin = sb("absa", [P, 2, LANES, HEADS * AS]), sb("lin", [P, 2, LANES, HEADS])
        w_lin = sb("w_lin", [96, HEADS * AS])
        headsum = sb("headsum", [P, LANES, HEADS])
        weighed = sb("weighed", [P, LANES, HEADS * AS])
        val = sb("val", [P, 2, LANES, 96])
        sxy, sxy_late = sb("sxy", [P, LANES, 3, V0]), sb("sxy_late", [P, LANES, 3, V0])
        outv = sb("outv", [P, SLOTS, LANES, 192])
        outl = sb("outl", [P, SLOTS, LANES, HEADS])
        names = ["zero", "weights", "chain", "pre", "wg", "ready", "w", "tp1", "mid", "post", "turn1", "turned1", "turn2",
                 "turned2", "val", "sig", "sy0", "prod2", "copied", "msg0", "vy0", "vec"]
        (s_zero, s_weights, s_chain, s_pre, s_wg, s_ready, s_w, s_tp1, s_mid, s_post, s_turn1, s_turned1, s_turn2,
         s_turned2, s_val, s_sig, s_sy0, s_prod2, s_copied, s_msg0, s_vy0, s_vec) = [k.sem("e1_" + n) for n in names]
        s_load = [k.sem(f"e1_load{q}") for q in range(U)]
        s_src = [k.sem(f"e1_src{q}") for q in range(SLOTS)]
        s_dst = [k.sem(f"e1_dst{q}") for q in range(SLOTS)]
        s_store = [k.sem(f"e1_store{q}") for q in range(SLOTS)]
        w_ps = k.bank(0, 2).rearrange("p (l n) -> p l n", l=LANES)
        turn_ps = [k.bank(2), k.bank(3)]
        val_ps = k.bank(4).rearrange("p (l n) -> p l n", l=LANES)
        vec_ps = k.bank(5).rearrange("p (l n) -> p l n", l=LANES)
        out_ps = k.bank(6, 2).rearrange("p (l n) -> p l n", l=LANES)
        ALPHA = 192
        K1, KM, KP = 13, 15, 4
        READ, GATED = 4, 6
        CHUNKS = ((0, 96), (96, P), (224, P))
        Wsv, Wvv, Wvs, Wvl = a["L1_gnn_Ws_val"], a["L1_gnn_Wv_val"], a["L1_gnn_Ws_vlin"], a["L1_gnn_Wv_vlin"]
        col = lambda name: a["L1_gnn_" + name].rearrange("(n a) -> n a", a=1)

        def head_cols(ap, lo, n):
            return ap[:, 0:D].rearrange("p (h n) -> p h n", h=HEADS)[:, :, lo:lo + n]

        def weight_loads():
            by_head = lambda w, n: w.rearrange("p (h n) -> p h n", h=HEADS)
            yield w_rbf[:, :], a["L1_gnn_W_rbf"]
            yield ws_val[:, :], Wsv
            yield wg[:, :], a["L1_gnn_Wg"]
            yield adot[:, :], a["L1_gnn_alpha_dot"].rearrange("a h s -> a (h s)").to_broadcast([P, HEADS * AS])
            yield w1a[:, 0:S0], Wsv
            yield w1a[:, 100:164], a["L1_gnn_W_alpha"]
            yield w1b[0:S0, 96:P], Wvv[0:S0, :]
            yield w1b[64:96, 0:32], Wvv[S0:96, :]
            yield w1b[96:P, 32:64], Wvv[S0:96, :]
            yield w1c[0:32, 64:96], Wvv[S0:96, :]
            for c in range(3):
                yield w1c[32 + 32 * c:64 + 32 * c, 32 * c:32 * c + 32], Wvv[96:P, :]
            yield head_cols(w2a[:, :], 0, AS), by_head(Wvs, AS)
            yield w2b[0:S0, D:192], Wvl[0:S0, :]
            for c in range(2):
                yield head_cols(w2b[64 + 32 * c:96 + 32 * c, :], AS + AV * c, AV), by_head(Wvl[S0:96, :], AV)
            yield head_cols(w2c[0:32, :], AS + 2 * AV, AV), by_head(Wvl[S0:96, :], AV)
            for c in range(3):
                yield head_cols(w2c[32 + 32 * c:64 + 32 * c, :], AS + AV * c, AV), by_head(Wvl[96:P, :], AV)
            yield c2a[0:S0, :], col("w2_ss")
            yield c2a[S0:96, :], col("w2_vv0")
            yield c2b[0:S0, :], col("w2_sv")
            yield c2b[64:96, :], col("w2_vs")
            yield c2b[96:P, :], col("w2_vs")
            yield c2c[0:32, :], col("w2_vs")
            for c in range(3):
                yield c2c[32 + 32 * c:64 + 32 * c, :], col("w2_vv1")

        n_weights = 16 * 30
        with nc.Block() as block:

            @block.sync
            def _(sp):
                sp.wait_ge(s_zero, 5)
                n = 0
                for t, w in weight_loads():
                    sp.dma_start(t, w).then_inc(s_weights, 16)
                    n += 16
                assert n == n_weights, n

                def load(i, par):
                    g = i + par
                    k.wait(sp, s_dst[par % SLOTS], left(i, par - SLOTS, SLOTS, 4))
                    k.wait(sp, s_w, g - U + 1)
                    k.wait(sp, s_mid, (g - U + 1) * KM)
                    k.wait(sp, s_vy0, (g - U + 1) * LANES)
                    k.wait(sp, s_sy0, (g - U + 1) * LANES)
                    sp.dma_start(idx_s[:, par, :], a["src_g"][bass.ds(g * P, P), :]).then_inc(s_load[par], 16)
                    sp.dma_start(idx_d[:, par, :], a["dst_g"][bass.ds(g * P, P), :]).then_inc(s_load[par], 16)
                    sp.dma_start(y[:, par, :, :].rearrange("p l c -> p (l c)"),
                                 a["ea6_g"][bass.ds(g * P, P), :]).then_inc(s_load[par], 16)
                    sp.dma_start(rbf[:, par, :], a["ea16_g"][bass.ds(g * NB1, NB1), :]).then_inc(s_load[par], 16)

                def store(i, par):
                    g = i + par
                    slot = par % SLOTS
                    k.wait(sp, s_post, (g + 1) * KP)
                    sp.dma_start(k.values.rearrange("(q l) d -> q l d", l=LANES)[bass.ds(g * P, P), :, :],
                                 outv[:, slot, :, 0:D]).then_inc(s_store[slot], 16)
                    sp.dma_start(k.logits.rearrange("(q l) h -> q (l h)", l=LANES)[bass.ds(g * P, P), :],
                                 outl[:, slot, :, :].rearrange("p l h -> p (l h)")).then_inc(s_store[slot], 16)

                def step(i, par):
                    if live(i, par, GROUPS):
                        load(i, par)
                    j, q = back(i, par, 4, U)
                    if live(j, q, GROUPS):
                        store(j, q)

                sweep(sp, GROUPS, step, 4, unroll=U)
                for q in range(SLOTS):
                    sp.wait_ge(s_store[q], 32 * (GROUPS // SLOTS))

            @block.gpsimd
            def _(pool):
                for t in (w1b, w1c, w2a, w2b, w2c):
                    pool.memset(t[:, :], 0.0).then_inc(s_zero, 1)

                def sources(i, par):
                    k.wait(pool, s_load[par], landed(i, par, U, 4))
                    slot = par % SLOTS
                    k.wait(pool, s_tp1, (i + (par - SLOTS + 1)) * K1)
                    k.wait(pool, s_msg0, (i + (par - SLOTS + 1)) * LANES)
                    for lane in range(LANES):
                        pool.indirect_dma_start(
                            out=msg[:, slot, lane, :], out_offset=None, in_=k.table_src[:, :],
                            in_offset=bass.IndirectOffsetOnAxis(ap=idx_s[:, par, lane:lane + 1], axis=0),
                        ).then_inc(s_src[slot], 16)

                def destinations(i, par):
                    slot = par % SLOTS
                    k.wait(pool, s_src[slot], landed(i, par, SLOTS, 4))
                    for lane in range(LANES):
                        pool.indirect_dma_start(
                            out=msg[:, slot, lane, :], out_offset=None, in_=k.table_dst[:, :],
                            in_offset=bass.IndirectOffsetOnAxis(ap=idx_d[:, par, lane:lane + 1], axis=0),
                            compute_op=ALU.add,
                        ).then_inc(s_dst[slot], 16)

                def step(i, par):
                    if live(i, par, GROUPS):
                        sources(i, par)
                    j, q = back(i, par, 1, U)
                    if live(j, q, GROUPS):
                        destinations(j, q)

                sweep(pool, GROUPS, step, 1, unroll=U)

            @block.tensor
            def _(pe):
                pe.wait_ge(s_weights, n_weights)
                pe.transpose(turn_ps[0][0:S0, 0:96], ws_val[:, :], k.ident[0:96, 0:96]).then_inc(s_pre, 1)
                pe.wait_ge(s_wg, 1)
                pe.matmul(val_ps[0:96, 0, 0:V0], ws_val_t[:, :], wg[:, :], start=True, stop=True).then_inc(s_pre, 1)
                pe.wait_ge(s_ready, 1)

                def radial(i, par):
                    pe.wait_ge(s_load[par], landed(i, par, U, 4))
                    wait(pe, s_tp1, (i + par) * K1)
                    for lane in range(LANES):
                        ins = pe.matmul(w_ps[:, lane, 0:WN1], rbf[:, par, lane * P:(lane + 1) * P], w_rbf[:, :],
                                        start=True, stop=True)
                    ins.then_inc(s_w, 1)

                def turn(src, chunk, bank, sem):
                    lo, m = CHUNKS[chunk]
                    for lane in range(LANES):
                        ins = pe.transpose(turn_ps[bank][0:m, lane * P:(lane + 1) * P], src[:, lane, lo:lo + m],
                                           k.ident[:, :])
                    ins.then_inc(sem, 1)

                def turn_first(i, par, chunk):
                    g = i + par
                    pe.wait_ge(s_tp1, (g + 1) * K1)
                    if chunk < 2:
                        wait(pe, s_turned2, (g - 2) * 3 + chunk + 2)
                    else:
                        pe.wait_ge(s_turned1, g * 3 + 1)
                    turn(q1[:, par % 2], chunk, chunk % 2, s_turn1)

                def turn_second(i, par, chunk):
                    g = i + par
                    pe.wait_ge(s_mid, (g + 1) * KM)
                    pe.wait_ge(s_vy0, (g + 1) * LANES)
                    pe.wait_ge(s_sy0, (g + 1) * LANES)
                    if chunk < 2:
                        last = isinstance(g, int) and g == GROUPS - 1
                        pe.wait_ge(s_turned1, GROUPS * 3 if last else (g + 1) * 3 + chunk + 2)
                        if last:
                            pe.wait_ge(s_turned2, (GROUPS - 1) * 3)
                    else:
                        pe.wait_ge(s_turned2, g * 3 + 1)
                    turn(q2[:, par % 2], chunk, (chunk + 1) % 2, s_turn2)

                def values(i, par):
                    g = i + par
                    pe.wait_ge(s_turned1, g * 3 + 1)
                    wait(pe, s_sig, g * 4)
                    wait(pe, s_copied, g - 1)
                    for lane in range(LANES):
                        e = slice(lane * P, (lane + 1) * P)
                        pe.matmul(val_ps[:, lane, 0:100], t1[0:96, 0, e], w1a[:, 0:100], start=True, stop=True)
                        ins = pe.matmul(out_ps[:, lane, ALPHA:ALPHA + 64], t1[0:96, 0, e], w1a[:, 100:164],
                                        start=True, stop=True)
                    ins.then_inc(s_val, 1)

                def vectors(i, par):
                    g = i + par
                    pe.wait_ge(s_turned1, (g + 1) * 3)
                    wait(pe, s_mid, (g - 1) * KM + READ)
                    for lane in range(LANES):
                        e = slice(lane * P, (lane + 1) * P)
                        pe.matmul(vec_ps[:, lane, :], t1[:, 1, e], w1b[:, :], start=True, stop=False)
                        ins = pe.matmul(vec_ps[:, lane, :], t1[:, 2, e], w1c[:, :], start=False, stop=True)
                    ins.then_inc(s_vec, 1)

                def outputs(i, par):
                    g = i + par
                    pe.wait_ge(s_turned2, (g + 1) * 3)
                    wait(pe, s_copied, g)
                    for lane in range(LANES):
                        e = slice(lane * P, (lane + 1) * P)
                        pe.matmul(out_ps[:, lane, 0:192], t2[:, 1, e], w2b[:, :], start=True, stop=False)
                        pe.matmul(out_ps[:, lane, 0:D], t2[0:96, 0, e], w2a[:, :], start=False, stop=False,
                                  skip_group_check=True)
                        ins = pe.matmul(out_ps[:, lane, 0:192], t2[:, 2, e], w2c[:, :], start=False, stop=True)
                    ins.then_inc(s_prod2, 1)

                def step(i, par):
                    this, (j, q), (n, r) = live(i, par, GROUPS), back(i, par, 1, U), back(i, par, -1, U)
                    if this:
                        turn_first(i, par, 0)
                        turn_first(i, par, 1)
                    if not isinstance(n, int) or n + r < GROUPS:
                        radial(n, r)
                    if this:
                        turn_first(i, par, 2)
                        values(i, par)
                    if live(j, q, GROUPS):
                        turn_second(j, q, 0)
                        turn_second(j, q, 1)
                    if this:
                        vectors(i, par)
                    if live(j, q, GROUPS):
                        turn_second(j, q, 2)
                        outputs(j, q)

                radial(0, 0)
                sweep(pe, GROUPS, step, 1, last=U, unroll=U)

            @block.scalar
            def _(act):
                act.wait_ge(s_pre, 1)
                act.copy(ws_val_t[:, :], turn_ps[0][0:S0, 0:96]).then_inc(s_wg, 1)

                def evacuate(i, par, dst, bank, turn_sem, turned_sem):
                    g = i + par
                    for c, (lo, m) in enumerate(CHUNKS):
                        act.wait_ge(turn_sem, g * 3 + (c + 1))
                        if c == 0:
                            wait(act, s_vec if dst is t1 else s_prod2, g)
                        act.copy(dst[0:m, c, :], turn_ps[(bank + c) % 2][0:m, :]).then_inc(turned_sem, 1)

                def gates(i, par):
                    g, t = i + par, par % 2
                    act.wait_ge(s_val, g + 1)
                    wait(act, s_turn2, (g - 1) * 3)
                    wait(act, s_mid, (g - 1) * KM)
                    act.activation(q2[:, t, :, 96:160], val_ps[:, :, 0:S0], ACT.Sigmoid).then_inc(s_sig, 1)
                    act.activation(gate[:, t], val_ps[:, :, S0:96], ACT.Sigmoid).then_inc(s_sig, 1)
                    act.activation(absa[:, t], out_ps[:, :, ALPHA:ALPHA + 64], ACT.Abs).then_inc(s_sig, 1)
                    act.copy(lin[:, t], val_ps[:, :, 96:100]).then_inc(s_sig, 1)
                    act.wait_ge(s_sig, (g + 1) * 4)
                    for lane in range(LANES):
                        act.mul(q2[:, t, lane, 0:S0], q2[:, t, lane, 96:160], y[:, par, lane, 0:1]).then_inc(s_sy0, 1)

                def vectors_y0(i, par):
                    g, t = i + par, par % 2
                    act.wait_ge(s_mid, g * KM + GATED)
                    for lane in range(LANES):
                        act.mul(q2[:, t, lane, 160:256], val[:, t, lane, :], y[:, par, lane, 0:1]).then_inc(s_vy0, 1)

                def messages_y0(i, par):
                    act.wait_ge(s_load[par], landed(i, par, U, 4))
                    act.wait_ge(s_dst[par % SLOTS], landed(i, par, SLOTS, 4))
                    wait(act, s_tp1, (i + (par - 1)) * K1)
                    for lane in range(LANES):
                        act.mul(msg0[:, par % 2, lane, :], msg[:, par % SLOTS, lane, :], y[:, par, lane, 0:1]).then_inc(s_msg0, 1)

                def copy_out(i, par):
                    act.wait_ge(s_prod2, i + (par + 1))
                    wait(act, s_store[par % SLOTS], left(i, par, SLOTS, 2))
                    act.copy(outv[:, par % SLOTS, :, :], out_ps[:, :, 0:192]).then_inc(s_copied, 1)

                def step(i, par):
                    this, (j, q), (o, r) = live(i, par, GROUPS), back(i, par, 1, U), back(i, par, 2, U)
                    if live(o, r, GROUPS):
                        copy_out(o, r)
                    if this:
                        evacuate(i, par, t1, 0, s_turn1, s_turned1)
                    if live(j, q, GROUPS):
                        vectors_y0(j, q)
                    if this:
                        gates(i, par)
                    if live(j, q, GROUPS):
                        evacuate(j, q, t2, 1, s_turn2, s_turned2)
                    n, r = back(i, par, -1, U)
                    if not isinstance(n, int) or n + r < GROUPS:
                        messages_y0(n, r)

                messages_y0(0, 0)
                sweep(act, GROUPS, step, 2, last=U, unroll=U)

            @block.vector
            def _(dve):
                link = Chain(dve, s_chain)
                dve.wait_ge(s_weights, n_weights)
                dve.wait_ge(s_pre, 2)
                link(dve.tensor_copy(w1a[:, S0:96], val_ps[0:96, 0, 0:V0]))
                link(dve.tensor_tensor(w_lin[:, :], w1a[:, 100:164], adot[0:96, :], ALU.mult))
                link(dve.tensor_scalar(w_lin[:, :], w_lin[:, :], 0.6, None, ALU.mult))
                link(dve.tensor_reduce(w1a[:, 96:100], w_lin[:, :].rearrange("p (h s) -> p h s", h=HEADS), AX, ALU.add))
                link(dve.tensor_scalar(adot[:, :], adot[:, :], 0.4, None, ALU.mult))
                link(dve.tensor_scalar(w1a[S0:96, :], w1a[S0:96, :], 1.0 / R3, None, ALU.mult))
                for c in range(3):
                    r = slice(32 + 32 * c, 64 + 32 * c)
                    link(dve.tensor_scalar(w1c[r, :], w1c[r, :], 1.0 / R2, None, ALU.mult))
                    link(dve.tensor_scalar(c2c[r, :], c2c[r, :], 1.0 / R2, None, ALU.mult))
                link(dve.tensor_scalar(c2a[S0:96, :], c2a[S0:96, :], 1.0 / R3, None, ALU.mult))
                for w, c in ((w2a, c2a), (w2b, c2b), (w2c, c2c)):
                    link(dve.tensor_scalar(w[:, :], w[:, :], c[:, 0:1], None, ALU.mult))
                dve.memset(dot[:, 0, 0:1], 0.0).then_inc(s_ready, 1)

                comp = lambda ap: ap.rearrange("p l (c m) -> p l c m", c=3)
                one = lambda ap: ap.rearrange("p l (a m) -> p l a m", a=1)
                two = lambda ap: ap.rearrange("p l (c m) -> p l c m", c=2)
                three = lambda ap: bc(one(ap), [P, LANES, 3, V0])
                ys = lambda t, lo, n: bc(t[:, :, lo:lo + n].rearrange("p l (c a) -> p l c a", a=1), [P, LANES, n, V0])

                def products(done, v, y, h):
                    a, b = cross_a[h], cross_b[h]
                    done(dve.tensor_tensor(two(a[:, :, 0:64]), two(v[:, :, 32:96]), ys(y, 3, 2), ALU.mult))
                    done(dve.tensor_tensor(one(a[:, :, 64:96]), one(v[:, :, 0:32]), ys(y, 5, 1), ALU.mult))
                    done(dve.tensor_tensor(one(b[:, :, 0:32]), one(v[:, :, 64:96]), ys(y, 2, 1), ALU.mult))
                    done(dve.tensor_tensor(two(b[:, :, 32:96]), two(v[:, :, 0:64]), ys(y, 3, 2), ALU.mult))
                    done(dve.tensor_tensor(vy[h][:, :, :, :], comp(v), ys(y, 1, 3), ALU.mult))

                def first(i, par):
                    g, t = i + par, par % 2
                    done = Count(dve, s_tp1, g, K1)
                    m, yy, q, w = msg[:, par % SLOTS], y[:, par], q1[:, t], w_ps
                    dve.wait_ge(s_load[par], landed(i, par, U, 4))
                    dve.wait_ge(s_dst[par % SLOTS], landed(i, par, SLOTS, 4))
                    wait(dve, s_tp1, g * K1)
                    products(done, m[:, :, S0:D], yy, 0)
                    done.at(4)
                    done(dve.tensor_tensor(cross_a[0][:, :, :], cross_a[0][:, :, :], cross_b[0][:, :, :], ALU.subtract))
                    wait(dve, s_turn1, (g - 1) * 3)
                    dve.wait_ge(s_w, g + 1)
                    done.at(5)
                    done(dve.tensor_tensor(dot2[0][:, :, :], vy[0][:, :, 0, :], vy[0][:, :, 1, :], ALU.add))
                    done(dve.tensor_tensor(q[:, :, 96:160], w[:, :, S0:2 * S0], m[:, :, 0:S0], ALU.mult))
                    done.at(7)
                    done(dve.tensor_tensor(dot[:, :, :], dot2[0][:, :, :], vy[0][:, :, 2, :], ALU.add))
                    done(dve.tensor_tensor(comp(q[:, :, 256:352]), three(w[:, :, 192:224]), comp(cross_a[0][:, :, :]), ALU.mult))
                    dve.wait_ge(s_msg0, (g + 1) * LANES)
                    done(dve.tensor_tensor(q[:, :, 0:S0], w[:, :, 0:S0], msg0[:, t, :, 0:S0], ALU.mult))
                    done.at(9)
                    done(dve.tensor_tensor(q[:, :, S0:96], w[:, :, 160:192], dot[:, :, :], ALU.mult))
                    done(dve.tensor_tensor(comp(q[:, :, 160:256]), three(w[:, :, 128:160]), comp(msg0[:, t, :, S0:D]), ALU.mult))
                    assert done.n == K1, done.n

                def middle(i, par):
                    g, t = i + par, par % 2
                    done = Count(dve, s_mid, g, KM)
                    yy, q, v = y[:, par], q2[:, t], val[:, t]
                    dve.wait_ge(s_sig, (g + 1) * 4)
                    dve.wait_ge(s_vec, g + 1)
                    wait(dve, s_mid, g * KM)
                    wait(dve, s_vy0, (g - 1) * LANES)
                    done(dve.tensor_tensor(sxy[:, :, :, :], three(vec_ps[:, :, 96:P]), ys(yy, 1, 3), ALU.mult))
                    done(dve.tensor_tensor(weighed[:, :, :], absa[:, t],
                                           bc(adot[:, :].rearrange("p (a n) -> p a n", a=1), [P, LANES, HEADS * AS]), ALU.mult))
                    done(dve.tensor_copy(y_late[:, t], yy[:, :, 1:4]))
                    done.at(1)
                    done(dve.tensor_tensor(comp(v), sxy[:, :, :, :], comp(vec_ps[:, :, 0:96]), ALU.add))
                    assert done.n == READ
                    done.at(2)
                    done(dve.tensor_reduce(headsum[:, :, :], weighed[:, :, :].rearrange("p l (h s) -> p l h s", h=HEADS),
                                           AX, ALU.add))
                    done.at(4)
                    done(dve.tensor_tensor(comp(v), comp(v), three(gate[:, t]), ALU.mult))
                    assert done.n == GATED
                    wait(dve, s_store[par % SLOTS], left(i, par, SLOTS, 2))
                    done.at(5)
                    done(dve.tensor_tensor(outl[:, par % SLOTS, :, :], headsum[:, :, :], lin[:, t], ALU.add))
                    done.at(6)
                    products(done, v, yy, 1)
                    done.at(11)
                    done(dve.tensor_tensor(q[:, :, 256:352], cross_a[1][:, :, :], cross_b[1][:, :, :], ALU.subtract))
                    done.at(12)
                    done(dve.tensor_tensor(dot2[1][:, :, :], vy[1][:, :, 0, :], vy[1][:, :, 1, :], ALU.add))
                    done.at(14)
                    done(dve.tensor_tensor(q[:, :, S0:96], dot2[1][:, :, :], vy[1][:, :, 2, :], ALU.add))
                    assert done.n == KM, done.n

                def post(i, par):
                    g, t = i + par, par % 2
                    done = Count(dve, s_post, g, KP)
                    dve.wait_ge(s_copied, g + 1)
                    wait(dve, s_post, g * KP)
                    dve.wait_ge(s_mid, (g + 1) * KM)
                    done(dve.tensor_tensor(sxy_late[:, :, :, :], three(outv[:, par % SLOTS, :, D:192]), ys(y_late[:, t], 0, 3), ALU.mult))
                    done.at(1)
                    for c in range(3):
                        lo = AS + AV * c
                        o = outv[:, par % SLOTS, :, 0:D].rearrange("p l (h n) -> p l h n", h=HEADS)[:, :, :, lo:lo + AV]
                        done(dve.tensor_tensor(o, o, sxy_late[:, :, c, :].rearrange("p l (h n) -> p l h n", h=HEADS), ALU.add))

                def step(i, par):
                    if live(i, par, GROUPS):
                        first(i, par)
                    j, q = back(i, par, 1, U)
                    if live(j, q, GROUPS):
                        middle(j, q)
                    j, q = back(i, par, 2, U)
                    if live(j, q, GROUPS):
                        post(j, q)

                sweep(dve, GROUPS, step, 2, unroll=U)


def softmax_weights(k):
    nc, a = k.nc, k.a
    with ExitStack() as ctx:
        sb = lambda name, shape, dt=F32: k.sb("sm_" + name, shape, dt, ctx)
        lg, run, top = sb("lg", [P, CH, HEADS]), sb("run", [P, CH, HEADS]), sb("top", [P, CH, HEADS])
        cur, near = sb("cur", [P, CH], I32), sb("near", [P, 2, CH], I32)
        pen = sb("pen", [P, 2, CH])
        ends = sb("ends", [P, 2 * HEADS])
        rows = sb("rows", [HEADS, 2 * P])
        inc = sb("inc", [HEADS, P])
        hand = sb("hand", [HEADS, P])
        start = sb("start", [P, HEADS])
        s_load, s_chain, s_pe, s_ends = k.sem("sm_load"), k.sem("sm_chain"), k.sem("sm_pe"), k.sem("sm_ends")
        s_exp, s_max, s_out = k.sem("sm_exp"), k.sem("sm_max"), k.sem("sm_out")
        flat = lambda t: t.rearrange("(p n) h -> p (n h)", p=P)
        edge = a["dst_edge"]
        with nc.Block() as block:

            @block.sync
            def _(sp):
                sp.dma_start(lg[:, :, :].rearrange("p n h -> p (n h)"), flat(k.logits)).then_inc(s_load, 16)
                for t, off in ((cur[:, :], 1), (near[:, 0, :], 0), (near[:, 1, :], 2)):
                    sp.dma_start(t, edge[off:off + EP].rearrange("(p n) -> p n", p=P)).then_inc(s_load, 16)
                sp.wait_ge(s_exp, 1)
                sp.dma_start(flat(k.weights_e), lg[:, :, :].rearrange("p n h -> p (n h)")).then_inc(s_out, 16)
                sp.wait_ge(s_out, 16)

            @block.tensor
            def _(pe):
                for d in range(2):
                    pe.wait_ge(s_ends, 2 * d + 1)
                    pe.transpose(k.bank(0)[0:HEADS, 0:P], ends[:, 0:HEADS], k.ident[:, :])
                    pe.transpose(k.bank(0)[0:HEADS, P:2 * P], ends[:, HEADS:2 * HEADS], k.ident[:, :]).then_inc(s_pe, 1)
                    pe.wait_ge(s_ends, 2 * d + 2)
                    pe.transpose(k.bank(1)[:, 0:HEADS], hand[:, :], k.ident[0:HEADS, 0:HEADS]).then_inc(s_pe, 1)

            @block.scalar
            def _(act):
                act.wait_ge(s_max, 1)
                act.activation(lg[:, :, :], lg[:, :, :], ACT.Exp).then_inc(s_exp, 1)

            @block.vector
            def _(dve):
                link = Chain(dve, s_chain)
                dve.wait_ge(s_load, 64)
                for d in range(2):
                    link(dve.tensor_tensor(pen[:, d, :], cur[:, :], near[:, d, :], ALU.is_equal))
                    link(dve.tensor_scalar(pen[:, d, :], pen[:, d, :], 1.0, BIG, ALU.subtract, ALU.mult))
                for d, (src, out) in enumerate(((lg, run), (run, top))):
                    way = (lambda t: t[:, ::-1]) if d else (lambda t: t)
                    end = 0 if d else CH - 1
                    for h in range(HEADS):
                        link(dve.tensor_tensor_scan(way(out[:, :, h]), way(pen[:, d, :]), way(src[:, :, h]), -BIG,
                                                    ALU.add, ALU.max))
                    link(dve.tensor_copy(ends[:, 0:HEADS], out[:, end, :]))
                    link(dve.tensor_reduce(ends[:, HEADS:HEADS + 1], pen[:, d, :], AX, ALU.min))
                    dve.tensor_copy(ends[:, HEADS + 1:2 * HEADS],
                                    bc(ends[:, HEADS:HEADS + 1], [P, HEADS - 1])).then_inc(s_ends, 1)
                    dve.wait_ge(s_pe, 2 * d + 1)
                    link(dve.tensor_copy(rows[:, :], k.bank(0)[0:HEADS, 0:2 * P]))
                    link(dve.tensor_tensor_scan(way(inc[:, :]), way(rows[:, P:2 * P]), way(rows[:, 0:P]), -BIG, ALU.add, ALU.max))
                    link(dve.memset(hand[:, :], -BIG))
                    if d:
                        dve.tensor_copy(hand[:, 0:P - 1], inc[:, 1:P]).then_inc(s_ends, 1)
                    else:
                        dve.tensor_copy(hand[:, 1:P], inc[:, 0:P - 1]).then_inc(s_ends, 1)
                    dve.wait_ge(s_pe, 2 * d + 2)
                    link(dve.tensor_copy(start[:, :], k.bank(1)[:, 0:HEADS]))
                    for h in range(HEADS):
                        link(dve.tensor_tensor_scan(way(out[:, :, h]), way(pen[:, d, :]), way(src[:, :, h]),
                                                    start[:, h:h + 1], ALU.add, ALU.max))
                dve.tensor_tensor(lg[:, :, :], lg[:, :, :], top[:, :, :], ALU.subtract).then_inc(s_max, 1)


def sums1(k):
    nc, a = k.nc, k.a
    with ExitStack() as ctx:
        sb = lambda name, shape, dt=F32: k.sb("s1_" + name, shape, dt, ctx)
        dst = sb("dst", [P, 2, LANES], I32)
        ex = sb("ex", [P, 2, LANES, HEADS])
        value = sb("value", [P, 2, LANES, D])
        rel = sb("rel", [P, 2, LANES])
        sel = sb("sel", [P, 2, LANES, P])
        rhs = sb("rhs", [P, 2, LANES, AGG1])
        acc = sb("acc", [P, 2, AGG1])
        s_vec, s_agg, s_acc = k.sem("s1_vec"), k.sem("s1_agg"), k.sem("s1_acc")
        s_load = [k.sem(f"s1_load{q}") for q in range(2)]
        s_flush = [k.sem(f"s1_flush{q}") for q in range(2)]
        agg_ps = [k.bank(5), k.bank(6)]
        NV = 7
        with nc.Block() as block:

            @block.sync
            def _(sp):
                def load(i, par):
                    g = sp.value_load(k.step_group[0:1, bass.ds(i + par, 1)], min_val=0, max_val=GROUPS - 1)
                    k.wait(sp, s_vec, (i + (par - 1)) * NV)
                    sp.dma_start(dst[:, par, :], a["dst_g"][bass.ds(g * P, P), :]).then_inc(s_load[par], 16)
                    sp.dma_start(ex[:, par, :, :].rearrange("p l h -> p (l h)"),
                                 k.weights_e.rearrange("(q l) h -> q (l h)", l=LANES)[bass.ds(g * P, P), :]).then_inc(s_load[par], 16)
                    sp.dma_start(value[:, par, :, :].rearrange("p l d -> p (l d)"),
                                 k.values.rearrange("(q l) d -> q (l d)", l=LANES)[bass.ds(g * P, P), :]).then_inc(s_load[par], 16)

                def flush(i, par):
                    r = sp.value_load(k.step_row[0:1, bass.ds(i + par, 1)], min_val=0, max_val=WINDOWS + 1)
                    k.wait(sp, s_acc, i + (par + 1))
                    sp.dma_start(k.agg1[bass.ds(r * P, P), :], acc[:, par, :]).then_inc(s_flush[par], 16)

                def step(i, par):
                    if live(i, par, STEPS):
                        load(i, par)
                    j, q = back(i, par, 2)
                    if live(j, q, STEPS):
                        flush(j, q)

                sweep(sp, STEPS, step, 2)
                for q in range(2):
                    sp.wait_ge(s_flush[q], 16 * (STEPS // 2))

            @block.tensor
            def _(pe):
                def sums(i, par):
                    pe.wait_ge(s_vec, (i + (par + 1)) * NV)
                    wait(pe, s_acc, i + (par - 1))
                    for lane in range(LANES):
                        ins = pe.matmul(agg_ps[par][:, 0:AGG1], sel[:, par, lane, :], rhs[:, par, lane, :],
                                        start=(lane == 0), stop=(lane == LANES - 1))
                    ins.then_inc(s_agg, 1)

                sweep(pe, STEPS, sums)

            @block.vector
            def _(dve):
                def weigh(i, par):
                    done = Count(dve, s_vec, i + par, NV)
                    dve.wait_ge(s_load[par], uses(i, 3))
                    wait(dve, s_agg, i + (par - 1))
                    done(dve.tensor_scalar(rel[:, par, :], dst[:, par, :], k.step_base[:, bass.ds(i + par, 1)], None, ALU.subtract))
                    done.last()
                    for lane in range(LANES):
                        done(dve.tensor_scalar(sel[:, par, lane, :], k.iota[:, :], rel[:, par, lane:lane + 1], None, ALU.is_equal))
                    by_head = lambda t: t.rearrange("p l (h n) -> p l h n", h=HEADS)
                    done(dve.tensor_tensor(by_head(rhs[:, par, :, 0:D]), by_head(value[:, par, :, :]),
                                           bc(ex[:, par, :, :].rearrange("p l (h a) -> p l h a", a=1), [P, LANES, HEADS, D // HEADS]), ALU.mult))
                    done(dve.tensor_copy(rhs[:, par, :, D:AGG1], ex[:, par, :, :]))

                add_sums = accumulate(k, dve, s_agg, s_acc, s_flush, acc, agg_ps, AGG1)

                def step(i, par):
                    if live(i, par, STEPS):
                        weigh(i, par)
                    j, q = back(i, par, 1)
                    if live(j, q, STEPS):
                        add_sums(j, q)

                sweep(dve, STEPS, step, 1)


def output(k):
    nc, a, W = k.nc, k.a, WINDOWS
    with ExitStack() as ctx:
        sb = lambda name, shape, dt=F32: k.sb("o_" + name, shape, dt, ctx)
        sums = sb("sums", [P, W, AGG1])
        rden = sb("rden", [P, W, HEADS])
        wt = sb("wt", [P, 2, D])
        stage = sb("stage", [P, 2, D])
        turned = sb("turned", [P, 2, 2 * P])
        outb = sb("outb", [P, 2, D])
        s_zero, s_weights, s_sums, s_chain = k.sem("o_zero"), k.sem("o_weights"), k.sem("o_sums"), k.sem("o_chain")
        s_stage, s_turn, s_turned, s_prod, s_out = [k.sem("o_" + n) for n in ("stage", "turn", "turned", "prod", "out")]
        s_store = [k.sem(f"o_store{q}") for q in range(2)]
        turn_ps, prod_ps = [k.bank(0), k.bank(1)], [k.bank(2), k.bank(3)]
        n_dma = 17 * 16
        with nc.Block() as block:

            @block.gpsimd
            def _(pool):
                pool.memset(wt[:, :, :], 0.0).then_inc(s_zero, 1)

            @block.sync
            def _(sp):
                sp.dma_start(sums[:, :, :], k.agg1[0:NP, :].rearrange("(j p) d -> p j d", p=P)).then_inc(s_sums, 16)
                sp.wait_ge(s_zero, 1)
                n = 0
                for h in range(HEADS):
                    r = 40 * h
                    n += place(sp, s_weights, wt, r, 0, a["L1_gnn_Wps"][AS * h:AS * (h + 1), :])
                    for c in range(3):
                        n += place(sp, s_weights, wt, r + AS + AV * c, S0 + V0 * c, a["L1_gnn_Wpv"][AV * h:AV * (h + 1), :])
                assert n == n_dma, n

                def store(i, par):
                    g = i + par
                    k.wait(sp, s_out, g + 1)
                    m = N - g * P if isinstance(g, int) and g == W - 1 else P
                    sp.dma_start(a["out"][bass.ds(g * P, m), :], outb[0:m, par, :]).then_inc(s_store[par], 16)

                sweep(sp, W, store)
                sp.wait_ge(s_store[0], 16 * ((W + 1) // 2))
                sp.wait_ge(s_store[1], 16 * (W // 2))

            @block.tensor
            def _(pe):
                def turn(i, par):
                    pe.wait_ge(s_stage, i + (par + 1))
                    wait(pe, s_turned, (i + (par - 1)) * 2)
                    pe.transpose(turn_ps[par][:, 0:P], stage[:, par, 0:P], k.ident[:, :])
                    pe.transpose(turn_ps[par][0:D - P, P:2 * P], stage[:, par, P:D], k.ident[:, :]).then_inc(s_turn, 1)

                def product(i, par):
                    pe.wait_ge(s_turned, (i + (par + 1)) * 2)
                    wait(pe, s_out, i + (par - 1))
                    pe.matmul(prod_ps[par][:, 0:D], turned[:, par, 0:P], wt[:, 0, :], start=True, stop=False)
                    pe.matmul(prod_ps[par][:, 0:D], turned[0:D - P, par, P:2 * P], wt[0:D - P, 1, :],
                              start=False, stop=True).then_inc(s_prod, 1)

                def step(i, par):
                    if live(i, par, W):
                        turn(i, par)
                    j, q = back(i, par, 1)
                    if live(j, q, W):
                        product(j, q)

                pe.wait_ge(s_weights, n_dma)
                sweep(pe, W, step, 1)

            @block.scalar
            def _(act):
                def evacuate(i, par):
                    act.wait_ge(s_turn, i + (par + 1))
                    wait(act, s_prod, i + (par - 1))
                    act.copy(turned[:, par, 0:P], turn_ps[par][:, 0:P]).then_inc(s_turned, 1)
                    act.copy(turned[0:D - P, par, P:2 * P], turn_ps[par][0:D - P, P:2 * P]).then_inc(s_turned, 1)

                sweep(act, W, evacuate)

            @block.vector
            def _(dve):
                link = Chain(dve, s_chain)
                dve.wait_ge(s_sums, 16)
                link(dve.tensor_scalar(rden[:, :, :], sums[:, :, D:AGG1], 1e-16, None, ALU.add))
                link(dve.reciprocal(rden[:, :, :], rden[:, :, :]))
                def scale(i, par):
                    wait(dve, s_turn, i + (par - 1))
                    j = bass.ds(i + par, 1)
                    dve.tensor_tensor(stage[:, par, :].rearrange("p (a h n) -> p a h n", a=1, h=HEADS),
                                      sums[:, j, 0:D].rearrange("p a (h n) -> p a h n", h=HEADS),
                                      bc(rden[:, j, :].rearrange("p a (h b) -> p a h b", b=1), [P, 1, HEADS, D // HEADS]),
                                      ALU.mult).then_inc(s_stage, 1)

                def emit(i, par):
                    dve.wait_ge(s_prod, i + (par + 1))
                    wait(dve, s_store[par], i * 8)
                    j = bass.ds(i + par, 1)
                    dve.tensor_tensor(outb[:, par, 0:S0].rearrange("p (a n) -> p a n", a=1),
                                      prod_ps[par][:, 0:S0].rearrange("p (a n) -> p a n", a=1), k.resid[:, j, 0:S0], ALU.add)
                    dve.tensor_tensor(outb[:, par, S0:D].rearrange("p (a m c) -> p a c m", a=1, c=3),
                                      prod_ps[par][:, S0:D].rearrange("p (a c m) -> p a c m", a=1, c=3),
                                      k.resid[:, j, S0:D].rearrange("p a (c m) -> p a c m", c=3), ALU.add).then_inc(s_out, 1)

                def step(i, par):
                    if live(i, par, W):
                        scale(i, par)
                    j, q = back(i, par, 1)
                    if live(j, q, W):
                        emit(j, q)

                sweep(dve, W, step, 1)


def build(nc, a):
    with ExitStack() as ctx:
        k = Kernel(nc, ctx, a)
        setup_steps(k)
        with ExitStack() as first:
            k.selfc = k.sb("selfc", [P, WINDOWS, 192], ctx=first)
            node_phase(k, 0)
            edges0(k)
            layer0_update(k)
        node_phase(k, 1)
        edges1(k)
        softmax_weights(k)
        sums1(k)
        output(k)


def kernel(**inputs):
    import numpy as _np
    import concourse.bacc as _bacc
    from concourse import mybir as _mybir
    from concourse.bass_utils import run_bass_kernel_spmd as _run

    nc = _bacc.Bacc("TRN2", target_bir_lowering=False, num_devices=1)
    pad = EP - E
    lay = lambda x: _np.ascontiguousarray(x)
    src = _np.pad(lay(inputs["src"]), (0, pad))
    dst = _np.pad(lay(inputs["dst"]), (0, pad), constant_values=N)
    rows = {n: _np.pad(lay(inputs[n]), ((0, pad), (0, 0))) for n in ("edge_attr_16", "edge_attr_4", "edge_attr_8")}
    turned = lambda x: lay(x.reshape(GROUPS, P, LANES, -1).transpose(0, 3, 2, 1)).reshape(-1, GE)
    arrays = {
        "x": _np.pad(lay(inputs["x"]), ((0, NP - N), (0, 0))),
        "src_g": src.reshape(-1, LANES),
        "dst_g": dst.reshape(-1, LANES),
        "dst_first": lay(dst[::GE]).reshape(1, GROUPS),
        "dst_edge": _np.pad(dst, (1, 1), constant_values=-1),
        "ea6_g": lay(rows["edge_attr_4"][:, [0, 1, 2, 3, 1, 2]]).reshape(-1, LANES * 6),
        "ea8_g": turned(rows["edge_attr_8"]),
        "ea16_g": turned(rows["edge_attr_16"]),
    }
    for name in inputs:
        if name.startswith("L"):
            arrays[name] = lay(inputs[name])
    a = {n: nc.dram_tensor("in_" + n, v.shape, _mybir.dt.from_np(v.dtype), kind="ExternalInput").ap() for n, v in arrays.items()}
    a["out"] = nc.dram_tensor("out_0", (N, D), F32, kind="ExternalOutput").ap()
    build(nc, a)
    r = _run(nc, [{"in_" + n: v for n, v in arrays.items()}], core_ids=[0])
    return r.results[0]["out_0"]
```

```python
from contextlib import ExitStack

import numpy as np

import concourse.bass as bass
from concourse import mybir

F32 = mybir.dt.float32
I32 = mybir.dt.int32
ALU = mybir.AluOpType
ACT = mybir.ActivationFunctionType
AX = mybir.AxisListType.X

P = 128
N = 6250
E = 106250
S0, V0 = 64, 32
D = S0 + 3 * V0
NB0, HID, WN0 = 8, 64, 2 * S0 + 2 * V0
NB1, WN1 = 16, 2 * S0 + 3 * V0
HEADS, AS, AV = 4, 16, 8
LANES = 4
GE = P * LANES
GROUPS = -(-E // GE)
EP = GROUPS * GE
WINDOWS = -(-N // P)
NP = WINDOWS * P
STEPS = GROUPS + WINDOWS - 1
SPARE = 4
CH = EP // P
AGG0 = 384
AGG1 = D + HEADS
QW = 352
BIG = 3.0e38
EPS = 1e-5
AVG_DEG = 16.0
R3 = float(np.sqrt(3.0))
R2 = float(np.sqrt(2.0))


def sweep(eng, n, step, lag=0, first=None, last=0, unroll=2):
    first = first or unroll
    end = n - last - (n - last) % unroll
    for g in range(first):
        step(g - g % unroll, g % unroll)
    with eng.Fori(first, end - unroll + 1, unroll) as i:
        for par in range(unroll):
            step(i, par)
    for g in range(end, n + lag):
        step(g - g % unroll, g % unroll)


def back(i, par, lag, unroll=2):
    q = (par - lag) % unroll
    return i + (par - lag - q), q


def live(i, par, n):
    return not isinstance(i, int) or 0 <= i + par < n


def landed(i, par, slots, n):
    return i * (16 * n // slots) + (par // slots + 1) * 16 * n


def left(i, par, slots, n):
    return i * (16 * n // slots) + par // slots * 16 * n


def wait(eng, sem, val):
    if not isinstance(val, int) or val > 0:
        eng.wait_ge(sem, val)


def bc(ap, shape):
    return ap.to_broadcast(shape)


class Kernel:
    def __init__(self, nc, ctx, a):
        self.nc, self.ctx, self.a = nc, ctx, a
        self.psum = ctx.enter_context(nc.psum_tensor("psum", [P, 8 * 512], F32))
        dram = lambda name, shape, dt=F32: nc.dram_tensor(name, shape, dt, kind="Internal").ap()
        self.steps_row = dram("steps_row", [1, STEPS])
        self.table0 = dram("table0", [NP, D])
        self.table_src = dram("table_src", [NP, D])
        self.table_dst = dram("table_dst", [NP, D])
        self.agg0 = dram("agg0", [(WINDOWS + SPARE) * P, AGG0])
        self.agg1 = dram("agg1", [(WINDOWS + SPARE) * P, AGG1])
        self.logits = dram("logits", [EP, HEADS])
        self.weights_e = dram("weights_e", [EP, HEADS])
        self.values = dram("values", [EP, D])
        self.s_begin = {nc.sync.engine: self.sem("begin_sp"), nc.gpsimd.engine: self.sem("begin_pool")}
        sb = self.sb
        self.ident = sb("ident", [P, P])
        self.iota = sb("iota", [P, P])
        self.resid = sb("resid", [P, WINDOWS, D])
        self.step_group = sb("step_group", [1, STEPS], I32)
        self.step_row = sb("step_row", [1, STEPS], I32)
        self.step_base = sb("step_base", [P, STEPS])
        self.step_keep = sb("step_keep", [P, STEPS])

    def bank(self, i, n=1):
        return self.psum[:, 512 * i:512 * (i + n)]

    def wait(self, eng, sem, val):
        wait(eng, sem, val)
        if not isinstance(val, int):
            eng.sem_inc(self.s_begin[eng.engine], 1)

    def sb(self, name, shape, dt=F32, ctx=None):
        return (ctx or self.ctx).enter_context(self.nc.sbuf_tensor(name, shape, dt))

    def sem(self, name):
        return self.ctx.enter_context(self.nc.semaphore(name))


class Chain:

    def __init__(self, eng, sem):
        self.eng, self.sem, self.n = eng, sem, 0

    def __call__(self, ins):
        self.n += 1
        ins.then_inc(self.sem, 1)
        self.eng.wait_ge(self.sem, self.n)


def setup_steps(k):
    nc, a = k.nc, k.a
    with ExitStack() as ctx:
        sb = lambda name, shape, dt=F32: k.sb(name, shape, dt, ctx)
        first = sb("first", [P, GROUPS], I32)
        win_i = sb("win_i", [P, GROUPS], I32)
        start = sb("start", [P, GROUPS])
        col = sb("col", [P, GROUPS])
        kp = sb("kp", [P, 2])
        cmp = sb("cmp", [P, 2, GROUPS])
        gk = sb("gk", [P, 2])
        gk_out = sb("gk_out", [P, 2])
        grp = sb("grp", [P, STEPS])
        kk = sb("kk", [P, STEPS])
        win = sb("win", [P, STEPS])
        fin = sb("fin", [P, STEPS])
        pid = sb("pid", [P, 1])
        spare = sb("spare", [P, STEPS])
        s_first, s_iota, s_chain = k.sem("su_first"), k.sem("su_iota"), k.sem("su_chain")
        s_gk, s_row, s_grp = k.sem("su_gk"), k.sem("su_row"), k.sem("su_grp")
        with nc.Block() as block:

            @block.sync
            def _(sp):
                sp.dma_start(first[:, :], a["dst_first"].to_broadcast([P, GROUPS])).then_inc(s_first, 16)
                sp.wait_ge(s_gk, 1)
                for q in range(2):
                    sp.dma_start(k.steps_row[0:1, q * P:(q + 1) * P].rearrange("a p -> p a"),
                                 gk_out[:, q:q + 1]).then_inc(s_row, 16)
                sp.wait_ge(s_row, 32)
                sp.dma_start(grp[:, :], k.steps_row.to_broadcast([P, STEPS])).then_inc(s_grp, 16)

            @block.gpsimd
            def _(pool):
                kw = dict(allow_small_or_imprecise_dtypes=True)
                pool.iota(k.iota[:, :], [[1, P]], 0, 0, **kw).then_inc(s_iota, 1)
                pool.iota(col[:, :], [[1, GROUPS]], 0, 0, **kw).then_inc(s_iota, 1)
                pool.iota(kp[:, :], [[P, 2]], 0, 1, **kw).then_inc(s_iota, 1)
                pool.iota(kk[:, :], [[1, STEPS]], 0, 0, **kw).then_inc(s_iota, 1)
                pool.iota(spare[:, :], [[0, STEPS // SPARE], [1, SPARE]], WINDOWS, 0, **kw).then_inc(s_iota, 1)
                pool.iota(pid[:, :], [[1, 1]], 0, 1, **kw).then_inc(s_iota, 1)

            @block.vector
            def _(dve):
                link = Chain(dve, s_chain)
                dve.wait_ge(s_iota, 6)
                link(dve.tensor_scalar(k.ident[:, :], k.iota[:, :], pid[:, 0:1], None, ALU.is_equal))
                dve.wait_ge(s_first, 16)
                link(dve.tensor_scalar(win_i[:, :], first[:, :], 7, None, ALU.arith_shift_right))
                link(dve.tensor_tensor(start[:, :], win_i[:, :], col[:, :], ALU.add))
                link(dve.memset(start[:, 0:1], float(2 * STEPS)))
                for q in range(2):
                    link(dve.tensor_scalar(cmp[:, q, :], start[:, :], kp[:, q:q + 1], None, ALU.is_le))
                link(dve.tensor_reduce(gk[:, :], cmp[:, :, :], AX, ALU.add))
                dve.tensor_copy(gk_out[:, :], gk[:, :]).then_inc(s_gk, 1)
                dve.wait_ge(s_grp, 16)
                link(dve.tensor_copy(k.step_group[0:1, :], grp[0:1, :]))
                link(dve.tensor_tensor(win[:, :], kk[:, :], grp[:, :], ALU.subtract))
                link(dve.tensor_scalar(k.step_base[:, :], win[:, :], float(P), None, ALU.mult))
                link(dve.memset(k.step_keep[:, 0:1], 0.0))
                link(dve.memset(fin[:, STEPS - 1:STEPS], 1.0))
                link(dve.tensor_tensor(k.step_keep[:, 1:STEPS], win[:, 1:STEPS], win[:, 0:STEPS - 1], ALU.is_equal))
                link(dve.tensor_tensor(fin[:, 0:STEPS - 1], win[:, 0:STEPS - 1], win[:, 1:STEPS], ALU.not_equal))
                link(dve.tensor_tensor(win[:, :], win[:, :], spare[:, :], ALU.subtract))
                link(dve.tensor_tensor(win[:, :], win[:, :], fin[:, :], ALU.mult))
                link(dve.tensor_tensor(win[:, :], win[:, :], spare[:, :], ALU.add))
                link(dve.tensor_copy(k.step_row[0:1, :], win[0:1, :]))


def place(sp, sem, tile, row, col, w):
    n, done, r = w.shape[0], 0, 0
    while r < n:
        m = min(n - r, P - (row + r) % P)
        q = (row + r) % P
        c = (row + r) // P
        sp.dma_start(tile[q:q + m, c, col:col + w.shape[1]], w[r:r + m, :]).then_inc(sem, 16)
        done += 16
        r += m
    return done


def node_phase(k, layer):
    nc, a, W = k.nc, k.a, WINDOWS
    L = f"n{layer}_"
    cols = 352 if layer == 0 else 320
    with ExitStack() as ctx:
        sb = lambda name, shape, dt=F32: k.sb(L + name, shape, dt, ctx)
        raw = sb("raw", [P, W, D])
        feat = sb("feat", [P, W, D])
        stat = sb("stat", [P, 4, W])
        wt = sb("wt", [P, 2, 512])
        stage = sb("stage", [P, 4, D])
        turned = sb("turned", [P, 2, 2 * P])
        outb = sb("outb", [P, 4, cols])
        if layer == 1:
            gamma_s, beta_s = sb("gamma_s", [P, S0]), sb("beta_s", [P, S0])
            gamma_v = sb("gamma_v", [P, V0])
        s_load, s_zero, s_chain = k.sem(L + "load"), k.sem(L + "zero"), k.sem(L + "chain")
        s_weights, s_std_in, s_std_out = k.sem(L + "weights"), k.sem(L + "std_in"), k.sem(L + "std_out")
        s_ready, s_stage, s_turn, s_turned = k.sem(L + "ready"), k.sem(L + "stage"), k.sem(L + "turn"), k.sem(L + "turned")
        s_prod, s_out = k.sem(L + "prod"), k.sem(L + "out")
        s_store = [k.sem(L + f"store{q}") for q in range(4)]
        turn_ps = [k.bank(0), k.bank(1)]
        prod_ps = [k.bank(2), k.bank(3)]
        n_weights = 8 * 16
        n_store = 1 if layer == 0 else 2
        with nc.Block() as block:

            @block.sync
            def _(sp):
                if layer == 0:
                    sp.dma_start(raw[:, :, :], a["x"].rearrange("(j p) d -> p j d", p=P)).then_inc(s_load, 16)
                sp.wait_ge(s_zero, 1)
                w_n = 0
                if layer == 0:
                    Ws, Wv, Cs, Cv = a["L0_gnn_W1_s"], a["L0_gnn_W1_v"], a["L0_gnn_Wsc_s"], a["L0_gnn_Wsc_v"]
                    w_n += place(sp, s_weights, wt, 0, 0, Ws)
                    w_n += place(sp, s_weights, wt, 0, D, Cs)
                    for c in range(3):
                        w_n += place(sp, s_weights, wt, S0 + V0 * c, S0 + V0 * c, Wv)
                        w_n += place(sp, s_weights, wt, S0 + V0 * c, D + 96 + V0 * c, Cv)
                else:
                    for q, end in enumerate(("src", "dst")):
                        w_n += place(sp, s_weights, wt, 0, D * q, a[f"L1_gnn_Ws_{end}"])
                        for c in range(3):
                            w_n += place(sp, s_weights, wt, S0 + V0 * c, D * q + S0 + V0 * c, a[f"L1_gnn_Wv_{end}"])
                    for t, name in ((gamma_s, "gamma_s"), (beta_s, "beta_s"), (gamma_v, "gamma_v")):
                        row = a["L1_gnn_" + name].rearrange("(a n) -> a n", a=1)
                        sp.dma_start(t[:, :], row.to_broadcast([P, row.shape[1]])).then_inc(s_load, 16)

                def store(i, par):
                    k.wait(sp, s_out, i + (par + 1))
                    rows = bass.ds((i + par) * P, P)
                    if layer == 0:
                        sp.dma_start(k.table0[rows, :], outb[:, par, 0:D]).then_inc(s_store[par], 16)
                    else:
                        sp.dma_start(k.table_src[rows, :], outb[:, par, 0:D]).then_inc(s_store[par], 16)
                        sp.dma_start(k.table_dst[rows, :], outb[:, par, D:2 * D]).then_inc(s_store[par], 16)

                sweep(sp, W, store, unroll=4)
                for q in range(4):
                    sp.wait_ge(s_store[q], 16 * n_store * ((W - q + 3) // 4))
                assert w_n == n_weights

            @block.gpsimd
            def _(pool):
                pool.memset(wt[:, :, :], 0.0).then_inc(s_zero, 1)
                pool.wait_ge(s_ready, 1)

                def copy(i, par):
                    k.wait(pool, s_turn, i + (par - 3))
                    pool.tensor_copy(stage[:, par, :], feat[:, i + par, :] if isinstance(i, int) else
                                     feat[:, bass.ds(i + par, 1), :]).then_inc(s_stage, 1)

                sweep(pool, W, copy, unroll=4)

            @block.tensor
            def _(pe):
                def turn(i, par):
                    pe.wait_ge(s_stage, i + (par + 1))
                    wait(pe, s_turned, (i + (par - 1)) * 2)
                    t = par % 2
                    pe.transpose(turn_ps[t][:, 0:P], stage[:, par, 0:P], k.ident[:, :])
                    pe.transpose(turn_ps[t][0:D - P, P:2 * P], stage[:, par, P:D], k.ident[:, :]).then_inc(s_turn, 1)

                def product(i, par):
                    pe.wait_ge(s_turned, (i + (par + 1)) * 2)
                    wait(pe, s_out, i + (par - 1))
                    t = par % 2
                    own = lambda ap: ap[:, P:P + 2 * (cols - D)].rearrange("p (q n) -> p q n", q=2)[:, :, 0:V0]
                    pe.matmul(prod_ps[t][:, 0:cols], turned[:, t, 0:P], wt[:, 0, 0:cols], start=True, stop=True)
                    pe.matmul(own(prod_ps[t]), turned[0:D - P, t, P:2 * P], own(wt[0:D - P, 1, :]),
                              start=False, stop=True, skip_group_check=True).then_inc(s_prod, 1)

                def step(i, par):
                    if live(i, par, W):
                        turn(i, par)
                    j, q = back(i, par, 1, 4)
                    if live(j, q, W):
                        product(j, q)

                pe.wait_ge(s_ready, 1)
                sweep(pe, W, step, 1, unroll=4)

            @block.scalar
            def _(act):
                for n in range(1 if layer == 0 else 3):
                    act.wait_ge(s_std_in, n + 1)
                    act.activation(stat[:, 3, :], stat[:, 2, :], ACT.Sqrt).then_inc(s_std_out, 1)

                def evacuate(i, par):
                    act.wait_ge(s_turn, i + (par + 1))
                    wait(act, s_prod, i + (par - 1))
                    t = par % 2
                    act.copy(turned[:, t, 0:P], turn_ps[t][:, 0:P]).then_inc(s_turned, 1)
                    act.copy(turned[0:D - P, t, P:2 * P], turn_ps[t][0:D - P, P:2 * P]).then_inc(s_turned, 1)

                sweep(act, W, evacuate, unroll=4)

            @block.vector
            def _(dve):
                link = Chain(dve, s_chain)
                comp = lambda t, lo=S0: t[:, :, lo:lo + 3 * V0].rearrange("p j (c m) -> p j c m", c=3)
                inter = lambda t: t[:, :, S0:D].rearrange("p j (m c) -> p j c m", c=3)
                mean, rstd = stat[:, 0, :], stat[:, 1, :]
                over = lambda s, n: bc(s.rearrange("p (j a) -> p j a", a=1), [P, W, n])

                def over3(s):
                    return bc(s.rearrange("p (j a b) -> p j a b", a=1, b=1), [P, W, 3, V0])

                def norm_relu(src, src_vec):
                    link(dve.tensor_reduce(mean, src[:, :, :], AX, ALU.add))
                    link(dve.tensor_scalar(mean, mean, 1.0 / D, None, ALU.mult))
                    link(dve.tensor_tensor(feat[:, :, 0:S0], src[:, :, 0:S0], over(mean, S0), ALU.subtract))
                    link(dve.tensor_tensor(comp(feat), src_vec(src), over3(mean), ALU.subtract))

                def scale_of(x, scratch, lo, hi, inv_n, turn):
                    link(dve.tensor_tensor(scratch[:, :, lo:hi], x[:, :, lo:hi], x[:, :, lo:hi], ALU.mult))
                    link(dve.tensor_reduce(rstd, scratch[:, :, lo:hi], AX, ALU.add))
                    dve.tensor_scalar(stat[:, 2, :], rstd, inv_n, EPS, ALU.mult, ALU.add).then_inc(s_std_in, 1)
                    dve.wait_ge(s_std_out, turn)
                    link(dve.reciprocal(rstd, stat[:, 3, :]))

                if layer == 0:
                    dve.wait_ge(s_load, 16)
                    norm_relu(raw, inter)
                    scale_of(feat, k.resid, 0, D, 1.0 / D, 1)
                    link(dve.scalar_tensor_tensor(feat[:, :, :], feat[:, :, :], 0.0, over(rstd, D), ALU.max, ALU.mult))
                    link(dve.tensor_tensor(k.resid[:, :, 0:S0], feat[:, :, 0:S0], raw[:, :, 0:S0], ALU.add))
                    link(dve.tensor_tensor(comp(k.resid), comp(feat), inter(raw), ALU.add))
                else:
                    norm_relu(k.resid, comp)
                    scale_of(feat, raw, 0, D, 1.0 / D, 1)
                    link(dve.scalar_tensor_tensor(feat[:, :, :], feat[:, :, :], 0.0, over(rstd, D), ALU.max, ALU.mult))
                    link(dve.tensor_tensor(k.resid[:, :, :], feat[:, :, :], k.resid[:, :, :], ALU.add))
                    dve.wait_ge(s_load, 48)
                    fs = feat[:, :, 0:S0]
                    along = lambda t, n: bc(t[:, :].rearrange("p (a n) -> p a n", a=1), [P, W, n])
                    link(dve.tensor_reduce(mean, fs, AX, ALU.add))
                    link(dve.tensor_scalar(mean, mean, 1.0 / S0, None, ALU.mult))
                    link(dve.tensor_tensor(fs, fs, over(mean, S0), ALU.subtract))
                    scale_of(feat, raw, 0, S0, 1.0 / S0, 2)
                    link(dve.tensor_tensor(fs, fs, over(rstd, S0), ALU.mult))
                    link(dve.tensor_tensor(fs, fs, along(gamma_s, S0), ALU.mult))
                    link(dve.tensor_tensor(fs, fs, along(beta_s, S0), ALU.add))
                    scale_of(feat, raw, S0, D, 1.0 / V0, 3)
                    fv = feat[:, :, S0:D]
                    link(dve.tensor_tensor(fv, fv, over(rstd, 3 * V0), ALU.mult))
                    for c in range(3):
                        fc = feat[:, :, S0 + V0 * c:S0 + V0 * (c + 1)]
                        link(dve.tensor_tensor(fc, fc, along(gamma_v, V0), ALU.mult))
                dve.wait_ge(s_weights, n_weights)
                if layer == 0:
                    link(dve.tensor_scalar(wt[0:S0, 0, :], wt[0:S0, 0, :], 1.0 / np.sqrt(S0), None, ALU.mult))
                    link(dve.tensor_scalar(wt[S0:P, 0, :], wt[S0:P, 0, :], float(1.0 / np.sqrt(V0)), None, ALU.mult))
                    link(dve.tensor_scalar(wt[0:V0, 1, :], wt[0:V0, 1, :], float(1.0 / np.sqrt(V0)), None, ALU.mult))
                dve.tensor_copy(stat[:, 2, 0:1], stat[:, 3, 0:1]).then_inc(s_ready, 1)

                def emit(i, par):
                    dve.wait_ge(s_prod, i + (par + 1))
                    wait(dve, s_store[par], left(i, par, 4, n_store))
                    if layer == 0:
                        j = (i + par) if isinstance(i, int) else bass.ds(i + par, 1)
                        dve.tensor_copy(k.selfc[:, j, :], prod_ps[par % 2][:, D:cols])
                        dve.tensor_copy(outb[:, par, 0:D], prod_ps[par % 2][:, 0:D]).then_inc(s_out, 1)
                    else:
                        dve.tensor_copy(outb[:, par, :], prod_ps[par % 2][:, 0:cols]).then_inc(s_out, 1)

                sweep(dve, W, emit, unroll=4)


def layer0_update(k):
    nc, a, W = k.nc, k.a, WINDOWS
    with ExitStack() as ctx:
        sb = lambda name, shape, dt=F32: k.sb("u_" + name, shape, dt, ctx)
        wt = sb("wt", [P, 3, 192])
        sums = sb("sums", [P, 4, AGG0])
        turned = sb("turned", [P, 2, AGG0])
        scol = sb("scol", [P, 3])
        sil = sb("sil", [P, W, 96])
        s_zero, s_weights, s_chain, s_wready = k.sem("u_zero"), k.sem("u_weights"), k.sem("u_chain"), k.sem("u_wready")
        s_sums = [k.sem(f"u_sums{q}") for q in range(4)]
        s_turn, s_turned, s_prod, s_out, s_sil = k.sem("u_turn"), k.sem("u_turned"), k.sem("u_prod"), k.sem("u_out"), k.sem("u_sil")
        turn_ps = [k.bank(0), k.bank(1)]
        prod_ps = [k.bank(2), k.bank(3)]
        W2s, W2v = a["L0_gnn_W2_s"], a["L0_gnn_W2_v"]
        blocks = [(0, 0, W2s[0:S0, :])]
        blocks += [(S0 + V0 * c, 96 + V0 * c, W2v[S0:96, :]) for c in range(3)]
        blocks += [(160 + S0 * c, 96 + V0 * c, W2v[0:S0, :]) for c in range(3)]
        blocks += [(352, 0, W2s[S0:96, :])]
        n_dma = 16 * (len(blocks) + 1)
        with nc.Block() as block:

            @block.gpsimd
            def _(pool):
                pool.memset(wt[:, :, :], 0.0).then_inc(s_zero, 1)

            @block.sync
            def _(sp):
                sp.wait_ge(s_zero, 1)
                n = sum(place(sp, s_weights, wt, r, c, w) for r, c, w in blocks)
                assert n == n_dma

                def load(i, par):
                    k.wait(sp, s_turn, i + (par - 3))
                    sp.dma_start(sums[:, par, :], k.agg0[bass.ds((i + par) * P, P), :]).then_inc(s_sums[par], 16)

                sweep(sp, W, load, unroll=4)

            @block.tensor
            def _(pe):
                def turn(i, par):
                    pe.wait_ge(s_sums[par], landed(i, par, 4, 1))
                    wait(pe, s_turned, i + (par - 1))
                    for c in range(3):
                        ins = pe.transpose(turn_ps[par % 2][:, c * P:(c + 1) * P], sums[:, par, c * P:(c + 1) * P], k.ident[:, :])
                    ins.then_inc(s_turn, 1)

                def product(i, par):
                    pe.wait_ge(s_turned, i + (par + 1))
                    wait(pe, s_out, i + (par - 1))
                    for c in range(3):
                        ins = pe.matmul(prod_ps[par % 2][:, 0:192], turned[:, par % 2, c * P:(c + 1) * P], wt[:, c, :],
                                        start=(c == 0), stop=(c == 2))
                    ins.then_inc(s_prod, 1)

                def step(i, par):
                    if live(i, par, W):
                        turn(i, par)
                    j, q = back(i, par, 1, 4)
                    if live(j, q, W):
                        product(j, q)

                pe.wait_ge(s_wready, 1)
                sweep(pe, W, step, 1, unroll=4)

            @block.scalar
            def _(act):
                def evacuate(i, par):
                    act.wait_ge(s_turn, i + (par + 1))
                    wait(act, s_prod, i + (par - 1))
                    act.copy(turned[:, par % 2, :], turn_ps[par % 2][:, 0:AGG0]).then_inc(s_turned, 1)

                sweep(act, W, evacuate, unroll=4)
                act.wait_ge(s_out, W)
                act.activation(sil[:, :, :], k.selfc[:, :, 0:96], ACT.Silu).then_inc(s_sil, 1)

            @block.vector
            def _(dve):
                link = Chain(dve, s_chain)
                base = float(1.0 / (np.sqrt(AVG_DEG) * np.sqrt(96.0)))
                link(dve.memset(scol[:, :], base))
                q, c = 352 % P, 352 // P
                link(dve.memset(scol[q:q + V0, c:c + 1], base / R3))
                dve.wait_ge(s_weights, n_dma)
                for c in range(3):
                    link(dve.tensor_scalar(wt[:, c, :], wt[:, c, :], scol[:, c:c + 1], None, ALU.mult))
                dve.tensor_copy(scol[:, 0:1], scol[:, 1:2]).then_inc(s_wready, 1)

                def add(i, par):
                    dve.wait_ge(s_prod, i + (par + 1))
                    j = bass.ds(i + par, 1)
                    dve.tensor_tensor(k.selfc[:, j, :], k.selfc[:, j, :],
                                      prod_ps[par % 2][:, 0:192].rearrange("p (a n) -> p a n", a=1), ALU.add).then_inc(s_out, 1)

                sweep(dve, W, add, unroll=4)
                dve.wait_ge(s_sil, 1)
                link(dve.tensor_tensor(k.resid[:, :, 0:S0], k.resid[:, :, 0:S0], sil[:, :, 0:S0], ALU.add))
                comp = lambda t, lo: t[:, :, lo:lo + 96].rearrange("p j (c m) -> p j c m", c=3)
                for c in range(3):
                    t = k.selfc[:, :, 96 + V0 * c:96 + V0 * (c + 1)]
                    link(dve.tensor_tensor(t, t, sil[:, :, S0:96], ALU.mult))
                link(dve.tensor_tensor(k.resid[:, :, S0:D], k.resid[:, :, S0:D], k.selfc[:, :, 96:192], ALU.add))


def edges0(k):
    nc, a = k.nc, k.a
    U = 8
    with ExitStack() as ctx:
        sb = lambda name, shape, dt=F32: k.sb("e0_" + name, shape, dt, ctx)
        fc1, b1 = sb("fc1", [NB0, HID]), sb("b1", [HID, 1])
        fc2 = sb("fc2", [HID + 1, WN0])
        ends = sb("ends", [P, U, 2, LANES], I32)
        sh = sb("sh", [P, U, LANES, 6])
        embed = sb("embed", [NB0, U, GE])
        hid = sb("hid", [HID + 1, 2, GE])
        xg = sb("xg", [P, U, LANES, D])
        x0 = sb("x0", [P, 2, LANES, D])
        rel = sb("rel", [P, 2, LANES])
        sel = sb("sel", [P, 2, LANES, P])
        wsv, wvv = sb("wsv", [P, 2, LANES, S0]), sb("wvv", [P, 2, LANES, 96])
        vy, dot2 = sb("vy", [P, LANES, 96]), sb("dot2", [P, LANES, V0])
        msg = sb("msg", [P, 2, LANES, AGG0])
        acc = sb("acc", [P, 2, AGG0])
        names = ["weights", "ones", "hid", "hidS", "wps", "vec", "agg", "acc", "x0", "far"]
        s_weights, s_ones, s_hid, s_hidS, s_wps, s_vec, s_agg, s_acc, s_x0, s_far = [k.sem("e0_" + n) for n in names]
        s_load = [k.sem(f"e0_load{q}") for q in range(U)]
        s_gather = [k.sem(f"e0_gather{q}") for q in range(U)]
        s_flush = [k.sem(f"e0_flush{q}") for q in range(2)]
        hid_ps = k.bank(0)
        w_ps = [k.bank(q, 2).rearrange("p (l n) -> p l n", l=LANES) for q in (1, 3)]
        agg_ps = [k.bank(5), k.bank(6)]
        NV = 10
        NF = 6
        with nc.Block() as block:

            @block.sync
            def _(sp):
                sp.dma_start(fc1[:, :], a["L0_gnn_fc_w1"]).then_inc(s_weights, 16)
                sp.dma_start(b1[:, :], a["L0_gnn_fc_b1"].rearrange("(n a) -> n a", a=1)).then_inc(s_weights, 16)
                sp.dma_start(fc2[0:HID, :], a["L0_gnn_fc_w2"]).then_inc(s_weights, 16)
                sp.dma_start(fc2[HID:HID + 1, :], a["L0_gnn_fc_b2"].rearrange("(a n) -> a n", a=1)).then_inc(s_weights, 16)

                def load(i, par):
                    g = sp.value_load(k.step_group[0:1, bass.ds(i + par, 1)], min_val=0, max_val=GROUPS - 1)
                    k.wait(sp, s_gather[par], left(i, par, U, 4))
                    k.wait(sp, s_vec, (i + (par - U + 1)) * NV)
                    k.wait(sp, s_far, (i + (par - U + 1)) * NF)
                    k.wait(sp, s_hid, i + (par - U + 1))
                    for t, name in ((ends, "ends_g"), (sh, "ea6_g")):
                        sp.dma_start(t[:, par, :, :].rearrange("p l c -> p (l c)"),
                                     a[name][bass.ds(g * P, P), :]).then_inc(s_load[par], 16)
                    sp.dma_start(embed[:, par, :], a["ea8_g"][bass.ds(g * NB0, NB0), :]).then_inc(s_load[par], 16)

                def flush(i, par):
                    r = sp.value_load(k.step_row[0:1, bass.ds(i + par, 1)], min_val=0, max_val=WINDOWS + SPARE - 1)
                    k.wait(sp, s_acc, i + (par + 1))
                    sp.dma_start(k.agg0[bass.ds(r * P, P), :], acc[:, par % 2, :]).then_inc(s_flush[par % 2], 16)

                def step(i, par):
                    if live(i, par, STEPS):
                        load(i, par)
                    j, q = back(i, par, 5, U)
                    if live(j, q, STEPS):
                        flush(j, q)

                sweep(sp, STEPS, step, 5, first=U, unroll=U)
                for q in range(2):
                    sp.wait_ge(s_flush[q], 16 * (STEPS // 2))

            @block.gpsimd
            def _(pool):
                pool.memset(hid[HID:HID + 1, :, :], 1.0).then_inc(s_ones, 1)

                def gather(i, par):
                    k.wait(pool, s_load[par], landed(i, par, U, 3))
                    k.wait(pool, s_vec, (i + (par - U + 1)) * NV)
                    k.wait(pool, s_x0, (i + (par - U + 1)) * LANES)
                    for lane in range(LANES):
                        pool.indirect_dma_start(
                            out=xg[:, par, lane, :], out_offset=None, in_=k.table0[:, :],
                            in_offset=bass.IndirectOffsetOnAxis(ap=ends[:, par, 0, lane:lane + 1], axis=0),
                        ).then_inc(s_gather[par], 16)

                sweep(pool, STEPS, gather, unroll=U)

            @block.tensor
            def _(pe):
                def hidden(i, par):
                    pe.wait_ge(s_load[par], landed(i, par, U, 3))
                    wait(pe, s_hidS, i + par)
                    pe.matmul(hid_ps[0:HID, :], fc1[:, :], embed[:, par, :], start=True, stop=True).then_inc(s_hid, 1)

                def weights(i, par):
                    pe.wait_ge(s_hidS, i + (par + 1))
                    wait(pe, s_vec, (i + (par - 1)) * NV)
                    for lane in range(LANES):
                        ins = pe.matmul(w_ps[par % 2][:, lane, 0:WN0], hid[:, par % 2, lane * P:(lane + 1) * P], fc2[:, :],
                                        start=True, stop=True)
                    ins.then_inc(s_wps, 1)

                def sums(i, par):
                    pe.wait_ge(s_vec, (i + (par + 1)) * NV)
                    pe.wait_ge(s_far, (i + (par + 1)) * NF)
                    wait(pe, s_acc, i + (par - 1))
                    for lane in range(LANES):
                        ins = pe.matmul(agg_ps[par % 2][:, 0:AGG0], sel[:, par % 2, lane, :], msg[:, par % 2, lane, :],
                                        start=(lane == 0), stop=(lane == LANES - 1))
                    ins.then_inc(s_agg, 1)

                def step(i, par):
                    if live(i, par, STEPS):
                        hidden(i, par)
                    j, q = back(i, par, 1, U)
                    if live(j, q, STEPS):
                        weights(j, q)
                    j, q = back(i, par, 3, U)
                    if live(j, q, STEPS):
                        sums(j, q)

                pe.wait_ge(s_weights, 64)
                pe.wait_ge(s_ones, 1)
                sweep(pe, STEPS, step, 3, unroll=U)

            @block.scalar
            def _(act):
                act.wait_ge(s_weights, 64)

                def silu(i, par):
                    act.wait_ge(s_hid, i + (par + 1))
                    wait(act, s_wps, i + (par - 1))
                    act.activation(hid[0:HID, par % 2, :], hid_ps[0:HID, :], ACT.Silu, bias=b1[:, 0:1]).then_inc(s_hidS, 1)

                def times_y0(i, par):
                    act.wait_ge(s_load[par], landed(i, par, U, 3))
                    act.wait_ge(s_gather[par], landed(i, par, U, 4))
                    wait(act, s_vec, (i + (par - 1)) * NV)
                    for lane in range(LANES):
                        act.mul(x0[:, par % 2, lane, :], xg[:, par, lane, :], sh[:, par, lane, 0:1]).then_inc(s_x0, 1)

                def far_lanes(i, par):
                    act.wait_ge(s_vec, (i + par) * NV + 2)
                    wait(act, s_agg, i + (par - 1))
                    for lane in (2, 3):
                        for c in range(3):
                            act.mul(msg[:, par % 2, lane, 160 + S0 * c:160 + S0 * (c + 1)], wsv[:, par % 2, lane, :],
                                    sh[:, par, lane, 1 + c:2 + c]).then_inc(s_far, 1)

                def step(i, par):
                    j, q = back(i, par, 2, U)
                    if live(j, q, STEPS):
                        times_y0(j, q)
                    j, q = back(i, par, 3, U)
                    if live(j, q, STEPS):
                        far_lanes(j, q)
                    if live(i, par, STEPS):
                        silu(i, par)

                sweep(act, STEPS, step, 3, unroll=U)

            @block.vector
            def _(dve):
                def messages(i, par):
                    done = Count(dve, s_vec, i + par, NV)
                    t = par % 2
                    dve.wait_ge(s_load[par], landed(i, par, U, 3))
                    dve.wait_ge(s_gather[par], landed(i, par, U, 4))
                    dve.wait_ge(s_wps, i + (par + 1))
                    wait(dve, s_agg, i + (par - 1))
                    wait(dve, s_far, (i + (par - 1)) * NF)
                    w = w_ps[t]
                    out = msg[:, t]
                    s, v = xg[:, par, :, 0:S0], xg[:, par, :, S0:D].rearrange("p l (c m) -> p l c m", c=3)
                    comp = lambda ap, n=V0: ap.rearrange("p l (c m) -> p l c m", m=n)
                    wv = lambda lo: bc(w[:, :, lo:lo + V0].rearrange("p l (a m) -> p l a m", a=1), [P, LANES, 3, V0])
                    yc = lambda lanes, n: bc(sh[:, par, 0:lanes, 1:4].rearrange("p l (c a) -> p l c a", a=1), [P, lanes, 3, n])
                    done(dve.tensor_scalar(rel[:, t, :], ends[:, par, 1, :], k.step_base[:, bass.ds(i + par, 1)], None, ALU.subtract))
                    done(dve.tensor_tensor(wsv[:, t], w[:, :, S0:2 * S0], s, ALU.mult))
                    done(dve.tensor_tensor(comp(wvv[:, t]), wv(160), v, ALU.mult))
                    done.at(1)
                    done(dve.tensor_tensor(sel[:, t], bc(k.iota[:, :].rearrange("p (a n) -> p a n", a=1), [P, LANES, P]),
                                           bc(rel[:, t, :].rearrange("p (l a) -> p l a", a=1), [P, LANES, P]), ALU.is_equal))
                    done.at(3)
                    done(dve.tensor_tensor(comp(out[:, 0:2, 160:352], S0),
                                           bc(wsv[:, t, 0:2].rearrange("p l (a m) -> p l a m", a=1), [P, 2, 3, S0]), yc(2, S0), ALU.mult))
                    done(dve.tensor_tensor(comp(vy[:, :, :]), comp(wvv[:, t]), yc(LANES, V0), ALU.mult))
                    dve.wait_ge(s_x0, (i + (par + 1)) * LANES)
                    done(dve.tensor_tensor(out[:, :, 0:S0], w[:, :, 0:S0], x0[:, t, :, 0:S0], ALU.mult))
                    done.at(6)
                    done(dve.tensor_tensor(dot2[:, :, :], vy[:, :, 0:V0], vy[:, :, V0:2 * V0], ALU.add))
                    done(dve.tensor_tensor(comp(out[:, :, S0:160]), wv(128), comp(x0[:, t, :, S0:D]), ALU.mult))
                    done.at(8)
                    done(dve.tensor_tensor(out[:, :, 352:384], dot2[:, :, :], vy[:, :, 2 * V0:96], ALU.add))
                    assert done.n == NV

                add_sums = accumulate(k, dve, s_agg, s_acc, s_flush, acc, agg_ps, AGG0)

                def step(i, par):
                    if live(i, par, STEPS):
                        messages(i, par)
                    j, q = back(i, par, 2, U)
                    if live(j, q, STEPS):
                        add_sums(j, q)

                sweep(dve, STEPS, step, 2, unroll=U)


def accumulate(k, dve, s_agg, s_acc, s_flush, acc, agg_ps, width):
    slots = len(s_flush)

    def add_sums(i, par):
        t, ps = par % slots, agg_ps[par % 2][:, 0:width]
        dve.wait_ge(s_agg, i + (par + 1))
        wait(dve, s_flush[t], left(i, par, slots, 1))
        wait(dve, s_acc, i + par)
        if isinstance(i, int) and i + par == 0:
            dve.tensor_copy(acc[:, t, :], ps).then_inc(s_acc, 1)
        else:
            dve.scalar_tensor_tensor(acc[:, t, :], acc[:, (t - 1) % slots, :], k.step_keep[:, bass.ds(i + par, 1)],
                                     ps, ALU.mult, ALU.add).then_inc(s_acc, 1)
    return add_sums


class Count:

    def __init__(self, eng, sem, item, per):
        self.eng, self.sem, self.item, self.per, self.n = eng, sem, item, per, 0

    def __call__(self, ins):
        self.n += 1
        assert self.n <= self.per
        ins.then_inc(self.sem, 1)

    def at(self, n):
        self.eng.wait_ge(self.sem, self.item * self.per + n)

    def last(self):
        self.at(self.n)


def edges1(k):
    nc, a = k.nc, k.a
    U, SLOTS = 8, 4
    with ExitStack() as ctx:
        sb = lambda name, shape, dt=F32: k.sb("e1_" + name, shape, dt, ctx)
        w_rbf = sb("w_rbf", [NB1, WN1])
        ws_val, ws_val_t, wg = sb("ws_val", [96, S0]), sb("ws_val_t", [S0, 96]), sb("wg", [S0, V0])
        adot = sb("adot", [P, HEADS * AS])
        w1a, w1b, w1c = sb("w1a", [96, 164]), sb("w1b", [P, P]), sb("w1c", [P, 96])
        HC, PART = 48, 24
        w2a, w2b, w2c = sb("w2a", [96, HEADS * PART]), sb("w2b", [P, HEADS * PART]), sb("w2c", [P, HEADS * PART])
        c2a, c2b, c2c = sb("c2a", [96, 1]), sb("c2b", [P, 1]), sb("c2c", [P, 1])
        ends = sb("ends", [P, U, 2, LANES], I32)
        YW = LANES * (6 + 3 * HEADS)
        y_all = sb("y", [P, U, YW])
        y = y_all[:, :, 0:LANES * 6].rearrange("p u (l c) -> p u l c", l=LANES)
        rbf = sb("rbf", [NB1, U, GE])
        msg = sb("msg", [P, SLOTS, LANES, D])
        msg0 = sb("msg0", [P, SLOTS, LANES, D])
        vy = [sb(f"vy{q}", [P, LANES, 3, V0]) for q in range(2)]
        cross_a, cross_b = [sb(f"cross_a{q}", [P, LANES, 96]) for q in range(2)], [sb(f"cross_b{q}", [P, LANES, 96]) for q in range(2)]
        dot2, dot = [sb(f"dot2{q}", [P, LANES, V0]) for q in range(2)], sb("dot", [P, LANES, V0])
        q1, q2 = sb("q1", [P, 2, LANES, QW]), sb("q2", [P, 2, LANES, QW])
        t1, t2 = sb("t1", [P, 3, GE]), sb("t2", [P, 3, GE])
        gate = sb("gate", [P, 2, LANES, V0])
        absa, lin = sb("absa", [P, 2, LANES, HEADS * AS]), sb("lin", [P, 2, LANES, HEADS])
        w_lin = sb("w_lin", [96, HEADS * AS])
        headsum = sb("headsum", [P, LANES, HEADS])
        weighed = sb("weighed", [P, LANES, HEADS * AS])
        val = sb("val", [P, 2, LANES, 96])
        sxy, sxy_late = sb("sxy", [P, LANES, 3, V0]), sb("sxy_late", [P, LANES * HEADS, 3, AV])
        outv = sb("outv", [P, SLOTS, LANES, D])
        vec_out = sb("vec_out", [P, 2, LANES, P])
        outl = sb("outl", [P, SLOTS, LANES, HEADS])
        names = ["zero", "weights", "chain", "pre", "wg", "ready", "w", "tp1", "mid", "post", "turn1", "turned1", "turn2",
                 "turned2", "val", "sig", "sy0", "prod2", "copied", "msg0", "vy0", "vec"]
        (s_zero, s_weights, s_chain, s_pre, s_wg, s_ready, s_w, s_tp1, s_mid, s_post, s_turn1, s_turned1, s_turn2,
         s_turned2, s_val, s_sig, s_sy0, s_prod2, s_copied, s_msg0, s_vy0, s_vec) = [k.sem("e1_" + n) for n in names]
        s_load = [k.sem(f"e1_load{q}") for q in range(U)]
        s_src = [k.sem(f"e1_src{q}") for q in range(SLOTS)]
        s_dst = [k.sem(f"e1_dst{q}") for q in range(SLOTS)]
        s_store = [k.sem(f"e1_store{q}") for q in range(SLOTS)]
        w_ps = k.bank(0, 2).rearrange("p (l n) -> p l n", l=LANES)
        turn_ps = [k.bank(2), k.bank(3)]
        val_ps = k.bank(4).rearrange("p (l n) -> p l n", l=LANES)
        vec_ps = k.bank(5).rearrange("p (l n) -> p l n", l=LANES)
        out_ps = k.bank(6, 2).rearrange("p (l n) -> p l n", l=LANES)
        ALPHA = 192
        K1, KM, KP = 13, 14, 2
        READ, GATED = 3, 5
        CHUNKS = ((0, 96), (96, P), (224, P))
        Wsv, Wvv, Wvs, Wvl = a["L1_gnn_Ws_val"], a["L1_gnn_Wv_val"], a["L1_gnn_Ws_vlin"], a["L1_gnn_Wv_vlin"]
        col = lambda name: a["L1_gnn_" + name].rearrange("(n a) -> n a", a=1)

        def head_cols(ap, lo, n):
            return ap.rearrange("p (h n) -> p h n", h=HEADS)[:, :, lo:lo + n]

        def weight_loads():
            by_head = lambda w, n: w.rearrange("p (h n) -> p h n", h=HEADS)
            yield w_rbf[:, :], a["L1_gnn_W_rbf"]
            yield ws_val[:, :], Wsv
            yield wg[:, :], a["L1_gnn_Wg"]
            yield adot[:, :], a["L1_gnn_alpha_dot"].rearrange("a h s -> a (h s)").to_broadcast([P, HEADS * AS])
            yield w1a[:, 0:S0], Wsv
            yield w1a[:, 100:164], a["L1_gnn_W_alpha"]
            yield w1b[0:S0, 96:P], Wvv[0:S0, :]
            yield w1b[64:96, 0:32], Wvv[S0:96, :]
            yield w1b[96:P, 32:64], Wvv[S0:96, :]
            yield w1c[0:32, 64:96], Wvv[S0:96, :]
            for c in range(3):
                yield w1c[32 + 32 * c:64 + 32 * c, 32 * c:32 * c + 32], Wvv[96:P, :]
            yield head_cols(w2a[:, :], 0, AS), by_head(Wvs, AS)
            yield head_cols(w2b[0:S0, :], 2 * AV, AV), by_head(Wvl[0:S0, :], AV)
            for c in range(2):
                yield head_cols(w2b[64 + 32 * c:96 + 32 * c, :], AV * c, AV), by_head(Wvl[S0:96, :], AV)
            yield head_cols(w2c[0:32, :], 0, AV), by_head(Wvl[S0:96, :], AV)
            for c in range(3):
                yield head_cols(w2c[32 + 32 * c:64 + 32 * c, :], AV * ((c + 1) % 3), AV), by_head(Wvl[96:P, :], AV)
            yield c2a[0:S0, :], col("w2_ss")
            yield c2a[S0:96, :], col("w2_vv0")
            yield c2b[0:S0, :], col("w2_sv")
            yield c2b[64:96, :], col("w2_vs")
            yield c2b[96:P, :], col("w2_vs")
            yield c2c[0:32, :], col("w2_vs")
            for c in range(3):
                yield c2c[32 + 32 * c:64 + 32 * c, :], col("w2_vv1")

        n_weights = 16 * 30
        with nc.Block() as block:

            @block.sync
            def _(sp):
                sp.wait_ge(s_zero, 5)
                n = 0
                for t, w in weight_loads():
                    sp.dma_start(t, w).then_inc(s_weights, 16)
                    n += 16
                assert n == n_weights, n

                def load(i, par):
                    g = i + par
                    k.wait(sp, s_dst[par % SLOTS], left(i, par - SLOTS, SLOTS, 4))
                    k.wait(sp, s_w, g - U + 1)
                    k.wait(sp, s_mid, (g - U + 1) * KM)
                    k.wait(sp, s_post, (g - U + 1) * KP)
                    k.wait(sp, s_vy0, (g - U + 1) * LANES)
                    k.wait(sp, s_sy0, (g - U + 1) * LANES)
                    sp.dma_start(ends[:, par, :, :].rearrange("p q l -> p (q l)"),
                                 a["ends_g"][bass.ds(g * P, P), :]).then_inc(s_load[par], 16)
                    sp.dma_start(y_all[:, par, :], a["ea18_g"][bass.ds(g * P, P), :]).then_inc(s_load[par], 16)
                    sp.dma_start(rbf[:, par, :], a["ea16_g"][bass.ds(g * NB1, NB1), :]).then_inc(s_load[par], 16)

                def store(i, par):
                    g = i + par
                    slot = par % SLOTS
                    k.wait(sp, s_post, (g + 1) * KP)
                    sp.dma_start(k.values.rearrange("(q l) d -> q l d", l=LANES)[bass.ds(g * P, P), :, :],
                                 outv[:, slot, :, 0:D]).then_inc(s_store[slot], 16)
                    sp.dma_start(k.logits.rearrange("(q l) h -> q (l h)", l=LANES)[bass.ds(g * P, P), :],
                                 outl[:, slot, :, :].rearrange("p l h -> p (l h)")).then_inc(s_store[slot], 16)

                def step(i, par):
                    if live(i, par, GROUPS):
                        load(i, par)
                    j, q = back(i, par, 6, U)
                    if live(j, q, GROUPS):
                        store(j, q)

                sweep(sp, GROUPS, step, 6, unroll=U)
                for q in range(SLOTS):
                    sp.wait_ge(s_store[q], 32 * (GROUPS // SLOTS))

            @block.gpsimd
            def _(pool):
                for t in (w1b, w1c, w2a, w2b, w2c):
                    pool.memset(t[:, :], 0.0).then_inc(s_zero, 1)

                def sources(i, par):
                    k.wait(pool, s_load[par], landed(i, par, U, 3))
                    slot = par % SLOTS
                    k.wait(pool, s_tp1, (i + (par - SLOTS + 1)) * K1)
                    k.wait(pool, s_msg0, (i + (par - SLOTS + 1)) * LANES)
                    for lane in range(LANES):
                        pool.indirect_dma_start(
                            out=msg[:, slot, lane, :], out_offset=None, in_=k.table_src[:, :],
                            in_offset=bass.IndirectOffsetOnAxis(ap=ends[:, par, 0, lane:lane + 1], axis=0),
                        ).then_inc(s_src[slot], 16)

                def destinations(i, par):
                    slot = par % SLOTS
                    k.wait(pool, s_src[slot], landed(i, par, SLOTS, 4))
                    for lane in range(LANES):
                        pool.indirect_dma_start(
                            out=msg[:, slot, lane, :], out_offset=None, in_=k.table_dst[:, :],
                            in_offset=bass.IndirectOffsetOnAxis(ap=ends[:, par, 1, lane:lane + 1], axis=0),
                            compute_op=ALU.add,
                        ).then_inc(s_dst[slot], 16)

                def step(i, par):
                    if live(i, par, GROUPS):
                        sources(i, par)
                    j, q = back(i, par, 1, U)
                    if live(j, q, GROUPS):
                        destinations(j, q)

                sweep(pool, GROUPS, step, 1, unroll=U)

            @block.tensor
            def _(pe):
                pe.wait_ge(s_weights, n_weights)
                pe.transpose(turn_ps[0][0:S0, 0:96], ws_val[:, :], k.ident[0:96, 0:96]).then_inc(s_pre, 1)
                pe.wait_ge(s_wg, 1)
                pe.matmul(val_ps[0:96, 0, 0:V0], ws_val_t[:, :], wg[:, :], start=True, stop=True).then_inc(s_pre, 1)
                pe.wait_ge(s_ready, 1)

                def radial(i, par):
                    pe.wait_ge(s_load[par], landed(i, par, U, 3))
                    wait(pe, s_tp1, (i + par) * K1)
                    for lane in range(LANES):
                        ins = pe.matmul(w_ps[:, lane, 0:WN1], rbf[:, par, lane * P:(lane + 1) * P], w_rbf[:, :],
                                        start=True, stop=True)
                    ins.then_inc(s_w, 1)

                def turn(src, chunk, bank, sem):
                    lo, m = CHUNKS[chunk]
                    for lane in range(LANES):
                        ins = pe.transpose(turn_ps[bank][0:m, lane * P:(lane + 1) * P], src[:, lane, lo:lo + m],
                                           k.ident[:, :])
                    ins.then_inc(sem, 1)

                def turn_first(i, par, chunk):
                    g = i + par
                    pe.wait_ge(s_tp1, (g + 1) * K1)
                    if chunk < 2:
                        wait(pe, s_turned2, (g - 2) * 3 + chunk + 2)
                    else:
                        pe.wait_ge(s_turned1, g * 3 + 1)
                    turn(q1[:, par % 2], chunk, chunk % 2, s_turn1)

                def turn_second(i, par, chunk):
                    g = i + par
                    pe.wait_ge(s_mid, (g + 1) * KM)
                    pe.wait_ge(s_vy0, (g + 1) * LANES)
                    pe.wait_ge(s_sy0, (g + 1) * LANES)
                    if chunk < 2:
                        last = isinstance(g, int) and g == GROUPS - 1
                        pe.wait_ge(s_turned1, GROUPS * 3 if last else (g + 1) * 3 + chunk + 2)
                        if last:
                            pe.wait_ge(s_turned2, (GROUPS - 1) * 3)
                    else:
                        pe.wait_ge(s_turned2, g * 3 + 1)
                    turn(q2[:, par % 2], chunk, (chunk + 1) % 2, s_turn2)

                def values(i, par):
                    g = i + par
                    pe.wait_ge(s_turned1, g * 3 + 1)
                    wait(pe, s_sig, g * 4)
                    wait(pe, s_copied, (g - 1) * 2)
                    for lane in range(LANES):
                        e = slice(lane * P, (lane + 1) * P)
                        pe.matmul(val_ps[:, lane, 0:100], t1[0:96, 0, e], w1a[:, 0:100], start=True, stop=True)
                        ins = pe.matmul(out_ps[:, lane, ALPHA:ALPHA + 64], t1[0:96, 0, e], w1a[:, 100:164],
                                        start=True, stop=True)
                    ins.then_inc(s_val, 1)

                def vectors(i, par, lanes):
                    g = i + par
                    pe.wait_ge(s_turned1, (g + 1) * 3)
                    wait(pe, s_mid, (g - 1) * KM + READ)
                    for lane in lanes:
                        e = slice(lane * P, (lane + 1) * P)
                        pe.matmul(vec_ps[:, lane, :], t1[:, 1, e], w1b[:, :], start=True, stop=True)
                        ins = pe.matmul(vec_ps[:, lane, 0:96], t1[:, 2, e], w1c[:, :], start=False, stop=True,
                                        skip_group_check=True)
                    ins.then_inc(s_vec, 1)

                def outputs(i, par):
                    g = i + par
                    pe.wait_ge(s_turned2, (g + 1) * 3)
                    wait(pe, s_copied, g * 2)
                    part = lambda ap, lo: ap.rearrange("p (h n) -> p h n", h=HEADS)[:, :, lo:lo + PART]
                    for lane in range(LANES):
                        e, o = slice(lane * P, (lane + 1) * P), out_ps[:, lane, 0:192]
                        pe.matmul(part(o, 0), t2[0:96, 0, e], part(w2a[:, :], 0), start=True, stop=True)
                        pe.matmul(part(o, PART), t2[:, 1, e], part(w2b[:, :], 0), start=False, stop=True,
                                  skip_group_check=True)
                        ins = pe.matmul(part(o, AS), t2[:, 2, e], part(w2c[:, :], 0), start=False, stop=True,
                                        skip_group_check=True)
                    ins.then_inc(s_prod2, 1)

                def step(i, par):
                    this, (j, q), (n, r) = live(i, par, GROUPS), back(i, par, 1, U), back(i, par, -1, U)
                    if this:
                        turn_first(i, par, 0)
                        turn_first(i, par, 1)
                    if not isinstance(n, int) or n + r < GROUPS:
                        radial(n, r)
                    if this:
                        turn_first(i, par, 2)
                        values(i, par)
                    if live(j, q, GROUPS):
                        turn_second(j, q, 0)
                        turn_second(j, q, 1)
                    if this:
                        vectors(i, par, (0, 1))
                    if live(j, q, GROUPS):
                        turn_second(j, q, 2)
                    if this:
                        vectors(i, par, (2, 3))
                    if live(j, q, GROUPS):
                        outputs(j, q)

                radial(0, 0)
                sweep(pe, GROUPS, step, 1, last=U, unroll=U)

            @block.scalar
            def _(act):
                act.wait_ge(s_pre, 1)
                act.copy(ws_val_t[:, :], turn_ps[0][0:S0, 0:96]).then_inc(s_wg, 1)

                def evacuate(i, par, dst, bank, turn_sem, turned_sem, chunks=(0, 1, 2)):
                    g = i + par
                    for c in chunks:
                        m = CHUNKS[c][1]
                        act.wait_ge(turn_sem, g * 3 + (c + 1))
                        if c == 0:
                            wait(act, s_vec if dst is t1 else s_prod2, g * 2 if dst is t1 else g)
                        act.copy(dst[0:m, c, :], turn_ps[(bank + c) % 2][0:m, :]).then_inc(turned_sem, 1)

                def gates(i, par):
                    g, t = i + par, par % 2
                    act.wait_ge(s_val, g + 1)
                    wait(act, s_turn2, (g - 1) * 3)
                    wait(act, s_mid, (g - 1) * KM)
                    act.activation(q2[:, t, :, 96:160], val_ps[:, :, 0:S0], ACT.Sigmoid).then_inc(s_sig, 1)
                    act.activation(gate[:, t], val_ps[:, :, S0:96], ACT.Sigmoid).then_inc(s_sig, 1)
                    act.activation(absa[:, t], out_ps[:, :, ALPHA:ALPHA + 64], ACT.Abs).then_inc(s_sig, 1)
                    act.copy(lin[:, t], val_ps[:, :, 96:100]).then_inc(s_sig, 1)

                def scalars_y0(i, par):
                    g, t = i + par, par % 2
                    act.wait_ge(s_sig, (g + 1) * 4)
                    for lane in range(LANES):
                        act.mul(q2[:, t, lane, 0:S0], q2[:, t, lane, 96:160], y[:, par, lane, 0:1]).then_inc(s_sy0, 1)

                def vectors_y0(i, par):
                    g, t = i + par, par % 2
                    act.wait_ge(s_mid, g * KM + GATED)
                    for lane in range(LANES):
                        act.mul(q2[:, t, lane, 160:256], val[:, t, lane, :], y[:, par, lane, 0:1]).then_inc(s_vy0, 1)

                def messages_y0(i, par):
                    act.wait_ge(s_load[par], landed(i, par, U, 3))
                    act.wait_ge(s_dst[par % SLOTS], landed(i, par, SLOTS, 4))
                    wait(act, s_tp1, (i + (par - SLOTS + 1)) * K1)
                    for lane in range(LANES):
                        act.mul(msg0[:, par % SLOTS, lane, :], msg[:, par % SLOTS, lane, :], y[:, par, lane, 0:1]).then_inc(s_msg0, 1)

                def copy_out(i, par):
                    act.wait_ge(s_prod2, i + (par + 1))
                    wait(act, s_store[par % SLOTS], left(i, par, SLOTS, 2))
                    wait(act, s_post, (i + (par - 1)) * KP)
                    by_head = lambda ap: ap.rearrange("p l (h n) -> p l h n", h=HEADS)
                    o = by_head(out_ps[:, :, 0:192])
                    act.copy(by_head(vec_out[:, par % 2, :, :]), o[:, :, :, AS:HC]).then_inc(s_copied, 1)
                    act.copy(by_head(outv[:, par % SLOTS, :, :])[:, :, :, 0:AS], o[:, :, :, 0:AS]).then_inc(s_copied, 1)

                def step(i, par):
                    this, (j, q), (o, r) = live(i, par, GROUPS), back(i, par, 1, U), back(i, par, 2, U)
                    if live(o, r, GROUPS):
                        copy_out(o, r)
                    if this:
                        evacuate(i, par, t1, 0, s_turn1, s_turned1, (0, 1))
                    if live(j, q, GROUPS):
                        vectors_y0(j, q)
                    if this:
                        evacuate(i, par, t1, 0, s_turn1, s_turned1, (2,))
                        gates(i, par)
                    if live(j, q, GROUPS):
                        evacuate(j, q, t2, 1, s_turn2, s_turned2)
                    if this:
                        scalars_y0(i, par)
                    n, r = back(i, par, -2, U)
                    if not isinstance(n, int) or n + r < GROUPS:
                        messages_y0(n, r)

                messages_y0(0, 0)
                messages_y0(0, 1)
                sweep(act, GROUPS, step, 2, last=U, unroll=U)

            @block.vector
            def _(dve):
                link = Chain(dve, s_chain)
                dve.wait_ge(s_weights, n_weights)
                dve.wait_ge(s_pre, 2)
                link(dve.tensor_copy(w1a[:, S0:96], val_ps[0:96, 0, 0:V0]))
                link(dve.tensor_tensor(w_lin[:, :], w1a[:, 100:164], adot[0:96, :], ALU.mult))
                link(dve.tensor_scalar(w_lin[:, :], w_lin[:, :], 0.6, None, ALU.mult))
                link(dve.tensor_reduce(w1a[:, 96:100], w_lin[:, :].rearrange("p (h s) -> p h s", h=HEADS), AX, ALU.add))
                link(dve.tensor_scalar(adot[:, :], adot[:, :], 0.4, None, ALU.mult))
                link(dve.tensor_scalar(w1a[S0:96, :], w1a[S0:96, :], 1.0 / R3, None, ALU.mult))
                for c in range(3):
                    r = slice(32 + 32 * c, 64 + 32 * c)
                    link(dve.tensor_scalar(w1c[r, :], w1c[r, :], 1.0 / R2, None, ALU.mult))
                    link(dve.tensor_scalar(c2c[r, :], c2c[r, :], 1.0 / R2, None, ALU.mult))
                link(dve.tensor_scalar(c2a[S0:96, :], c2a[S0:96, :], 1.0 / R3, None, ALU.mult))
                for w, c in ((w2a, c2a), (w2b, c2b), (w2c, c2c)):
                    link(dve.tensor_scalar(w[:, :], w[:, :], c[:, 0:1], None, ALU.mult))
                dve.memset(dot[:, 0, 0:1], 0.0).then_inc(s_ready, 1)

                comp = lambda ap: ap.rearrange("p l (c m) -> p l c m", c=3)
                one = lambda ap: ap.rearrange("p l (a m) -> p l a m", a=1)
                two = lambda ap: ap.rearrange("p l (c m) -> p l c m", c=2)
                three = lambda ap: bc(one(ap), [P, LANES, 3, V0])
                ys = lambda t, lo, n: bc(t[:, :, lo:lo + n].rearrange("p l (c a) -> p l c a", a=1), [P, LANES, n, V0])

                def products(done, v, y, h):
                    a, b = cross_a[h], cross_b[h]
                    done(dve.tensor_tensor(two(a[:, :, 0:64]), two(v[:, :, 32:96]), ys(y, 3, 2), ALU.mult))
                    done(dve.tensor_tensor(one(a[:, :, 64:96]), one(v[:, :, 0:32]), ys(y, 5, 1), ALU.mult))
                    done(dve.tensor_tensor(one(b[:, :, 0:32]), one(v[:, :, 64:96]), ys(y, 2, 1), ALU.mult))
                    done(dve.tensor_tensor(two(b[:, :, 32:96]), two(v[:, :, 0:64]), ys(y, 3, 2), ALU.mult))
                    done(dve.tensor_tensor(vy[h][:, :, :, :], comp(v), ys(y, 1, 3), ALU.mult))

                def first(i, par):
                    g, t = i + par, par % 2
                    done = Count(dve, s_tp1, g, K1)
                    m, yy, q, w = msg[:, par % SLOTS], y[:, par], q1[:, t], w_ps
                    dve.wait_ge(s_load[par], landed(i, par, U, 3))
                    dve.wait_ge(s_dst[par % SLOTS], landed(i, par, SLOTS, 4))
                    wait(dve, s_tp1, g * K1)
                    products(done, m[:, :, S0:D], yy, 0)
                    done.at(4)
                    done(dve.tensor_tensor(cross_a[0][:, :, :], cross_a[0][:, :, :], cross_b[0][:, :, :], ALU.subtract))
                    wait(dve, s_turn1, (g - 1) * 3)
                    dve.wait_ge(s_w, g + 1)
                    done.at(5)
                    done(dve.tensor_tensor(dot2[0][:, :, :], vy[0][:, :, 0, :], vy[0][:, :, 1, :], ALU.add))
                    done(dve.tensor_tensor(q[:, :, 96:160], w[:, :, S0:2 * S0], m[:, :, 0:S0], ALU.mult))
                    done.at(7)
                    done(dve.tensor_tensor(dot[:, :, :], dot2[0][:, :, :], vy[0][:, :, 2, :], ALU.add))
                    done(dve.tensor_tensor(comp(q[:, :, 256:352]), three(w[:, :, 192:224]), comp(cross_a[0][:, :, :]), ALU.mult))
                    dve.wait_ge(s_msg0, (g + 1) * LANES)
                    done(dve.tensor_tensor(q[:, :, 0:S0], w[:, :, 0:S0], msg0[:, par % SLOTS, :, 0:S0], ALU.mult))
                    done.at(9)
                    done(dve.tensor_tensor(q[:, :, S0:96], w[:, :, 160:192], dot[:, :, :], ALU.mult))
                    done(dve.tensor_tensor(comp(q[:, :, 160:256]), three(w[:, :, 128:160]), comp(msg0[:, par % SLOTS, :, S0:D]), ALU.mult))
                    assert done.n == K1, done.n

                def middle(i, par):
                    g, t = i + par, par % 2
                    done = Count(dve, s_mid, g, KM)
                    yy, q, v = y[:, par], q2[:, t], val[:, t]
                    dve.wait_ge(s_sig, (g + 1) * 4)
                    wait(dve, s_mid, g * KM)
                    wait(dve, s_vy0, (g - 1) * LANES)
                    done(dve.tensor_tensor(weighed[:, :, :], absa[:, t],
                                           bc(adot[:, :].rearrange("p (a n) -> p a n", a=1), [P, LANES, HEADS * AS]), ALU.mult))
                    dve.wait_ge(s_vec, (g + 1) * 2)
                    done(dve.tensor_tensor(sxy[:, :, :, :], three(vec_ps[:, :, 96:P]), ys(yy, 1, 3), ALU.mult))
                    done.at(2)
                    done(dve.tensor_tensor(comp(v), sxy[:, :, :, :], comp(vec_ps[:, :, 0:96]), ALU.add))
                    assert done.n == READ
                    done.at(2)
                    done(dve.tensor_reduce(headsum[:, :, :], weighed[:, :, :].rearrange("p l (h s) -> p l h s", h=HEADS),
                                           AX, ALU.add))
                    done.at(3)
                    done(dve.tensor_tensor(comp(v), comp(v), three(gate[:, t]), ALU.mult))
                    assert done.n == GATED
                    wait(dve, s_store[par % SLOTS], left(i, par, SLOTS, 2))
                    done.at(4)
                    done(dve.tensor_tensor(outl[:, par % SLOTS, :, :], headsum[:, :, :], lin[:, t], ALU.add))
                    done.at(5)
                    products(done, v, yy, 1)
                    done.at(10)
                    done(dve.tensor_tensor(q[:, :, 256:352], cross_a[1][:, :, :], cross_b[1][:, :, :], ALU.subtract))
                    done.at(11)
                    done(dve.tensor_tensor(dot2[1][:, :, :], vy[1][:, :, 0, :], vy[1][:, :, 1, :], ALU.add))
                    done.at(13)
                    done(dve.tensor_tensor(q[:, :, S0:96], dot2[1][:, :, :], vy[1][:, :, 2, :], ALU.add))
                    assert done.n == KM, done.n

                def post(i, par):
                    g, t = i + par, par % 2
                    done = Count(dve, s_post, g, KP)
                    dve.wait_ge(s_copied, (g + 1) * 2)
                    wait(dve, s_post, g * KP)
                    dve.wait_ge(s_mid, (g + 1) * KM)
                    v = vec_out[:, t].rearrange("p l (h n) -> p (l h) n", h=HEADS)
                    o = outv[:, par % SLOTS, :, :].rearrange("p l (h n) -> p (l h) n", h=HEADS)[:, :, AS:AS + 3 * AV]
                    comps = lambda ap: ap.rearrange("p q (c m) -> p q c m", m=AV)
                    full = [P, LANES * HEADS, 3, AV]
                    done(dve.tensor_tensor(sxy_late[:, :, :, :], bc(comps(v[:, :, 3 * AV:4 * AV]), full),
                                           bc(y_all[:, par, LANES * 6:YW].rearrange("p (q c a) -> p q c a", c=3, a=1), full), ALU.mult))
                    done.at(1)
                    done(dve.tensor_tensor(comps(o), comps(v[:, :, 0:3 * AV]), sxy_late[:, :, :, :], ALU.add))

                def step(i, par):
                    if live(i, par, GROUPS):
                        first(i, par)
                    j, q = back(i, par, 1, U)
                    if live(j, q, GROUPS):
                        middle(j, q)
                    j, q = back(i, par, 2, U)
                    if live(j, q, GROUPS):
                        post(j, q)

                sweep(dve, GROUPS, step, 2, unroll=U)


def softmax_weights(k):
    nc, a = k.nc, k.a
    with ExitStack() as ctx:
        sb = lambda name, shape, dt=F32: k.sb("sm_" + name, shape, dt, ctx)
        lg, run, top = sb("lg", [P, CH, HEADS]), sb("run", [P, CH, HEADS]), sb("top", [P, CH, HEADS])
        cur, near = sb("cur", [P, CH], I32), sb("near", [P, 2, CH], I32)
        pen = sb("pen", [P, 2, CH])
        ends = sb("ends", [P, 2 * HEADS])
        rows = sb("rows", [HEADS, 2 * P])
        inc = sb("inc", [HEADS, P])
        hand = sb("hand", [HEADS, P])
        start = sb("start", [P, HEADS])
        s_load, s_chain, s_pe, s_ends = k.sem("sm_load"), k.sem("sm_chain"), k.sem("sm_pe"), k.sem("sm_ends")
        s_exp, s_max, s_out = k.sem("sm_exp"), k.sem("sm_max"), k.sem("sm_out")
        flat = lambda t: t.rearrange("(p n) h -> p (n h)", p=P)
        edge = a["dst_edge"]
        with nc.Block() as block:

            @block.sync
            def _(sp):
                sp.dma_start(lg[:, :, :].rearrange("p n h -> p (n h)"), flat(k.logits)).then_inc(s_load, 16)
                for t, off in ((cur[:, :], 1), (near[:, 0, :], 0), (near[:, 1, :], 2)):
                    sp.dma_start(t, edge[off:off + EP].rearrange("(p n) -> p n", p=P)).then_inc(s_load, 16)
                sp.wait_ge(s_exp, 1)
                sp.dma_start(flat(k.weights_e), lg[:, :, :].rearrange("p n h -> p (n h)")).then_inc(s_out, 16)
                sp.wait_ge(s_out, 16)

            @block.tensor
            def _(pe):
                for d in range(2):
                    pe.wait_ge(s_ends, 2 * d + 1)
                    pe.transpose(k.bank(0)[0:HEADS, 0:P], ends[:, 0:HEADS], k.ident[:, :])
                    pe.transpose(k.bank(0)[0:HEADS, P:2 * P], ends[:, HEADS:2 * HEADS], k.ident[:, :]).then_inc(s_pe, 1)
                    pe.wait_ge(s_ends, 2 * d + 2)
                    pe.transpose(k.bank(1)[:, 0:HEADS], hand[:, :], k.ident[0:HEADS, 0:HEADS]).then_inc(s_pe, 1)

            @block.scalar
            def _(act):
                act.wait_ge(s_max, 1)
                act.activation(lg[:, :, :], lg[:, :, :], ACT.Exp).then_inc(s_exp, 1)

            @block.vector
            def _(dve):
                link = Chain(dve, s_chain)
                dve.wait_ge(s_load, 64)
                for d in range(2):
                    link(dve.tensor_tensor(pen[:, d, :], cur[:, :], near[:, d, :], ALU.is_equal))
                    link(dve.tensor_scalar(pen[:, d, :], pen[:, d, :], 1.0, BIG, ALU.subtract, ALU.mult))
                for d, (src, out) in enumerate(((lg, run), (run, top))):
                    way = (lambda t: t[:, ::-1]) if d else (lambda t: t)
                    end = 0 if d else CH - 1
                    for h in range(HEADS):
                        link(dve.tensor_tensor_scan(way(out[:, :, h]), way(pen[:, d, :]), way(src[:, :, h]), -BIG,
                                                    ALU.add, ALU.max))
                    link(dve.tensor_copy(ends[:, 0:HEADS], out[:, end, :]))
                    link(dve.tensor_reduce(ends[:, HEADS:HEADS + 1], pen[:, d, :], AX, ALU.min))
                    dve.tensor_copy(ends[:, HEADS + 1:2 * HEADS],
                                    bc(ends[:, HEADS:HEADS + 1], [P, HEADS - 1])).then_inc(s_ends, 1)
                    dve.wait_ge(s_pe, 2 * d + 1)
                    link(dve.tensor_copy(rows[:, :], k.bank(0)[0:HEADS, 0:2 * P]))
                    link(dve.tensor_tensor_scan(way(inc[:, :]), way(rows[:, P:2 * P]), way(rows[:, 0:P]), -BIG, ALU.add, ALU.max))
                    link(dve.memset(hand[:, :], -BIG))
                    if d:
                        dve.tensor_copy(hand[:, 0:P - 1], inc[:, 1:P]).then_inc(s_ends, 1)
                    else:
                        dve.tensor_copy(hand[:, 1:P], inc[:, 0:P - 1]).then_inc(s_ends, 1)
                    dve.wait_ge(s_pe, 2 * d + 2)
                    link(dve.tensor_copy(start[:, :], k.bank(1)[:, 0:HEADS]))
                    for h in range(HEADS):
                        link(dve.tensor_tensor_scan(way(out[:, :, h]), way(pen[:, d, :]), way(src[:, :, h]),
                                                    start[:, h:h + 1], ALU.add, ALU.max))
                dve.tensor_tensor(lg[:, :, :], lg[:, :, :], top[:, :, :], ALU.subtract).then_inc(s_max, 1)


def sums1(k):
    nc, a = k.nc, k.a
    U = 4
    with ExitStack() as ctx:
        sb = lambda name, shape, dt=F32: k.sb("s1_" + name, shape, dt, ctx)
        dst_all = sb("dst_all", [P, GROUPS, LANES], I32)
        dst = sb("dst", [P, U, LANES], I32)
        ex = sb("ex", [P, U, LANES, HEADS])
        value = sb("value", [P, U, LANES, D])
        rel = sb("rel", [P, 2, LANES])
        sel = sb("sel", [P, 2, LANES, P])
        rhs = sb("rhs", [P, 2, LANES, AGG1])
        acc = sb("acc", [P, U, AGG1])
        s_vec, s_copy, s_agg, s_acc = k.sem("s1_vec"), k.sem("s1_copy"), k.sem("s1_agg"), k.sem("s1_acc")
        s_load = [k.sem(f"s1_load{q}") for q in range(U)]
        s_dst_all, s_dst = k.sem("s1_dst_all"), k.sem("s1_dst")
        s_flush = [k.sem(f"s1_flush{q}") for q in range(U)]
        agg_ps = [k.bank(5), k.bank(6)]
        NV = 3
        with nc.Block() as block:

            @block.sync
            def _(sp):
                sp.dma_start(dst_all[:, :, :], a["dst_p"].rearrange("p (g l) -> p g l", l=LANES)).then_inc(s_dst_all, 16)

                def load(i, par):
                    g = sp.value_load(k.step_group[0:1, bass.ds(i + par, 1)], min_val=0, max_val=GROUPS - 1)
                    k.wait(sp, s_vec, (i + (par - U + 1)) * NV)
                    k.wait(sp, s_copy, i + (par - U + 1))
                    sp.dma_start(ex[:, par, :, :].rearrange("p l h -> p (l h)"),
                                 k.weights_e.rearrange("(q l) h -> q (l h)", l=LANES)[bass.ds(g * P, P), :]).then_inc(s_load[par], 16)
                    sp.dma_start(value[:, par, :, :].rearrange("p l d -> p (l d)"),
                                 k.values.rearrange("(q l) d -> q (l d)", l=LANES)[bass.ds(g * P, P), :]).then_inc(s_load[par], 16)

                sweep(sp, STEPS, load, first=2 * U, unroll=U)

            @block.gpsimd
            def _(pool):
                pool.wait_ge(s_dst_all, 16)

                def pick_dst(i, par):
                    g = pool.value_load(k.step_group[0:1, bass.ds(i + par, 1)], min_val=0, max_val=GROUPS - 1)
                    k.wait(pool, s_vec, (i + (par - U + 1)) * NV)
                    pool.tensor_copy(dst[:, par:par + 1, :], dst_all[:, bass.ds(g, 1), :]).then_inc(s_dst, 1)

                def flush(i, par):
                    r = pool.value_load(k.step_row[0:1, bass.ds(i + par, 1)], min_val=0, max_val=WINDOWS + SPARE - 1)
                    k.wait(pool, s_acc, i + (par + 1))
                    pool.dma_start(k.agg1[bass.ds(r * P, P), :], acc[:, par, :]).then_inc(s_flush[par], 16)

                def step(i, par):
                    if live(i, par, STEPS):
                        pick_dst(i, par)
                    j, q = back(i, par, 4, U)
                    if live(j, q, STEPS):
                        flush(j, q)

                sweep(pool, STEPS, step, 4, first=2 * U, unroll=U)
                for q in range(U):
                    pool.wait_ge(s_flush[q], 16 * (STEPS // U))

            @block.tensor
            def _(pe):
                def sums(i, par):
                    pe.wait_ge(s_vec, (i + (par + 1)) * NV)
                    pe.wait_ge(s_copy, i + (par + 1))
                    wait(pe, s_acc, i + (par - 1))
                    for lane in range(LANES):
                        ins = pe.matmul(agg_ps[par % 2][:, 0:AGG1], sel[:, par % 2, lane, :], rhs[:, par % 2, lane, :],
                                        start=(lane == 0), stop=(lane == LANES - 1))
                    ins.then_inc(s_agg, 1)

                sweep(pe, STEPS, sums, unroll=U)

            @block.scalar
            def _(act):
                def weights(i, par):
                    act.wait_ge(s_load[par], landed(i, par, U, 2))
                    wait(act, s_agg, i + (par - 1))
                    act.copy(rhs[:, par % 2, :, D:AGG1], ex[:, par, :, :]).then_inc(s_copy, 1)

                sweep(act, STEPS, weights, unroll=U)

            @block.vector
            def _(dve):
                def weigh(i, par):
                    t = par % 2
                    done = Count(dve, s_vec, i + par, NV)
                    dve.wait_ge(s_load[par], landed(i, par, U, 2))
                    dve.wait_ge(s_dst, i + (par + 1))
                    wait(dve, s_agg, i + (par - 1))
                    by_head = lambda ap: ap.rearrange("p l (h n) -> p l h n", h=HEADS)
                    done(dve.tensor_scalar(rel[:, t, :], dst[:, par, :], k.step_base[:, bass.ds(i + par, 1)], None, ALU.subtract))
                    done(dve.tensor_tensor(by_head(rhs[:, t, :, 0:D]), by_head(value[:, par, :, :]),
                                           bc(ex[:, par, :, :].rearrange("p l (h a) -> p l h a", a=1), [P, LANES, HEADS, D // HEADS]), ALU.mult))
                    done.at(1)
                    done(dve.tensor_tensor(sel[:, t], bc(k.iota[:, :].rearrange("p (a n) -> p a n", a=1), [P, LANES, P]),
                                           bc(rel[:, t, :].rearrange("p (l a) -> p l a", a=1), [P, LANES, P]), ALU.is_equal))
                    assert done.n == NV

                add_sums = accumulate(k, dve, s_agg, s_acc, s_flush, acc, agg_ps, AGG1)

                def step(i, par):
                    if live(i, par, STEPS):
                        weigh(i, par)
                    j, q = back(i, par, 2, U)
                    if live(j, q, STEPS):
                        add_sums(j, q)

                sweep(dve, STEPS, step, 2, unroll=U)


def output(k):
    nc, a, W = k.nc, k.a, WINDOWS
    with ExitStack() as ctx:
        sb = lambda name, shape, dt=F32: k.sb("o_" + name, shape, dt, ctx)
        sums = sb("sums", [P, W, AGG1])
        rden = sb("rden", [P, W, HEADS])
        wt = sb("wt", [P, 2, D])
        stage = sb("stage", [P, 4, D])
        turned = sb("turned", [P, 2, 2 * P])
        outb = sb("outb", [P, 4, D])
        s_zero, s_weights, s_sums, s_chain = k.sem("o_zero"), k.sem("o_weights"), k.sem("o_sums"), k.sem("o_chain")
        s_stage, s_turn, s_turned, s_prod, s_out = [k.sem("o_" + n) for n in ("stage", "turn", "turned", "prod", "out")]
        s_store = [k.sem(f"o_store{q}") for q in range(4)]
        turn_ps, prod_ps = [k.bank(0), k.bank(1)], [k.bank(2), k.bank(3)]
        n_dma = 17 * 16
        with nc.Block() as block:

            @block.gpsimd
            def _(pool):
                pool.memset(wt[:, :, :], 0.0).then_inc(s_zero, 1)

            @block.sync
            def _(sp):
                sp.dma_start(sums[:, :, :], k.agg1[0:NP, :].rearrange("(j p) d -> p j d", p=P)).then_inc(s_sums, 16)
                sp.wait_ge(s_zero, 1)
                n = 0
                for h in range(HEADS):
                    r = 40 * h
                    n += place(sp, s_weights, wt, r, 0, a["L1_gnn_Wps"][AS * h:AS * (h + 1), :])
                    for c in range(3):
                        n += place(sp, s_weights, wt, r + AS + AV * ((c + 1) % 3), S0 + V0 * c, a["L1_gnn_Wpv"][AV * h:AV * (h + 1), :])
                assert n == n_dma, n

                def store(i, par):
                    g = i + par
                    k.wait(sp, s_out, g + 1)
                    m = N - g * P if isinstance(g, int) and g == W - 1 else P
                    sp.dma_start(a["out"][bass.ds(g * P, m), :], outb[0:m, par, :]).then_inc(s_store[par], 16)

                sweep(sp, W, store, unroll=4)
                for q in range(4):
                    sp.wait_ge(s_store[q], 16 * ((W - q + 3) // 4))

            @block.tensor
            def _(pe):
                def turn(i, par):
                    pe.wait_ge(s_stage, i + (par + 1))
                    wait(pe, s_turned, (i + (par - 1)) * 2)
                    t = par % 2
                    pe.transpose(turn_ps[t][:, 0:P], stage[:, par, 0:P], k.ident[:, :])
                    pe.transpose(turn_ps[t][0:D - P, P:2 * P], stage[:, par, P:D], k.ident[:, :]).then_inc(s_turn, 1)

                def product(i, par):
                    pe.wait_ge(s_turned, (i + (par + 1)) * 2)
                    wait(pe, s_out, i + (par - 1))
                    t = par % 2
                    pe.matmul(prod_ps[t][:, 0:D], turned[:, t, 0:P], wt[:, 0, :], start=True, stop=False)
                    pe.matmul(prod_ps[t][:, 0:D], turned[0:D - P, t, P:2 * P], wt[0:D - P, 1, :],
                              start=False, stop=True).then_inc(s_prod, 1)

                def step(i, par):
                    if live(i, par, W):
                        turn(i, par)
                    j, q = back(i, par, 1, 4)
                    if live(j, q, W):
                        product(j, q)

                pe.wait_ge(s_weights, n_dma)
                sweep(pe, W, step, 1, unroll=4)

            @block.scalar
            def _(act):
                def evacuate(i, par):
                    act.wait_ge(s_turn, i + (par + 1))
                    wait(act, s_prod, i + (par - 1))
                    t = par % 2
                    act.copy(turned[:, t, 0:P], turn_ps[t][:, 0:P]).then_inc(s_turned, 1)
                    act.copy(turned[0:D - P, t, P:2 * P], turn_ps[t][0:D - P, P:2 * P]).then_inc(s_turned, 1)

                sweep(act, W, evacuate, unroll=4)

            @block.vector
            def _(dve):
                link = Chain(dve, s_chain)
                dve.wait_ge(s_sums, 16)
                link(dve.tensor_scalar(rden[:, :, :], sums[:, :, D:AGG1], 1e-16, None, ALU.add))
                link(dve.reciprocal(rden[:, :, :], rden[:, :, :]))
                def scale(i, par):
                    wait(dve, s_turn, i + (par - 3))
                    j = bass.ds(i + par, 1)
                    dve.tensor_tensor(stage[:, par, :].rearrange("p (a h n) -> p a h n", a=1, h=HEADS),
                                      sums[:, j, 0:D].rearrange("p a (h n) -> p a h n", h=HEADS),
                                      bc(rden[:, j, :].rearrange("p a (h b) -> p a h b", b=1), [P, 1, HEADS, D // HEADS]),
                                      ALU.mult).then_inc(s_stage, 1)

                def emit(i, par):
                    dve.wait_ge(s_prod, i + (par + 1))
                    wait(dve, s_store[par], left(i, par, 4, 1))
                    j = bass.ds(i + par, 1)
                    dve.tensor_tensor(outb[:, par, 0:S0].rearrange("p (a n) -> p a n", a=1),
                                      prod_ps[par % 2][:, 0:S0].rearrange("p (a n) -> p a n", a=1), k.resid[:, j, 0:S0], ALU.add)
                    dve.tensor_tensor(outb[:, par, S0:D].rearrange("p (a m c) -> p a c m", a=1, c=3),
                                      prod_ps[par % 2][:, S0:D].rearrange("p (a c m) -> p a c m", a=1, c=3),
                                      k.resid[:, j, S0:D].rearrange("p a (c m) -> p a c m", c=3), ALU.add).then_inc(s_out, 1)

                def step(i, par):
                    if live(i, par, W):
                        scale(i, par)
                    j, q = back(i, par, 2, 4)
                    if live(j, q, W):
                        emit(j, q)

                sweep(dve, W, step, 2, unroll=4)


def build(nc, a):
    with ExitStack() as ctx:
        k = Kernel(nc, ctx, a)
        setup_steps(k)
        with ExitStack() as first:
            k.selfc = k.sb("selfc", [P, WINDOWS, 192], ctx=first)
            node_phase(k, 0)
            edges0(k)
            layer0_update(k)
        node_phase(k, 1)
        edges1(k)
        softmax_weights(k)
        sums1(k)
        output(k)


def kernel(**inputs):
    import numpy as _np
    import concourse.bacc as _bacc
    from concourse import mybir as _mybir
    from concourse.bass_utils import run_bass_kernel_spmd as _run

    nc = _bacc.Bacc("TRN2", target_bir_lowering=False, num_devices=1)
    pad = EP - E
    lay = lambda x: _np.ascontiguousarray(x)
    src = _np.pad(lay(inputs["src"]), (0, pad))
    dst = _np.pad(lay(inputs["dst"]), (0, pad), constant_values=N)
    rows = {n: _np.pad(lay(inputs[n]), ((0, pad), (0, 0))) for n in ("edge_attr_16", "edge_attr_4", "edge_attr_8")}
    turned = lambda x: lay(x.reshape(GROUPS, P, LANES, -1).transpose(0, 3, 2, 1)).reshape(-1, GE)
    arrays = {
        "x": _np.pad(lay(inputs["x"]), ((0, NP - N), (0, 0))),
        "ends_g": _np.concatenate([src.reshape(-1, LANES), dst.reshape(-1, LANES)], axis=1),
        "dst_p": lay(dst.reshape(GROUPS, P, LANES).transpose(1, 0, 2)).reshape(P, -1),
        "dst_first": lay(dst[::GE]).reshape(1, GROUPS),
        "dst_edge": _np.pad(dst, (1, 1), constant_values=-1),
        "ea6_g": lay(rows["edge_attr_4"][:, [0, 1, 2, 3, 1, 2]]).reshape(-1, LANES * 6),
        "ea18_g": _np.concatenate([rows["edge_attr_4"][:, [0, 1, 2, 3, 1, 2]].reshape(-1, LANES * 6),
                                   rows["edge_attr_4"][:, [3, 1, 2] * HEADS].reshape(-1, LANES * HEADS * 3)], axis=1),
        "ea8_g": turned(rows["edge_attr_8"]),
        "ea16_g": turned(rows["edge_attr_16"]),
    }
    for name in inputs:
        if name.startswith("L"):
            arrays[name] = lay(inputs[name])
    a = {n: nc.dram_tensor("in_" + n, v.shape, _mybir.dt.from_np(v.dtype), kind="ExternalInput").ap() for n, v in arrays.items()}
    a["out"] = nc.dram_tensor("out_0", (N, D), F32, kind="ExternalOutput").ap()
    build(nc, a)
    r = _run(nc, [{"in_" + n: v for n, v in arrays.items()}], core_ids=[0])
    return r.results[0]["out_0"]
```
